# Optimizing a Trainium2 kernel written in Bass

```python
import numpy as np
import jax
import jax.numpy as jnp

def _softmax(x, axis=-1):
    return jax.nn.softmax(x, axis=axis)

def _gelu(x):
    return jax.nn.gelu(x, approximate=True)

def _silu(x):
    return jax.nn.silu(x)

def _sigmoid(x):
    return jax.nn.sigmoid(x)

def _layernorm(x, axis=-1, eps=1e-05):
    m = jnp.mean(x, axis=axis, keepdims=True)
    v = jnp.var(x, axis=axis, keepdims=True)
    return (x - m) / jnp.sqrt(v + eps)

def _scatter_add(tgt, idx, src, axis=0):
    return tgt.at[idx].add(src)

def _segment_sum(src, seg, n):
    return jax.ops.segment_sum(src, seg, n)
kernel_name = 'mk_decoder_postln_d2_seqx_r8_19b94d'

def setup_inputs(seed: int=0):
    np.random.seed(seed)
    _w = jnp.asarray

    def _rec_inputs():
        import jax
        import jax.numpy as jnp
        _rk = jax.random.key(seed)
        x = -0.0005207 + 1.001 * jax.random.normal(jax.random.fold_in(_rk, 1), (16, 128, 128), jnp.float32)
        _lenS = 128 - jax.random.randint(jax.random.fold_in(_rk, 7), (16,), 0, max(1, 128 // 4) + 1, jnp.int32)
        _lenS2 = 128 - jax.random.randint(jax.random.fold_in(_rk, 8), (16,), 0, max(1, 128 // 4) + 1, jnp.int32)
        _ctx_1024P = jax.random.normal(jax.random.fold_in(_rk, 11), (16, 16, 128), jnp.float32)
        _ctx_1024c = jax.random.dirichlet(jax.random.fold_in(_rk, 511), 0.3 * jnp.ones((16,), jnp.float32), (16, 128))
        _ctx_1024t = jnp.einsum('bsk,bkd->bsd', _ctx_1024c, _ctx_1024P)
        _ctx_1024t = _ctx_1024t * jax.lax.rsqrt(jnp.mean(jnp.square(_ctx_1024t)) + 1e-12) * 0.953939
        ctx_1024 = -0.000514642 + 1.00011 * (_ctx_1024t + 0.3 * jax.random.normal(jax.random.fold_in(_rk, 611), (16, 128, 128), jnp.float32))
        pos_S2 = jnp.arange(128, dtype=jnp.int32)
        _validS = jnp.arange(128)[None, :] < _lenS[:, None]
        _validS2 = jnp.arange(128)[None, :] < _lenS2[:, None]
        _causal = jnp.tril(jnp.ones((128, 128), dtype=bool))
        mask_BxS2_ik0 = jnp.where(jnp.broadcast_to(_validS2[:, :], (16, 128)), 0, 1).astype(jnp.int32)
        return (x, ctx_1024, pos_S2, mask_BxS2_ik0)
    x, ctx_1024, pos_S2, mask_BxS2_ik0 = _rec_inputs()

    def _L0_attn_setup():
        import jax, jax.numpy as jnp
        import numpy as np
        DIM = 128
        HEADS = 16
        DIM_HEAD = DIM // HEADS
        LATENT = DIM // 4
        SCALE = DIM_HEAD ** (-0.5)
        key = jax.random.key(seed)
        ks = jax.random.split(key, 8)
        B, S = (2, 256)
        init = lambda k, shape, fan_in: jax.random.normal(k, shape, jnp.float32) * fan_in ** (-0.5)
        return {'x': jax.random.normal(ks[0], (B, S, DIM), jnp.float32), 'Wq': init(ks[1], (DIM, DIM), DIM), 'bq': jnp.zeros((DIM,), jnp.float32), 'Wl': init(ks[2], (DIM, LATENT), DIM), 'bl': jnp.zeros((LATENT,), jnp.float32), 'Wk': init(ks[3], (LATENT, DIM), LATENT), 'bk': jnp.zeros((DIM,), jnp.float32), 'Wv': init(ks[4], (LATENT, DIM), LATENT), 'bv': jnp.zeros((DIM,), jnp.float32), 'Wo': init(ks[5], (DIM, DIM), DIM), 'bo': jnp.zeros((DIM,), jnp.float32)}
    _L0_attn_all = _L0_attn_setup()
    _L0_attn_in = {k: v for k, v in _L0_attn_all.items() if k in ('Wq', 'bq', 'Wl', 'bl', 'Wk', 'bk', 'Wv', 'bv', 'Wo', 'bo')}
    del _L0_attn_all

    def _L0_xattn_setup():
        import jax, jax.numpy as jnp
        import numpy as np
        N_HEADS = 16
        ROPE_BASE = 10000.0

        def _rotate_half(x):
            x1, x2 = jnp.split(x, 2, axis=-1)
            return jnp.concatenate([-x2, x1], axis=-1)

        def _rope_cos_sin(positions, d_k, dtype):
            inv_freq = 1.0 / ROPE_BASE ** (jnp.arange(0, d_k, 2, dtype=jnp.float32) / d_k)
            freqs = positions.astype(jnp.float32)[:, None] * inv_freq[None, :]
            emb = jnp.concatenate([freqs, freqs], axis=-1)
            return (jnp.cos(emb).astype(dtype), jnp.sin(emb).astype(dtype))
        key = jax.random.key(seed)
        ks = jax.random.split(key, 8)
        B, T, D = (1, 256, 128)
        s = 0.02
        return {'query': jax.random.normal(ks[0], (B, T, D), jnp.float32), 'key': jax.random.normal(ks[1], (B, T, D), jnp.float32), 'value': jax.random.normal(ks[2], (B, T, D), jnp.float32), 'yarn_positions': jnp.arange(T, dtype=jnp.int32), 'wq': jax.random.normal(ks[3], (D, D), jnp.float32) * s, 'wk': jax.random.normal(ks[4], (D, D), jnp.float32) * s, 'wv': jax.random.normal(ks[5], (D, D), jnp.float32) * s, 'wo_w': jax.random.normal(ks[6], (D, D), jnp.float32) * s, 'wo_b': jnp.zeros((D,), jnp.float32)}
    _L0_xattn_all = _L0_xattn_setup()
    _L0_xattn_in = {k: v for k, v in _L0_xattn_all.items() if k in ('wq', 'wk', 'wv', 'wo_w', 'wo_b')}
    del _L0_xattn_all

    def _L0_ffn_setup():
        import jax, jax.numpy as jnp
        import numpy as np
        B, S, D, H, F = (4, 512, 128, 16, 512)
        CAP = 0.125
        ROPE_BASE = 10000.0

        def rmsnorm(x, g):
            return x * jax.lax.rsqrt(jnp.mean(x * x, -1, keepdims=True) + 1e-06) * g

        def rope(t, pos):
            hd = t.shape[-1]
            inv = 1.0 / ROPE_BASE ** (jnp.arange(0, hd, 2, dtype=jnp.float32) / hd)
            f = pos[:, None, :, None].astype(jnp.float32) * inv
            emb = jnp.concatenate([f, f], axis=-1)
            cos, sin = (jnp.cos(emb), jnp.sin(emb))
            rot = jnp.concatenate([-t[..., hd // 2:], t[..., :hd // 2]], axis=-1)
            return t * cos + rot * sin
        key = jax.random.key(seed)
        ks = jax.random.split(key, 9)
        scale = 0.02
        x = jax.random.normal(ks[0], (B, S, D), jnp.float32)
        causal = jnp.where(jnp.tril(jnp.ones((S, S), bool)), 0.0, -1000000000.0).astype(jnp.float32)
        attention_mask = jnp.broadcast_to(causal[None, None], (B, 1, S, S))
        position_ids = jnp.broadcast_to(jnp.arange(S, dtype=jnp.int32), (B, S))
        return {'x': x, 'attention_mask': attention_mask, 'position_ids': position_ids, 'router_w': jax.random.normal(ks[1], (D, 1), jnp.float32) * scale, 'router_b': jnp.zeros((1,), jnp.float32), 'wq': jax.random.normal(ks[2], (D, D), jnp.float32) * scale, 'wk': jax.random.normal(ks[3], (D, D), jnp.float32) * scale, 'wv': jax.random.normal(ks[4], (D, D), jnp.float32) * scale, 'wo': jax.random.normal(ks[5], (D, D), jnp.float32) * scale, 'w1': jax.random.normal(ks[6], (D, F), jnp.float32) * scale, 'w2': jax.random.normal(ks[7], (F, D), jnp.float32) * scale, 'ln1': jnp.ones((D,), jnp.float32), 'ln2': jnp.ones((D,), jnp.float32)}
    _L0_ffn_all = _L0_ffn_setup()
    _L0_ffn_in = {k: v for k, v in _L0_ffn_all.items() if k in ('attention_mask', 'position_ids', 'router_w', 'router_b', 'wq', 'wk', 'wv', 'wo', 'w1', 'w2', 'ln1', 'ln2')}
    del _L0_ffn_all

    def _L1_attn_setup():
        import jax, jax.numpy as jnp
        import numpy as np
        H, HD, D = (16, 64, 128)
        SCALE = HD ** (-0.5)
        TEMP = 1.0
        EPS = 1e-05
        key = jax.random.key(seed)
        ks = jax.random.split(key, 10)
        B, N = (2, 256)
        lim = 1.0 / np.sqrt(D)

        def lin(k, out_d, in_d):
            k1, k2 = jax.random.split(k)
            W = jax.random.uniform(k1, (out_d, in_d), jnp.float32, -lim, lim)
            b = jax.random.uniform(k2, (out_d,), jnp.float32, -lim, lim)
            return (W, b)
        Wq, bq = lin(ks[0], H * HD, D)
        Wk, bk = lin(ks[1], H * HD, D)
        Wv, bv = lin(ks[2], H * HD, D)
        Wo, bo = lin(ks[3], D, H * HD)
        return {'x': jax.random.normal(ks[4], (B, N, D), jnp.float32), 'adaptive_scale': jnp.ones((H,), jnp.float32), 'Wq': Wq, 'bq': bq, 'Wk': Wk, 'bk': bk, 'Wv': Wv, 'bv': bv, 'Wo': Wo, 'bo': bo, 'gamma': jnp.ones((D,), jnp.float32), 'beta': jnp.zeros((D,), jnp.float32)}
    _L1_attn_all = _L1_attn_setup()
    _L1_attn_in = {k: v for k, v in _L1_attn_all.items() if k in ('adaptive_scale', 'Wq', 'bq', 'Wk', 'bk', 'Wv', 'bv', 'Wo', 'bo', 'gamma', 'beta')}
    del _L1_attn_all

    def _L1_xattn_setup():
        import jax, jax.numpy as jnp
        import numpy as np
        B, T1, T2, C, H = (4, 128, 256, 128, 16)
        D = C // H
        key = jax.random.key(seed)
        ks = jax.random.split(key, 8)
        s = 1.0 / np.sqrt(C)
        return {'query_states': jax.random.normal(ks[0], (B, T1, C), jnp.float32), 'key_value_states': jax.random.normal(ks[1], (B, T2, C), jnp.float32), 'kv_attention_mask': jax.random.randint(ks[2], (B, T2), 0, 2, jnp.int32), 'Wq': jax.random.normal(ks[3], (C, C), jnp.float32) * s, 'bq': jnp.zeros((C,), jnp.float32), 'Wk': jax.random.normal(ks[4], (C, C), jnp.float32) * s, 'bk': jnp.zeros((C,), jnp.float32), 'Wv': jax.random.normal(ks[5], (C, C), jnp.float32) * s, 'bv': jnp.zeros((C,), jnp.float32), 'Wp': jax.random.normal(ks[6], (C, C), jnp.float32) * s, 'bp': jnp.zeros((C,), jnp.float32)}
    _L1_xattn_all = _L1_xattn_setup()
    _L1_xattn_in = {k: v for k, v in _L1_xattn_all.items() if k in ('Wq', 'bq', 'Wk', 'bk', 'Wv', 'bv', 'Wp', 'bp')}
    del _L1_xattn_all

    def _L1_ffn_setup():
        import jax, jax.numpy as jnp
        import numpy as np
        from jax import lax
        T, B, I, M, O = (32, 64, 128, 128, 128)

        def _xavier(key, shape):
            fan_out, fan_in = shape
            limit = float(np.sqrt(6.0 / (fan_in + fan_out)))
            return jax.random.uniform(key, shape, jnp.float32, -limit, limit)
        key = jax.random.key(seed)
        ks = jax.random.split(key, 9)
        x = jax.random.normal(ks[0], (T, B, I), jnp.float32)
        return {'x': x, 'wf': _xavier(ks[1], (M, I)), 'uf': _xavier(ks[2], (M, M)), 'bf': jnp.zeros((M,), jnp.float32), 'wi': _xavier(ks[3], (M, I)), 'ui': _xavier(ks[4], (M, M)), 'bi': jnp.zeros((M,), jnp.float32), 'wc': _xavier(ks[5], (M, I)), 'uc': _xavier(ks[6], (M, M)), 'bc': jnp.zeros((M,), jnp.float32), 'wo': _xavier(ks[7], (O, I)), 'uo': _xavier(ks[8], (O, M)), 'bo': jnp.zeros((O,), jnp.float32), 'in_c': jnp.zeros((M,), jnp.float32)}
    _L1_ffn_all = _L1_ffn_setup()
    _L1_ffn_in = {k: v for k, v in _L1_ffn_all.items() if k in ('wf', 'uf', 'bf', 'wi', 'ui', 'bi', 'wc', 'uc', 'bc', 'wo', 'uo', 'bo', 'in_c')}
    del _L1_ffn_all
    return {'x': x, 'ctx_1024': ctx_1024, 'pos_S2': pos_S2, 'mask_BxS2_ik0': mask_BxS2_ik0, 'L0_attn_Wq': _L0_attn_in['Wq'], 'L0_attn_bq': _L0_attn_in['bq'], 'L0_attn_Wl': _L0_attn_in['Wl'], 'L0_attn_bl': _L0_attn_in['bl'], 'L0_attn_Wk': _L0_attn_in['Wk'], 'L0_attn_bk': _L0_attn_in['bk'], 'L0_attn_Wv': _L0_attn_in['Wv'], 'L0_attn_bv': _L0_attn_in['bv'], 'L0_attn_Wo': _L0_attn_in['Wo'], 'L0_attn_bo': _L0_attn_in['bo'], 'L0_xattn_wq': _L0_xattn_in['wq'], 'L0_xattn_wk': _L0_xattn_in['wk'], 'L0_xattn_wv': _L0_xattn_in['wv'], 'L0_xattn_wo_w': _L0_xattn_in['wo_w'], 'L0_xattn_wo_b': _L0_xattn_in['wo_b'], 'L0_ffn_attention_mask': _L0_ffn_in['attention_mask'], 'L0_ffn_position_ids': _L0_ffn_in['position_ids'], 'L0_ffn_router_w': _L0_ffn_in['router_w'], 'L0_ffn_router_b': _L0_ffn_in['router_b'], 'L0_ffn_wq': _L0_ffn_in['wq'], 'L0_ffn_wk': _L0_ffn_in['wk'], 'L0_ffn_wv': _L0_ffn_in['wv'], 'L0_ffn_wo': _L0_ffn_in['wo'], 'L0_ffn_w1': _L0_ffn_in['w1'], 'L0_ffn_w2': _L0_ffn_in['w2'], 'L0_ffn_ln1': _L0_ffn_in['ln1'], 'L0_ffn_ln2': _L0_ffn_in['ln2'], 'L1_attn_adaptive_scale': _L1_attn_in['adaptive_scale'], 'L1_attn_Wq': _L1_attn_in['Wq'], 'L1_attn_bq': _L1_attn_in['bq'], 'L1_attn_Wk': _L1_attn_in['Wk'], 'L1_attn_bk': _L1_attn_in['bk'], 'L1_attn_Wv': _L1_attn_in['Wv'], 'L1_attn_bv': _L1_attn_in['bv'], 'L1_attn_Wo': _L1_attn_in['Wo'], 'L1_attn_bo': _L1_attn_in['bo'], 'L1_attn_gamma': _L1_attn_in['gamma'], 'L1_attn_beta': _L1_attn_in['beta'], 'L1_xattn_Wq': _L1_xattn_in['Wq'], 'L1_xattn_bq': _L1_xattn_in['bq'], 'L1_xattn_Wk': _L1_xattn_in['Wk'], 'L1_xattn_bk': _L1_xattn_in['bk'], 'L1_xattn_Wv': _L1_xattn_in['Wv'], 'L1_xattn_bv': _L1_xattn_in['bv'], 'L1_xattn_Wp': _L1_xattn_in['Wp'], 'L1_xattn_bp': _L1_xattn_in['bp'], 'L1_ffn_wf': _L1_ffn_in['wf'], 'L1_ffn_uf': _L1_ffn_in['uf'], 'L1_ffn_bf': _L1_ffn_in['bf'], 'L1_ffn_wi': _L1_ffn_in['wi'], 'L1_ffn_ui': _L1_ffn_in['ui'], 'L1_ffn_bi': _L1_ffn_in['bi'], 'L1_ffn_wc': _L1_ffn_in['wc'], 'L1_ffn_uc': _L1_ffn_in['uc'], 'L1_ffn_bc': _L1_ffn_in['bc'], 'L1_ffn_wo': _L1_ffn_in['wo'], 'L1_ffn_uo': _L1_ffn_in['uo'], 'L1_ffn_bo': _L1_ffn_in['bo'], 'L1_ffn_in_c': _L1_ffn_in['in_c']}

def reference(x, ctx_1024, pos_S2, mask_BxS2_ik0, L0_attn_Wq, L0_attn_bq, L0_attn_Wl, L0_attn_bl, L0_attn_Wk, L0_attn_bk, L0_attn_Wv, L0_attn_bv, L0_attn_Wo, L0_attn_bo, L0_xattn_wq, L0_xattn_wk, L0_xattn_wv, L0_xattn_wo_w, L0_xattn_wo_b, L0_ffn_attention_mask, L0_ffn_position_ids, L0_ffn_router_w, L0_ffn_router_b, L0_ffn_wq, L0_ffn_wk, L0_ffn_wv, L0_ffn_wo, L0_ffn_w1, L0_ffn_w2, L0_ffn_ln1, L0_ffn_ln2, L1_attn_adaptive_scale, L1_attn_Wq, L1_attn_bq, L1_attn_Wk, L1_attn_bk, L1_attn_Wv, L1_attn_bv, L1_attn_Wo, L1_attn_bo, L1_attn_gamma, L1_attn_beta, L1_xattn_Wq, L1_xattn_bq, L1_xattn_Wk, L1_xattn_bk, L1_xattn_Wv, L1_xattn_bv, L1_xattn_Wp, L1_xattn_bp, L1_ffn_wf, L1_ffn_uf, L1_ffn_bf, L1_ffn_wi, L1_ffn_ui, L1_ffn_bi, L1_ffn_wc, L1_ffn_uc, L1_ffn_bc, L1_ffn_wo, L1_ffn_uo, L1_ffn_bo, L1_ffn_in_c):
    import jax
    import jax.numpy as jnp

    def _L0_attn_ref(x, Wq, bq, Wl, bl, Wk, bk, Wv, bv, Wo, bo):
        import jax, jax.numpy as jnp
        import numpy as np
        DIM = 128
        HEADS = 16
        DIM_HEAD = DIM // HEADS
        LATENT = DIM // 4
        SCALE = DIM_HEAD ** (-0.5)
        B, S, D = x.shape
        H, Dh = (HEADS, DIM_HEAD)
        q = (x @ Wq + bq).reshape(B, S, H, Dh)
        latent = x @ Wl + bl
        k = (latent @ Wk + bk).reshape(B, S, H, Dh)
        v = (latent @ Wv + bv).reshape(B, S, H, Dh)
        scores = jnp.einsum('bihd,bjhd->bhij', q, k) * SCALE
        attn = jax.nn.softmax(scores, axis=-1)
        out = jnp.einsum('bhij,bjhd->bihd', attn, v).reshape(B, S, D)
        out = out @ Wo + bo
        return out

    def _L0_xattn_ref(query, key, value, yarn_positions, wq, wk, wv, wo_w, wo_b):
        import jax, jax.numpy as jnp
        import numpy as np
        N_HEADS = 16
        ROPE_BASE = 10000.0

        def _rotate_half(x):
            x1, x2 = jnp.split(x, 2, axis=-1)
            return jnp.concatenate([-x2, x1], axis=-1)

        def _rope_cos_sin(positions, d_k, dtype):
            inv_freq = 1.0 / ROPE_BASE ** (jnp.arange(0, d_k, 2, dtype=jnp.float32) / d_k)
            freqs = positions.astype(jnp.float32)[:, None] * inv_freq[None, :]
            emb = jnp.concatenate([freqs, freqs], axis=-1)
            return (jnp.cos(emb).astype(dtype), jnp.sin(emb).astype(dtype))
        B, Tq, D = query.shape
        Tk = key.shape[1]
        H = N_HEADS
        dk = D // H
        Q = (query @ wq.T).reshape(B, Tq, H, dk).transpose(0, 2, 1, 3)
        K = (key @ wk.T).reshape(B, Tk, H, dk).transpose(0, 2, 1, 3)
        V = (value @ wv.T).reshape(B, Tk, H, dk).transpose(0, 2, 1, 3)
        cos, sin = _rope_cos_sin(yarn_positions, dk, Q.dtype)
        cos = cos[None, None, :, :]
        sin = sin[None, None, :, :]
        Q = Q * cos + _rotate_half(Q) * sin
        K = K * cos + _rotate_half(K) * sin
        scale = 1.0 / jnp.sqrt(jnp.asarray(dk, Q.dtype))
        scores = jnp.einsum('bhqd,bhkd->bhqk', Q, K) * scale
        causal = jnp.triu(jnp.ones((Tq, Tk), dtype=bool), 1)
        scores = jnp.where(causal[None, None], -jnp.inf, scores)
        attn = jax.nn.softmax(scores, axis=-1)
        out = jnp.einsum('bhqk,bhkd->bhqd', attn, V)
        out = out.transpose(0, 2, 1, 3).reshape(B, Tq, D)
        return out @ wo_w.T + wo_b

    def _L0_ffn_ref(x, attention_mask, position_ids, router_w, router_b, wq, wk, wv, wo, w1, w2, ln1, ln2):
        import jax, jax.numpy as jnp
        import numpy as np
        B, S, D, H, F = (4, 512, 128, 16, 512)
        CAP = 0.125
        ROPE_BASE = 10000.0

        def rmsnorm(x, g):
            return x * jax.lax.rsqrt(jnp.mean(x * x, -1, keepdims=True) + 1e-06) * g

        def rope(t, pos):
            hd = t.shape[-1]
            inv = 1.0 / ROPE_BASE ** (jnp.arange(0, hd, 2, dtype=jnp.float32) / hd)
            f = pos[:, None, :, None].astype(jnp.float32) * inv
            emb = jnp.concatenate([f, f], axis=-1)
            cos, sin = (jnp.cos(emb), jnp.sin(emb))
            rot = jnp.concatenate([-t[..., hd // 2:], t[..., :hd // 2]], axis=-1)
            return t * cos + rot * sin
        b, s, d = x.shape
        hd = d // H
        weights = (x @ router_w)[..., 0] + router_b[0]
        k = int(CAP * s)
        topv, topi = jax.lax.top_k(weights, k)
        thr = topv[:, -1]
        sel_mask = (weights > thr[:, None]).astype(x.dtype)
        kc = k - 1
        sel_idx = jnp.sort(topi[:, :kc], axis=1)
        bidx = jnp.arange(b)[:, None]
        x_sel = x[bidx, sel_idx]
        pos_sel = position_ids[bidx, sel_idx]
        w_sel = weights[bidx, sel_idx]
        m = attention_mask[:, 0]
        m_sel = m[bidx[:, :, None], sel_idx[:, :, None], sel_idx[:, None, :]]
        hn = rmsnorm(x_sel, ln1)

        def heads(t):
            return t.reshape(b, kc, H, hd).transpose(0, 2, 1, 3)
        q = rope(heads(hn @ wq), pos_sel)
        kk = rope(heads(hn @ wk), pos_sel)
        v = heads(hn @ wv)
        sc = jnp.einsum('bhqd,bhkd->bhqk', q, kk) / np.sqrt(hd).astype(np.float32)
        sc = sc + m_sel[:, None]
        a = jax.nn.softmax(sc, axis=-1)
        o = jnp.einsum('bhqk,bhkd->bhqd', a, v).transpose(0, 2, 1, 3).reshape(b, kc, d) @ wo
        x1 = x_sel + o
        x2 = x1 + jax.nn.gelu(rmsnorm(x1, ln2) @ w1) @ w2
        proc = x2 * w_sel[..., None]
        out = jnp.zeros_like(x).at[bidx, sel_idx].set(proc)
        return out + x * (1.0 - sel_mask)[..., None]

    def _L1_attn_ref(x, adaptive_scale, Wq, bq, Wk, bk, Wv, bv, Wo, bo, gamma, beta):
        import jax, jax.numpy as jnp
        import numpy as np
        H, HD, D = (16, 64, 128)
        SCALE = HD ** (-0.5)
        TEMP = 1.0
        EPS = 1e-05
        B, N, _ = x.shape
        Q = (x @ Wq.T + bq).reshape(B, N, H, HD)
        K = (x @ Wk.T + bk).reshape(B, N, H, HD)
        V = (x @ Wv.T + bv).reshape(B, N, H, HD)
        scores = jnp.einsum('bnhd,bmhd->bhnm', Q, K)
        scores = scores * (SCALE * adaptive_scale)[None, :, None, None] / TEMP
        w = jax.nn.softmax(scores, axis=-1)
        attn = jnp.einsum('bhnm,bmhd->bnhd', w, V).reshape(B, N, H * HD)
        y = x + (attn @ Wo.T + bo)
        mu = jnp.mean(y, axis=-1, keepdims=True)
        var = jnp.var(y, axis=-1, keepdims=True)
        return (y - mu) / jnp.sqrt(var + EPS) * gamma + beta

    def _L1_xattn_ref(query_states, key_value_states, kv_attention_mask, Wq, bq, Wk, bk, Wv, bv, Wp, bp):
        import jax, jax.numpy as jnp
        import numpy as np
        B, T1, T2, C, H = (4, 128, 256, 128, 16)
        D = C // H
        b, t1, c = query_states.shape
        t2 = key_value_states.shape[1]
        q = (query_states @ Wq.T + bq).reshape(b, t1, H, D).transpose(0, 2, 1, 3)
        k = (key_value_states @ Wk.T + bk).reshape(b, t2, H, D).transpose(0, 2, 1, 3)
        v = (key_value_states @ Wv.T + bv).reshape(b, t2, H, D).transpose(0, 2, 1, 3)
        scale = 1.0 / np.sqrt(D).astype(np.float32)
        att = jnp.einsum('bhqd,bhkd->bhqk', q, k) * scale
        att = kv_attention_mask[:, None, None, :].astype(att.dtype) * att
        att = jax.nn.softmax(att, axis=-1)
        y = jnp.einsum('bhqk,bhkd->bhqd', att, v)
        y = y.transpose(0, 2, 1, 3).reshape(b, t1, c)
        return y @ Wp.T + bp

    def _L1_ffn_ref(x, wf, uf, bf, wi, ui, bi, wc, uc, bc, wo, uo, bo, in_c):
        import jax, jax.numpy as jnp
        import numpy as np
        from jax import lax
        T, B, I, M, O = (32, 64, 128, 128, 128)

        def _xavier(key, shape):
            fan_out, fan_in = shape
            limit = float(np.sqrt(6.0 / (fan_in + fan_out)))
            return jax.random.uniform(key, shape, jnp.float32, -limit, limit)
        batch = x.shape[1]
        c0 = jnp.broadcast_to(in_c, (batch, in_c.shape[0]))

        def step(c, xt):
            ft = jax.nn.sigmoid(xt @ wf.T + c @ uf.T + bf)
            it = jax.nn.sigmoid(xt @ wi.T + c @ ui.T + bi)
            gt = jnp.tanh(xt @ wc.T + c @ uc.T + bc)
            c = ft * c + it * gt
            return (c, None)
        c_final, _ = lax.scan(step, c0, x)
        h = jnp.tanh(jnp.einsum('tbi,oi->tbo', x, wo) + c_final @ uo.T + bo)
        return h
    x = _layernorm(x + _L0_attn_ref(x, L0_attn_Wq, L0_attn_bq, L0_attn_Wl, L0_attn_bl, L0_attn_Wk, L0_attn_bk, L0_attn_Wv, L0_attn_bv, L0_attn_Wo, L0_attn_bo), axis=-1)
    x = _layernorm(x + _L0_xattn_ref(x, ctx_1024, ctx_1024, pos_S2, L0_xattn_wq, L0_xattn_wk, L0_xattn_wv, L0_xattn_wo_w, L0_xattn_wo_b), axis=-1)
    x = _layernorm(x + _L0_ffn_ref(x, L0_ffn_attention_mask, L0_ffn_position_ids, L0_ffn_router_w, L0_ffn_router_b, L0_ffn_wq, L0_ffn_wk, L0_ffn_wv, L0_ffn_wo, L0_ffn_w1, L0_ffn_w2, L0_ffn_ln1, L0_ffn_ln2), axis=-1)
    x = _layernorm(x + _L1_attn_ref(x, L1_attn_adaptive_scale, L1_attn_Wq, L1_attn_bq, L1_attn_Wk, L1_attn_bk, L1_attn_Wv, L1_attn_bv, L1_attn_Wo, L1_attn_bo, L1_attn_gamma, L1_attn_beta), axis=-1)
    x = _layernorm(x + _L1_xattn_ref(x, ctx_1024, mask_BxS2_ik0, L1_xattn_Wq, L1_xattn_bq, L1_xattn_Wk, L1_xattn_bk, L1_xattn_Wv, L1_xattn_bv, L1_xattn_Wp, L1_xattn_bp), axis=-1)
    x = _layernorm(x + _L1_ffn_ref(x, L1_ffn_wf, L1_ffn_uf, L1_ffn_bf, L1_ffn_wi, L1_ffn_ui, L1_ffn_bi, L1_ffn_wc, L1_ffn_uc, L1_ffn_bc, L1_ffn_wo, L1_ffn_uo, L1_ffn_bo, L1_ffn_in_c), axis=-1)
    return x

_drawn_inputs = setup_inputs


def setup_inputs(seed=0):
    import zlib

    import numpy as np

    out = dict(_drawn_inputs(seed))
    spreads = {'L0_attn_bq': (0.0, 0.427),
     'L0_attn_bl': (0.0, 0.1),
     'L0_attn_bk': (0.0, 0.8),
     'L0_attn_bv': (0.0, 0.1),
     'L0_attn_bo': (0.0, 0.1),
     'L0_xattn_wo_b': (0.0, 0.1),
     'L0_ffn_ln1': (1.0, 0.6),
     'L0_ffn_ln2': (1.0, 0.6),
     'L1_attn_adaptive_scale': (1.0, 0.6),
     'L1_attn_gamma': (1.0, 0.2),
     'L1_attn_beta': (0.0, 0.1),
     'L1_xattn_bq': (0.0, 0.8),
     'L1_xattn_bk': (0.0, 0.8),
     'L1_xattn_bv': (0.0, 0.1),
     'L1_xattn_bp': (0.0, 0.1),
     'L1_ffn_bf': (0.0, 0.644),
     'L1_ffn_bi': (0.0, 0.666),
     'L1_ffn_bc': (0.0, 0.1),
     'L1_ffn_bo': (0.0, 0.1),
     'L1_ffn_in_c': (0.0, 0.8)}
    factors = {'L0_xattn_wq': 8.0,
     'L0_xattn_wk': 8.0,
     'L0_ffn_router_w': 8.0,
     'L0_ffn_wq': 8.0,
     'L0_ffn_wk': 8.0,
     'L0_ffn_wv': 8.0,
     'L0_ffn_wo': 8.0,
     'L0_ffn_w1': 8.0,
     'L0_ffn_w2': 8.0,
     'L1_attn_Wq': 2.751,
     'L1_attn_bq': 8.0,
     'L1_attn_Wk': 2.71,
     'L1_attn_bk': 8.0}
    for name, (base, spread) in spreads.items():
        noise = np.random.default_rng([zlib.crc32(name.encode()), seed]).standard_normal(out[name].shape)
        drawn = base * np.exp(spread * noise) if base else spread * noise
        out[name] = jnp.asarray(drawn.astype(out[name].dtype))
    for name, factor in factors.items():
        out[name] = (out[name] * factor).astype(out[name].dtype)
    return out
```

```python
from contextlib import ExitStack

import concourse.bass as bass
import numpy as np
from concourse import mybir

ALU = mybir.AluOpType
ACT = mybir.ActivationFunctionType
AX = mybir.AxisListType
F32 = mybir.dt.float32
BF16 = mybir.dt.bfloat16
I32 = mybir.dt.int32

B, S, D = 16, 128, 128
H = 16
HD = D // H
LAT = D // 4
FF = 512
HW = 64
PAIRS = H // 2
SLOT = 2 * HD
UH = H // 2
UC = UH * S
LEAD, LAG = 2, 2
LN_EPS = 1e-5
RMS_EPS = 1e-6
ROPE_BASE = 10000.0
TWO_PI = 2 * np.pi
NEG = -1e30


def bc(ap, axis, n):
    shape = list(ap.shape)
    shape.insert(axis, n)
    return ap.unsqueeze(axis).to_broadcast(shape)


def after(eng, sem, count):
    if isinstance(count, int) and count <= 0:
        return
    eng.wait_ge(sem, count)


def has(b):
    return not isinstance(b, int) or 0 <= b < B


def slots(eng, slot):
    for i in range(-LEAD, LAG):
        slot(i, i % 2, i // 2)
    with eng.Fori(0, (B - LEAD - LAG) // 2) as j:
        for p in range(2):
            slot(j * 2 + (LAG + p), (LAG + p) % 2, j + LAG // 2)
    for i in range(B - LEAD, B + LAG):
        slot(i, i % 2, i // 2)


def one(t, i):
    return t[:, bass.ds(i, 1), :].rearrange("p o d -> p (o d)")


WEIGHTS = [
    ("a_q", 0, "L0_attn_Wq", D, D), ("a_lT", 0, "L0_attn_WlT", LAT, D), ("a_k0", 0, "L0_attn_Wk", LAT, D),
    ("a_v0", 0, "L0_attn_Wv", LAT, D), ("a_o", 0, "L0_attn_Wo", D, D),
    ("b_q", 0, "L0_xattn_wqT", D, D), ("b_k", 0, "L0_xattn_wkT", D, D), ("b_v", 0, "L0_xattn_wvT", D, D),
    ("b_o", 0, "L0_xattn_wo_wT", D, D),
    ("e_q", 0, "L1_xattn_WqT", D, D), ("e_k", 0, "L1_xattn_WkT", D, D), ("e_v", 0, "L1_xattn_WvT", D, D),
    ("e_o", 0, "L1_xattn_WpT", D, D),
    ("d_q", 0, "L1_attn_WqT", D, H * HW), ("d_k", 0, "L1_attn_WkT", D, H * HW), ("d_v", 0, "L1_attn_WvT", D, H * HW),
    ("d_o", 0, "L1_attn_Wo_pairs", 128, PAIRS * D),
    ("c_qkv", 0, "L0_ffn_wq", D, D), ("c_qkv", D, "L0_ffn_wk", D, D), ("c_qkv", 2 * D, "L0_ffn_wv", D, D),
    ("c_o", 0, "L0_ffn_wo", D, D), ("c_w1", 0, "L0_ffn_w1", D, FF), ("c_w2", 0, "L0_ffn_w2_chunks", 128, FF),
    ("r_w", 0, "L1_ffn_wfT", D, D), ("r_w", D, "L1_ffn_wiT", D, D), ("r_w", 2 * D, "L1_ffn_wcT", D, D),
    ("r_u", 0, "L1_ffn_ufT", D, D), ("r_u", D, "L1_ffn_uiT", D, D), ("r_u", 2 * D, "L1_ffn_ucT", D, D),
    ("r_wo", 0, "L1_ffn_woT", D, D), ("r_uo", 0, "L1_ffn_uoT", D, D),
    ("c_rw", 0, "L0_ffn_router_w", D, 1),
    ("d_qb", 0, "L1_attn_bq_pairs", 128, PAIRS), ("d_kb", 0, "L1_attn_bk_pairs", 128, PAIRS),
    ("d_vb", 0, "L1_attn_bv_pairs", 128, PAIRS),
]


def fold_value_bias(nc, sems, k, sb, vb, wo, n, bias_row, out, psum_bank):
    spread, product, done = sems

    def on_vector_spread():
        for c in range(n):
            last = nc.vector.tensor_scalar(sb["spread"][:, c * D:(c + 1) * D], sb["ones"][:], vb[:, c:c + 1], None,
                                           ALU.mult)
        last.then_inc(spread, 1)

    def on_tensor():
        nc.tensor.wait_ge(spread, k)
        for c in range(n):
            last = nc.tensor.matmul(psum_bank[:, 0:D], sb["spread"][:, c * D:(c + 1) * D],
                                    wo[:, c * D:(c + 1) * D], start=(c == 0), stop=(c == n - 1))
        last.then_inc(product, 1)

    def on_vector_add():
        nc.vector.wait_ge(product, k)
        nc.vector.tensor_tensor(out[:], psum_bank[:, 0:D], bias_row[:], ALU.add).then_inc(done, 1)

    return on_vector_spread, on_tensor, on_vector_add


def setup_small_heads(nc, ps, sb, X, dram):
    S_ps, PT_ps, O_ps, M_ps = ps
    columns = [("a_qb", "L0_attn_bq", D), ("a_bl", "L0_attn_bl", LAT), ("a_bk", "L0_attn_bk", D),
               ("a_bv", "L0_attn_bv", D), ("e_qb", "L1_xattn_bq", D), ("e_kb", "L1_xattn_bk", D),
               ("e_bv", "L1_xattn_bv", D),
               ("c_ln1", "L0_ffn_ln1", D), ("c_ln2", "L0_ffn_ln2", D),
               ("r_bf0", "L1_ffn_bf", D), ("r_bi0", "L1_ffn_bi", D), ("r_bc", "L1_ffn_bc", D),
               ("r_c00", "L1_ffn_in_c", D)]
    rows = [("a_bo", "L0_attn_bo"), ("b_bias", "L0_xattn_wo_b"), ("e_bp", "L1_xattn_bp"),
            ("d_bo", "L1_attn_bo"), ("gamma", "L1_attn_gamma"), ("beta", "L1_attn_beta"),
            ("c_rw_row", "L0_ffn_router_w_row"), ("c_rb", "L0_ffn_router_b"),
            ("r_bo", "L1_ffn_bo")]
    with ExitStack() as ctx:
        def sem(what):
            return ctx.enter_context(nc.semaphore(f"setup_{what}"))

        loaded, loaded_c, filled = sem("loaded"), sem("loaded_constants"), sem("filled")
        prepared = sem("prepared")
        products_a, copied_a = sem("products_a"), sem("copied_a")
        rope_step = sem("rope_step")
        sin_done, table_ready, mask_ready = sem("sin_done"), sem("table_ready"), sem("mask_ready")
        fold = sem("fold_spread"), sem("fold_product"), sem("fold_done")
        block = ctx.enter_context(nc.Block())
        d_steps = fold_value_bias(nc, fold, 3, sb, sb["d_vb"], sb["d_o"], PAIRS, sb["d_bo"], sb["d_bias"], O_ps)
        a_steps = fold_value_bias(nc, fold, 1, sb, sb["a_vb"], sb["a_o"], 1, sb["a_bo"], sb["a_bias"], O_ps)
        e_steps = fold_value_bias(nc, fold, 2, sb, sb["e_bv"], sb["e_o"], 1, sb["e_bp"], sb["e_bias"], M_ps)
        kmask_i = sb["P"][:].rearrange("p u h k -> p (u h k)").bitcast(I32)
        n_loads = len(WEIGHTS) + len(columns) + len(rows) + 4

        @block.sync
        def _(sp):
            for name, at, src, _, width in WEIGHTS:
                sp.dma_start(sb[name][:, at:at + width], dram[src]).then_inc(loaded, 16)
            for name, src, n in columns:
                sp.dma_start(sb[name][:], dram[src].rearrange("(n o) -> n o", o=1)).then_inc(loaded, 16)
            for name, src in rows:
                sp.dma_start(sb[name][:], bc(dram[src], 0, S)).then_inc(loaded, 16)
            for e in range(2):
                sp.dma_start(sb["d_as"][e * HW:(e + 1) * HW, :],
                             bc(dram["L1_attn_scale_pairs"][e, :], 0, HW))\
                    .then_inc(loaded, 16)
            sp.dma_start(sb["amask"][:], dram["L0_ffn_attention_mask"][:, 0, 0:S, 0:S].rearrange("m t k -> t m k"))\
                .then_inc(loaded, 16)
            sp.dma_start(X[:], dram["x"].rearrange("b s d -> s b d")).then_inc(loaded, 16)
            sp.wait_ge(loaded, 16 * n_loads)

        @block.scalar
        def _(act):
            act.dma_start(sb["ident"][:], dram["ident"]).then_inc(loaded_c, 16)
            act.dma_start(sb["headmask"][:], dram["headmask"]).then_inc(loaded_c, 16)
            act.dma_start(sb["causalf"][:], dram["causal"]).then_inc(loaded_c, 16)
            act.dma_start(sb["inv"][:], dram["inv_freq"]).then_inc(loaded_c, 16)
            for name in ("upper", "iota", "valid", "blocks2", "mbatch", "inv4"):
                dst = sb[name][:]
                if len(dst.shape) > 2:
                    dst = dst.rearrange("p a b -> p (a b)")
                act.dma_start(dst, dram[name]).then_inc(loaded_c, 16)
            act.dma_start(sb["QW"][:].rearrange("p u h k -> p (u h k)"), dram["repeat"]).then_inc(loaded_c, 16)
            act.dma_start(sb["pos4_i"][:], dram["L0_ffn_position_ids_t"][0:S, :]).then_inc(loaded_c, 16)
            act.dma_start(sb["pos_i"][:], bc(dram["pos_S2"], 0, D)).then_inc(loaded_c, 16)
            act.dma_start(kmask_i,
                          bc(dram["mask_BxS2_ik0"].rearrange("b k -> (b k)"), 0, D)).then_inc(loaded_c, 16)
            for half in range(2):
                act.wait_ge(rope_step, 6 * half + 6)
                nc.scalar.activation(sb["trig"][:, half, :], sb["ang"][:, half, :], ACT.Sin).then_inc(sin_done, 1)

        @block.gpsimd
        def _(pool):
            pool.wait_ge(loaded_c, 16 * 14)
            nc.gpsimd.tensor_copy(sb["kmask"][:].rearrange("p b k -> p (b k)"),
                                  kmask_i).then_inc(mask_ready, 1)
            nc.gpsimd.tensor_copy(sb["pos"][:], sb["pos_i"][:]).then_inc(mask_ready, 1)
            nc.gpsimd.tensor_copy(sb["pos4"][:], sb["pos4_i"][:]).then_inc(mask_ready, 1)
            nc.gpsimd.memset(sb["KW"][:], 0.0).then_inc(mask_ready, 1)
            nc.gpsimd.memset(sb["VW"][:], 0.0).then_inc(mask_ready, 1)
            pool.wait_ge(mask_ready, 5)

        @block.tensor
        def _(pe):
            pe.wait_ge(loaded, 16 * n_loads)
            nc.tensor.matmul(M_ps[:, 0:D], sb["a_lT"][:], sb["a_k0"][:], start=True, stop=True)
            nc.tensor.matmul(M_ps[:, D:2 * D], sb["a_lT"][:], sb["a_v0"][:], start=True, stop=True)
            nc.tensor.matmul(M_ps[:, 2 * D:2 * D + 1], sb["a_k0"][:], sb["a_bl"][:], start=True, stop=True)
            nc.tensor.matmul(M_ps[:, 2 * D + 1:2 * D + 2], sb["a_v0"][:], sb["a_bl"][:], start=True, stop=True)\
                .then_inc(products_a, 1)
            a_steps[1]()
            pe.wait_ge(copied_a, 4)
            e_steps[1]()
            d_steps[1]()

        @block.vector
        def _(dve):
            nc.vector.memset(sb["ones"][:], 1.0).then_inc(filled, 1)
            nc.vector.memset(sb["Vx"][:], 0.0).then_inc(filled, 1)
            nc.vector.memset(sb["mhalf"][:], -0.5).then_inc(filled, 1)
            nc.vector.memset(sb["eps"][:], LN_EPS).then_inc(filled, 1)
            dve.wait_ge(filled, 4)
            for p in range(2):
                nc.vector.memset(sb["Vx"][:, p, :].rearrange("p (h c) -> p h c", h=H)[:, :, HD], 1.0)\
                    .then_inc(filled, 1)
            dve.wait_ge(filled, 6)
            dve.wait_ge(loaded, 16 * n_loads)
            for src, dst in (("b_q", "b_qr"), ("b_k", "b_kr")):
                w_in = sb[src][:].rearrange("p (h c) -> p h c", h=H)
                w_out = sb[dst][:].rearrange("p (h c) -> p h c", h=H)
                nc.vector.tensor_scalar(w_out[:, :, 0:HD // 2], w_in[:, :, HD // 2:HD], -1.0, None, ALU.mult)\
                    .then_inc(prepared, 1)
                nc.vector.tensor_copy(w_out[:, :, HD // 2:HD], w_in[:, :, 0:HD // 2]).then_inc(prepared, 1)
            dve.wait_ge(prepared, 4)
            dve.wait_ge(products_a, 1)
            nc.vector.tensor_copy(sb["a_k"][:], M_ps[:, 0:D]).then_inc(copied_a, 1)
            nc.vector.tensor_copy(sb["a_v"][:], M_ps[:, D:2 * D]).then_inc(copied_a, 1)
            nc.vector.tensor_tensor(sb["a_kb"][:], M_ps[:, 2 * D:2 * D + 1], sb["a_bk"][:], ALU.add)\
                .then_inc(copied_a, 1)
            nc.vector.tensor_tensor(sb["a_vb"][:], M_ps[:, 2 * D + 1:2 * D + 2], sb["a_bv"][:], ALU.add)\
                .then_inc(copied_a, 1)
            dve.wait_ge(copied_a, 4)
            a_steps[0]()
            a_steps[2]()
            dve.wait_ge(fold[2], 1)
            e_steps[0]()
            e_steps[2]()
            dve.wait_ge(fold[2], 2)
            d_steps[0]()
            d_steps[2]()
            dve.wait_ge(fold[2], 3)
            nc.vector.tensor_scalar(sb["d_qs"][:], sb["d_as"][:], float(HW) ** -0.5, None, ALU.mult)\
                .then_inc(prepared, 1)
            dve.wait_ge(prepared, 5)
            nc.vector.tensor_tensor(sb["d_qbs"][:], sb["d_qb"][:], sb["d_qs"][:], ALU.mult).then_inc(prepared, 1)
            dve.wait_ge(prepared, 6)
            for name in ("a_qb", "e_qb"):
                nc.vector.tensor_scalar(sb[name + "s"][:], sb[name][:], float(HD) ** -0.5, None, ALU.mult)\
                    .then_inc(prepared, 1)
            dve.wait_ge(loaded_c, 16 * 14)
            nc.vector.tensor_copy(sb["identb"][:], sb["ident"][:]).then_inc(prepared, 1)
            nc.vector.tensor_copy(sb["causal"][:], bc(sb["causalf"][:], 1, 4)).then_inc(prepared, 1)
            dve.wait_ge(prepared, 10)
            dve.wait_ge(mask_ready, 5)
            turns, angle, rounding = sb["turns"], sb["angle"], 1.5 * 2.0 ** 23
            c1 = float(np.float32(6.28125))
            c2 = float(np.float32(np.floor((TWO_PI - c1) * 2 ** 22) / 2 ** 22))
            c3 = float(TWO_PI - c1 - c2)
            nc.vector.tensor_scalar(angle[:, 0:S], sb["pos"][:], sb["inv"][:], None, ALU.mult).then_inc(table_ready, 1)
            nc.vector.tensor_tensor(angle[:, S:S + 4 * MB].rearrange("p (m c) -> p m c", m=MB), bc(sb["pos4"][:], 2, 4),
                                    bc(sb["inv4"][:], 1, MB), ALU.mult).then_inc(table_ready, 1)
            dve.wait_ge(table_ready, 2)
            step = [0]

            def link(instruction):
                step[0] += 1
                instruction.then_inc(rope_step, 1)
                dve.wait_ge(rope_step, step[0])

            for half, (quarter, shift_) in enumerate(((0.25, np.pi / 2), (0.0, 0.0))):
                a = sb["ang"][:, half, :]
                link(nc.vector.tensor_scalar(turns[:], angle[:], float(1 / TWO_PI), quarter, ALU.mult, ALU.add))
                link(nc.vector.tensor_scalar(turns[:], turns[:], rounding, rounding, ALU.add, ALU.subtract))
                link(nc.vector.scalar_tensor_tensor(out=a, in0=turns[:], scalar=-c1, in1=angle[:],
                                                    op0=ALU.mult, op1=ALU.add))
                link(nc.vector.scalar_tensor_tensor(out=a, in0=turns[:], scalar=-c2, in1=a,
                                                    op0=ALU.mult, op1=ALU.add))
                link(nc.vector.scalar_tensor_tensor(out=a, in0=turns[:], scalar=-c3, in1=a,
                                                    op0=ALU.mult, op1=ALU.add))
                if half == 0:
                    link(nc.vector.tensor_scalar(a, a, float(shift_), 3.1415925, ALU.add, ALU.min))
                else:
                    link(nc.vector.tensor_scalar(a, a, -3.1415925, 3.1415925, ALU.max, ALU.min))
            dve.wait_ge(sin_done, 2)
            nc.vector.tensor_scalar(sb["rope"][:, 0:2, :], sb["trig"][:, :, 0:S], float(HD) ** -0.5, None, ALU.mult)\
                .then_inc(table_ready, 1)
            nc.vector.tensor_copy(sb["rope"][:, 2:4, :], sb["trig"][:, :, 0:S]).then_inc(table_ready, 1)
            for at, which, sign in ((0, 0, 1.0), (4, 0, 1.0), (8, 1, -1.0), (12, 1, 1.0)):
                nc.vector.tensor_scalar(sb["cs_table"][:, :, at:at + 4],
                                        sb["trig"][:, which, S:].rearrange("p (m c) -> p m c", m=MB), sign, None,
                                        ALU.mult).then_inc(table_ready, 1)
            for n, scale in enumerate((float(HD) ** -0.5, 1.0, 1.0)):
                part = sb["c_qkv"][:, n * D:(n + 1) * D]
                nc.vector.tensor_scalar(part, part, sb["c_ln1"][:], scale, ALU.mult, ALU.mult)\
                    .then_inc(table_ready, 1)
            nc.vector.tensor_scalar(sb["c_w1"][:], sb["c_w1"][:], sb["c_ln2"][:], None, ALU.mult)\
                .then_inc(table_ready, 1)
            nc.vector.tensor_scalar(sb["c_w2"][:], sb["c_w2"][:], 0.5, None, ALU.mult).then_inc(table_ready, 1)
            for dst, src, scale in (("r_u", "r_u", 0.5), ("r_uo", "r_uo", 0.5), ("r_bf", "r_bf0", 0.5),
                                    ("r_bi", "r_bi0", 0.5), ("r_c0", "r_c00", 2.0)):
                nc.vector.tensor_scalar(sb[dst][:], sb[src][:], scale, None, ALU.mult).then_inc(table_ready, 1)
            dve.wait_ge(table_ready, 18)


def small_head_attention(nc, name, ps, sb, X, xs, ctx_dram, w, rope=None, causal=None, key_mask=None):
    S_ps, PT_ps, O_ps, M_ps = ps
    cross = ctx_dram is not None
    with ExitStack() as ctx:
        def sem(what):
            return ctx.enter_context(nc.semaphore(f"{name}_{what}"))

        x_loaded = [sem("x_loaded0"), sem("x_loaded1")]
        loads = 2 if cross else 1
        xt_done, xt_ready = sem("xt_done"), sem("xt_ready")
        qk_done, q_ready, k_ready = sem("qk_done"), sem("q_ready"), sem("k_ready")
        rope_prod = sem("rope_prod") if rope else None
        kx_ready = sem("kx_ready")
        s_done, max_ready, sub_ready, exp_ready = sem("s_done"), sem("max_ready"), sem("sub_ready"), sem("exp_ready")
        pt_done, pt_ready, pv_done = sem("pt_done"), sem("pt_ready"), sem("pv_done")
        o_ready, ot_done, v_ready = sem("o_ready"), sem("ot_done"), sem("v_ready")
        rden_ready, on_ready = sem("rden_ready"), sem("on_ready")
        ont_done, ont_ready, out_done = sem("ont_done"), sem("ont_ready"), sem("out_done")
        xb_ready, y_ready, var_ready, rstd_ready, x_new = (
            sem("xb_ready"), sem("y_ready"), sem("var_ready"), sem("rstd_ready"), sem("x_new"))
        ve_ready = sem("ve_ready")
        block = ctx.enter_context(nc.Block())
        kv_src = sb["cT"] if cross else sb["xT"]

        @block.sync
        def _(sp):
            def slot(i, p, half):
                b = i + LEAD
                if has(b):
                    after(sp, xt_done, b - 1)
                    sp.dma_start(xs[:, p, :], one(X, b)).then_inc(x_loaded[p], 16)
                    if cross:
                        after(sp, ot_done, i + 1)
                        sp.dma_start(sb["cT"][:, p, :], ctx_dram[:, bass.ds(b * S, S)]).then_inc(x_loaded[p], 16)
            slots(sp, slot)

        @block.tensor
        def _(pe):
            def scores(b, u, p):
                pe.wait_ge(kx_ready, b + 1)
                pe.wait_ge(q_ready, b + 1)
                after(pe, sub_ready, 2 * b + u - 1)
                for g in range(2):
                    heads = slice(UH * u + 4 * g, UH * u + 4 * g + 4)
                    last = nc.tensor.matmul(S_ps[:, 2 * u + g, :], sb["QT"][:, p, :], 
                                            sb["Kx"][:, p, heads, :].rearrange("p h k -> p (h k)"),
                                            start=True, stop=causal is None)
                    if causal is not None:
                        last = nc.tensor.matmul(S_ps[:, 2 * u + g, :], sb["identb"][:], causal[:].rearrange("p h k -> p (h k)"),
                                                start=False, stop=True)
                last.then_inc(s_done, 1)

            def transpose_probs(b, u):
                pe.wait_ge(exp_ready, 2 * b + u + 1)
                after(pe, pt_ready, 2 * b + u)
                for h in range(UH):
                    last = nc.tensor.transpose(PT_ps[:, h // 4, (h % 4) * S:(h % 4 + 1) * S],
                                               sb["P"][:, u, h, :], sb["ident"][:])
                last.then_inc(pt_done, 1)

            def values(b, u, p):
                pe.wait_ge(pt_ready, 2 * b + u + 1)
                if u == 0:
                    pe.wait_ge(v_ready, b + 1)
                    after(pe, o_ready, b)
                for h in range(UH):
                    at = u * UH * (SLOT * (UH + 1)) + h * SLOT * UH
                    last = nc.tensor.matmul(O_ps[:, u * S:(u + 1) * S], sb["Vx"][:, p, at:at + S],
                                            sb["PT"][:, u, h, :], start=(h == 0), stop=(h == UH - 1))
                last.then_inc(pv_done, 1)

            def slot(i, p, half):
                q = 1 - p
                b, n, r = i + LEAD, i + 1, i - 1
                if has(i):
                    scores(i, 1, p)
                if has(b):
                    pe.wait_ge(x_loaded[p], (half + 2) * (16 * loads))
                    after(pe, y_ready, i - 1)
                    after(pe, v_ready, i + 1)
                    nc.tensor.transpose(M_ps[:, 0:S], xs[:, p, :], sb["ident"][:]).then_inc(xt_done, 1)
                if has(r):
                    values(r, 1, q)
                if has(i):
                    transpose_probs(i, 0)
                if has(b):
                    pe.wait_ge(xt_ready, b + 1)
                    srcs = [("q", sb["xT"])] + ([("qr", sb["xT"])] if rope else []) + [("k", kv_src)] \
                        + ([("kr", kv_src)] if rope else [])
                    for n_, (which, src) in enumerate(srcs):
                        last = nc.tensor.matmul(M_ps[:, n_ * S:(n_ + 1) * S], w[which][:], src[:, p, :],
                                                start=True, stop=True)
                    last.then_inc(qk_done, 1)
                if has(n):
                    scores(n, 0, q)
                if not has(b):
                    after(pe, y_ready, i - 1)
                elif rope:
                    pe.wait_ge(rope_prod, b + 1)
                else:
                    pe.wait_ge(q_ready, b + 1)
                    pe.wait_ge(k_ready, b + 1)
                if has(r) or has(n):
                    if has(r):
                        pe.wait_ge(o_ready, r + 1)
                        for t in range(2):
                            last = nc.tensor.transpose(M_ps[:, t * S:(t + 1) * S], sb["O"][:, t * S:(t + 1) * S],
                                                       sb["ident"][:])
                    if has(n):
                        last = nc.tensor.matmul(M_ps[:, 2 * S:3 * S], kv_src[:, q, :], w["v"][:],
                                                start=True, stop=True)
                    last.then_inc(ot_done, 1)
                if has(i):
                    values(i, 0, p)
                if has(r):
                    pe.wait_ge(on_ready, r + 1)
                    if has(n):
                        pe.wait_ge(v_ready, n + 1)
                    nc.tensor.transpose(M_ps[:, 0:S], sb["ON"][:], sb["ident"][:]).then_inc(ont_done, 1)
                if has(i):
                    transpose_probs(i, 1)
                if has(r):
                    pe.wait_ge(ont_ready, r + 1)
                    nc.tensor.matmul(M_ps[:, S:2 * S], sb["ONT"][:], w["o"][:], start=True, stop=True)\
                        .then_inc(out_done, 1)
            slots(pe, slot)

        @block.scalar
        def _(act):
            def exps(b, u):
                act.wait_ge(sub_ready, 2 * b + u + 1)
                nc.scalar.activation(sb["P"][:, u, :, :], sb["P"][:, u, :, :], ACT.Exp).then_inc(exp_ready, 1)

            def probs_out(b, u):
                act.wait_ge(pt_done, 2 * b + u + 1)
                after(act, pv_done, 2 * b + u - 1)
                nc.scalar.activation(sb["PT"][:, u, :, :].rearrange("p h q -> p (h q)"),
                                     PT_ps[:].rearrange("p a c -> p (a c)"), ACT.Copy).then_inc(pt_ready, 1)

            def slot(i, p, half):
                b, n, r = i + LEAD, i + 1, i - 1
                if has(i):
                    exps(i, 0)
                if has(b):
                    act.wait_ge(xt_done, b + 1)
                    after(act, ot_done, b - 1)
                    nc.scalar.activation(sb["xT"][:, p, :], M_ps[:, 0:S], ACT.Copy).then_inc(xt_ready, 1)
                if has(i):
                    probs_out(i, 0)
                if has(b) and not rope:
                    act.wait_ge(qk_done, b + 1)
                    if key_mask is None:
                        after(act, kx_ready, b)
                        nc.scalar.activation(sb["KT"][:], M_ps[:, S:2 * S], ACT.Identity, bias=w["kb"][:])\
                            .then_inc(k_ready, 1)
                    after(act, s_done, 2 * i + 2)
                    nc.scalar.activation(sb["QT"][:, p, :], M_ps[:, 0:S], ACT.Identity, bias=w["qb"][:],
                                         scale=w["qs"]).then_inc(q_ready, 1)
                if has(i):
                    exps(i, 1)
                if has(n):
                    act.wait_ge(ot_done, n + 1)
                    after(act, pv_done, 2 * i)
                    after(act, on_ready, r + 1)
                    nc.scalar.activation(sb["Vx"][:, 1 - p, :].rearrange("p (h c) -> p h c", h=H)[:, :, 0:HD],
                                         M_ps[:, 2 * S:3 * S].rearrange("p (h c) -> p h c", h=H), ACT.Copy)\
                        .then_inc(v_ready, 1)
                if has(r):
                    act.wait_ge(ont_done, r + 1)
                    after(act, out_done, r)
                    nc.scalar.activation(sb["ONT"][:], M_ps[:, 0:S], ACT.Copy).then_inc(ont_ready, 1)
                if has(i):
                    probs_out(i, 1)
            slots(act, slot)

        @block.vector
        def _(dve):
            def shift(b, u):
                unit = S_ps[:, 2 * u:2 * u + 2, :].rearrange("p a (h k) -> p (a h) k", k=S)
                dve.wait_ge(s_done, 2 * b + u + 1)
                after(dve, sub_ready, 2 * b + u)
                nc.vector.tensor_reduce(sb["mx"][:, 0:UH], unit, op=ALU.max, axis=AX.X).then_inc(max_ready, 1)
                dve.wait_ge(max_ready, 2 * b + u + 1)
                after(dve, pt_done, 2 * b + u - 1)
                nc.vector.tensor_tensor(sb["P"][:, u, :, :], unit, bc(sb["mx"][:, 0:UH], 2, S), ALU.subtract)\
                    .then_inc(sub_ready, 1)

            def slot(i, p, half):
                b, n, r, z = i + LEAD, i + 1, i - 1, i - LAG
                if has(z):
                    dve.wait_ge(out_done, z + 1)
                    dve.wait_ge(xb_ready, z + 1)
                    after(dve, x_new, z)
                    nc.vector.tensor_tensor(sb["Y"][:], M_ps[:, S:2 * S], sb["XB"][:, p, :], ALU.add)\
                        .then_inc(y_ready, 1)
                if has(i):
                    shift(i, 1)
                if has(r):
                    dve.wait_ge(pv_done, 2 * r + 2)
                    after(dve, ot_done, i + 1)
                    nc.vector.tensor_copy(sb["O"][:], O_ps[:, 0:2 * S]).then_inc(o_ready, 1)
                if has(z):
                    dve.wait_ge(y_ready, z + 1)
                    nc.vector.bn_stats(sb["bn"][:], sb["Y"][:])
                    nc.vector.drain()
                    nc.vector.bn_aggr(sb["mv"][:], sb["bn"][:]).then_inc(var_ready, 1)
                if has(b):
                    if rope:
                        dve.wait_ge(qk_done, b + 1)
                        after(dve, k_ready, b)
                        after(dve, q_ready, b)
                        nc.vector.tensor_tensor(sb["RP"][:], M_ps[:, 0:4 * S], rope[:], ALU.mult)\
                            .then_inc(rope_prod, 1)
                    elif key_mask is not None:
                        after(dve, kx_ready, b)
                        dve.wait_ge(q_ready, b + 1)
                        nc.vector.scalar_tensor_tensor(out=sb["KT"][:], in0=M_ps[:, S:2 * S], scalar=w["kb"][:],
                                                       in1=one(key_mask, b), op0=ALU.add, op1=ALU.mult)\
                            .then_inc(k_ready, 1)
                if has(n):
                    shift(n, 0)
                if has(r):
                    heads = M_ps[:, 0:2 * S].rearrange("p (h c) -> p h c", h=H)
                    dve.wait_ge(ot_done, i + 2)
                    nc.vector.reciprocal(sb["rden"][:], heads[:, :, HD]).then_inc(rden_ready, 1)
                    dve.wait_ge(rden_ready, r + 1)
                    after(dve, ont_done, r)
                    nc.vector.tensor_tensor(sb["ON"][:].rearrange("p (h c) -> p h c", h=H), heads[:, :, 0:HD],
                                            bc(sb["rden"][:], 2, HD), ALU.mult).then_inc(on_ready, 1)
                if has(z):
                    dve.wait_ge(rstd_ready, z + 1)
                    nc.vector.tensor_scalar(one(X, z), sb["Y"][:], sb["mv"][:, 0:1], sb["rstd"][:],
                                            ALU.subtract, ALU.mult).then_inc(x_new, 1)
            slots(dve, slot)

        @block.gpsimd
        def _(pool):
            def slot(i, p, half):
                b, r, z = i + LEAD, i - 1, i - LAG
                if has(z):
                    pool.wait_ge(var_ready, z + 1)
                    nc.gpsimd.tensor_tensor(sb["ve"][:], sb["mv"][:, 1:2], sb["eps"][:], ALU.add)\
                        .then_inc(ve_ready, 1)
                    pool.wait_ge(ve_ready, z + 1)
                    nc.gpsimd.tensor_tensor(sb["rstd"][:], sb["ve"][:], sb["mhalf"][:], ALU.pow)\
                        .then_inc(rstd_ready, 1)
                if has(r):
                    after(pool, y_ready, r - 1)
                    nc.gpsimd.tensor_tensor(sb["XB"][:, 1 - p, :], one(X, r), w["bias"][:], ALU.add)\
                        .then_inc(xb_ready, 1)
                if has(b):
                    if rope:
                        pool.wait_ge(rope_prod, b + 1)
                        after(pool, kx_ready, b)
                        nc.gpsimd.tensor_tensor(sb["KT"][:], sb["RP"][:, 2 * S:3 * S], sb["RP"][:, 3 * S:4 * S],
                                                ALU.add).then_inc(k_ready, 1)
                        after(pool, s_done, 2 * i + 2)
                        nc.gpsimd.tensor_tensor(sb["QT"][:, p, :], sb["RP"][:, 0:S], sb["RP"][:, S:2 * S],
                                                ALU.add).then_inc(q_ready, 1)
                    pool.wait_ge(k_ready, b + 1)
                    after(pool, s_done, 2 * i + 2)
                    nc.gpsimd.tensor_tensor(sb["Kx"][:, p, :, :], bc(sb["KT"][:], 1, H),
                                            bc(sb["headmask"][:], 2, S), ALU.mult).then_inc(kx_ready, 1)
            slots(pool, slot)


TOP = S // 8
KC = TOP - 1
NB = 128 // TOP
NT = B // NB
MB = 4
GELU_C = float(np.sqrt(2 / np.pi))


def counted(nc, ctx, prefix, **engines):
    sems, counts = {}, {}
    for engine, names in engines.items():
        sem = ctx.enter_context(nc.semaphore(f"{prefix}_{engine}_events"))
        for n, name in enumerate(names.split()):
            sems[name], counts[name] = sem, n + 1
    return sems, counts


def routed_ffn(nc, ps_all, sb, X):
    SB, SLOTS = 2048, NT * 128
    with ExitStack() as ctx:
        ev, nth = counted(
            nc, ctx, "ffn",
            tensor="spread_t gathered masks_u tables selected_t tokens qkv dense_mask k0 k1 v0 v1 attended_t "
                   "projected x1n_t hidden ff scattered",
            scalar="xsT u_ready selT_ready exps attended_sb x1n_sb hidden_sb tanhs",
            pool="eq_masked rstd scaled_x rstd2 rstd3",
            vector="weighed summed weights spread eq ge count_ge count_eq rank factor select cs_prod cs_ready "
                   "tokens_ready squares square_sum mean_square wsel mask_prod mask_ready qkv_ready rot_sin rot_cos "
                   "roped k0_prod k0_sum k1_prod k1_sum masked row_max shifted row_sum row_inv v0_prod v1_prod "
                   "v_sum attended x1 squares2 square_sum2 mean_square2 x1n cubed inner gated slot_w x2 spread_x2 "
                   "y aggregated var_eps centred x_new")

        block = ctx.enter_context(nc.Block())
        banks = [ps_all[:, n, :] for n in range(8)]
        scores4, upper4 = ps_all[:, 0:4, :], ps_all[:, 4:8, :]
        P, PT = (sb[n][:].rearrange("p u h k -> p (u h k)") for n in ("P", "PT"))
        big = sb["Kx"][:].rearrange("p u h k -> p (u h k)")
        wide = sb["QW"][:].rearrange("p u h k -> p (u h k)")
        hid, gate = wide[:, 0:NT * FF], wide[:, NT * FF:2 * NT * FF]
        repeat = wide.rearrange("p (j c) -> p j c", j=TOP)
        P3, PT3 = (t.rearrange("p (b d) -> p b d", b=B) for t in (P, PT))
        wt, sel, rank = sb["wt"], sb["sel"], sb["rank"]
        sel_flat = sel[:].rearrange("p b r -> p (b r)")
        qkv = sb["qkv"]
        qk = qkv[:, :, 0:2 * D].rearrange("p t (h c) -> p t h c", c=HD)
        roped = sb["roped"][:].rearrange("p t (h c) -> p t h c", c=HD)
        rot = sb["rot"][:].rearrange("p t (h c) -> p t h c", c=HD)
        keys = big.rearrange("p (j c) -> p j c", c=SLOTS)
        att = sb["att"]
        X3 = X[:]

        @block.tensor
        def _(pe):
            pe.wait_ge(ev["spread"], nth["spread"])
            for b in range(B):
                last = nc.tensor.transpose(banks[b // 4][:, (b % 4) * S:(b % 4 + 1) * S],
                                           big[:, b * S:(b + 1) * S], sb["ident"][:])
            last.then_inc(ev["spread_t"], 1)
            pe.wait_ge(ev["select"], nth["select"])
            for b in range(B):
                last = nc.tensor.matmul(banks[6][:, b * TOP:(b + 1) * TOP], X3[:, b, :], sel[:, b, :],
                                        start=True, stop=True)
            last.then_inc(ev["gathered"], 1)
            for m in range(MB):
                end = B if m == MB - 1 else m + 1
                last = nc.tensor.matmul(banks[4][:, m * TOP:end * TOP], sb["amask"][:, m, :],
                                        sel_flat[:, m * TOP:end * TOP], start=True, stop=True)
            last.then_inc(ev["masks_u"], 1)
            for t in range(NT):
                last = nc.tensor.matmul(banks[5][:, t * 64:(t + 1) * 64], sel_flat[:, t * 128:(t + 1) * 128],
                                        sb["cs_table"][:].rearrange("p m c -> p (m c)"), start=True, stop=True)
            last.then_inc(ev["tables"], 1)
            pe.wait_ge(ev["eq"], nth["eq"])
            for t in range(NT):
                last = nc.tensor.transpose(banks[0][:, t * 128:(t + 1) * 128], sel_flat[:, t * 128:(t + 1) * 128],
                                           sb["ident"][:])
            last.then_inc(ev["selected_t"], 1)
            pe.wait_ge(ev["xsT"], nth["xsT"])
            for t in range(NT):
                last = nc.tensor.transpose(banks[7][:, t * 128:(t + 1) * 128], sb["xsT"][:, t * 128:(t + 1) * 128],
                                           sb["ident"][:])
            last.then_inc(ev["tokens"], 1)
            for t in range(NT):
                tile = sb["xsT"][:, t * 128:(t + 1) * 128]
                nc.tensor.matmul(banks[1 + t][:, 0:3 * D], tile, sb["c_qkv"][:], start=True, stop=True)
                last = nc.tensor.matmul(banks[3][:, t:t + 1], tile, sb["c_rw"][:], start=True, stop=True)
            last.then_inc(ev["qkv"], 1)
            pe.wait_ge(ev["u_ready"], nth["u_ready"])
            pe.wait_ge(ev["xsT"], nth["xsT"])
            for t in range(NT):
                last = nc.tensor.matmul(banks[6][:, t * 128:(t + 1) * 128], sb["umask"][:, t * 128:(t + 1) * 128],
                                        sel_flat[:, t * 128:(t + 1) * 128], start=True, stop=True)
            last.then_inc(ev["dense_mask"], 1)
            pe.wait_ge(ev["roped"], nth["roped"])
            pe.wait_ge(ev["selT_ready"], nth["selT_ready"])
            pe.wait_ge(ev["tokens_ready"], nth["tokens_ready"])
            pe.wait_ge(ev["mask_prod"], nth["mask_prod"])
            pe.wait_ge(ev["wsel"], nth["wsel"])
            pe.wait_ge(ev["cs_prod"], nth["cs_prod"])
            for what, source, done in (("k", sb["roped"][:, :, D:2 * D], ("k0", "k1")),
                                       ("v", qkv[:, :, 2 * D:3 * D], ("v0", "v1"))):
                for part in range(2):
                    if what == "v":
                        pe.wait_ge(ev[f"k{part}_prod"], nth[f"k{part}_prod"])
                    for j in range(8 * part, min(8 * part + 8, KC)):
                        at = j % 8
                        last = nc.tensor.matmul(banks[4 * part + at // 2][:, (at % 2) * SLOTS:(at % 2 + 1) * SLOTS]
                                                .rearrange("p (t c) -> p t c", t=NT),
                                                repeat[:, j, :], source, start=True, stop=True)
                    last.then_inc(ev[done[part]], 1)
            pe.wait_ge(ev["attended"], nth["attended"])
            for t in range(NT):
                last = nc.tensor.transpose(banks[0][:, t * 128:(t + 1) * 128], sb["attended"][:, t * D:(t + 1) * D],
                                           sb["ident"][:])
            last.then_inc(ev["attended_t"], 1)
            pe.wait_ge(ev["attended_sb"], nth["attended_sb"])
            for t in range(NT):
                last = nc.tensor.matmul(banks[1][:, t * D:(t + 1) * D], sb["fT"][:, t * 128:(t + 1) * 128],
                                        sb["c_o"][:], start=True, stop=True)
            last.then_inc(ev["projected"], 1)
            pe.wait_ge(ev["x1n"], nth["x1n"])
            for t in range(NT):
                last = nc.tensor.transpose(banks[0][:, t * 128:(t + 1) * 128], sb["attended"][:, t * D:(t + 1) * D],
                                           sb["ident"][:])
            last.then_inc(ev["x1n_t"], 1)
            pe.wait_ge(ev["x1n_sb"], nth["x1n_sb"])
            for c in range(FF // 128):
                last = nc.tensor.matmul(banks[2 + c // 2][:, (c % 2) * SLOTS:(c % 2 + 1) * SLOTS],
                                        sb["c_w1"][:, c * 128:(c + 1) * 128], sb["x1nT"][:], start=True, stop=True)
            last.then_inc(ev["hidden"], 1)
            pe.wait_ge(ev["gated"], nth["gated"])
            for t in range(NT):
                for c in range(FF // 128):
                    last = nc.tensor.matmul(banks[1][:, t * D:(t + 1) * D],
                                            gate[:, c * SLOTS + t * 128:c * SLOTS + (t + 1) * 128],
                                            sb["c_w2"][:, c * D:(c + 1) * D], start=(c == 0), stop=(c == FF // 128 - 1))
            last.then_inc(ev["ff"], 1)
            pe.wait_ge(ev["spread_x2"], nth["spread_x2"])
            for t in range(NT):
                for g in range(2):
                    last = nc.tensor.matmul(banks[4 + 2 * t + g], sb["selT"][:, t * 128:(t + 1) * 128],
                                            big[:, (2 * t + g) * 512:(2 * t + g + 1) * 512], start=True, stop=True)
            last.then_inc(ev["scattered"], 1)

        @block.scalar
        def _(act):
            def out_of(event, bank, dst, ready):
                act.wait_ge(ev[event], nth[event])
                nc.scalar.activation(dst, bank, ACT.Copy).then_inc(ev[ready], 1)

            out_of("gathered", banks[6][:, 0:SLOTS], sb["xsT"][:], "xsT")
            out_of("masks_u", banks[4][:, 0:SLOTS], sb["umask"][:], "u_ready")
            out_of("selected_t", banks[0][:, 0:SLOTS], sb["selT"][:], "selT_ready")
            act.wait_ge(ev["shifted"], nth["shifted"])
            nc.scalar.activation(att[:], att[:], ACT.Exp).then_inc(ev["exps"], 1)
            out_of("attended_t", banks[0][:, 0:SLOTS], sb["fT"][:], "attended_sb")
            out_of("x1n_t", banks[0][:, 0:SLOTS], sb["x1nT"][:], "x1n_sb")
            act.wait_ge(ev["hidden"], nth["hidden"])
            nc.scalar.activation(hid, ps_all[:, 2:4, :].rearrange("p a c -> p (a c)"), ACT.Copy)\
                .then_inc(ev["hidden_sb"], 1)
            act.wait_ge(ev["inner"], nth["inner"])
            nc.scalar.activation(gate, gate, ACT.Tanh, scale=GELU_C).then_inc(ev["tanhs"], 1)

        @block.gpsimd
        def _(pool):
            pool.wait_ge(ev["eq"], nth["eq"])
            nc.gpsimd.tensor_tensor(PT3, PT3, bc(sb["upper"][:], 1, B), ALU.mult).then_inc(ev["eq_masked"], 1)
            pool.wait_ge(ev["mean_square"], nth["mean_square"])
            nc.gpsimd.tensor_tensor(sb["rms"][:], sb["ss"][:], sb["mhalf"][:].to_broadcast([128, NT]), ALU.pow)\
                .then_inc(ev["rstd"], 1)
            pool.wait_ge(ev["factor"], nth["factor"])
            pool.wait_ge(ev["count_ge"], nth["count_ge"])
            nc.gpsimd.tensor_tensor(P3, X3, bc(sb["factor"][:], 2, D), ALU.mult).then_inc(ev["scaled_x"], 1)
            pool.wait_ge(ev["mean_square2"], nth["mean_square2"])
            nc.gpsimd.tensor_tensor(sb["rms2"][:], sb["ss2"][:], sb["mhalf"][:].to_broadcast([128, NT]), ALU.pow)\
                .then_inc(ev["rstd2"], 1)
            pool.wait_ge(ev["var_eps"], nth["var_eps"])
            nc.gpsimd.tensor_tensor(sb["ln16"][:], sb["ve16"][:], sb["mhalf"][:].to_broadcast([128, B]), ALU.pow)\
                .then_inc(ev["rstd3"], 1)

        @block.vector
        def _(dve):
            def tt(out, a, b_, op, done):
                nc.vector.tensor_tensor(out, a, b_, op).then_inc(ev[done], 1)

            def total(out, in_, done, op=ALU.add):
                nc.vector.tensor_reduce(out, in_, op=op, axis=AX.X).then_inc(ev[done], 1)

            tt(P3, X3, bc(sb["c_rw_row"][:], 1, B), ALU.mult, "weighed")
            dve.wait_ge(ev["weighed"], nth["weighed"])
            total(wt[:], P3, "summed")
            dve.wait_ge(ev["summed"], nth["summed"])
            nc.vector.tensor_scalar(wt[:], wt[:], sb["c_rb"][:], None, ALU.add).then_inc(ev["weights"], 1)
            dve.wait_ge(ev["weights"], nth["weights"])
            nc.vector.tensor_copy(big[:, 0:SB].rearrange("p (b t) -> p b t", b=B), bc(wt[:], 2, S))\
                .then_inc(ev["spread"], 1)
            dve.wait_ge(ev["spread_t"], nth["spread_t"])
            others = scores4.rearrange("p a (b j) -> p (a b) j", j=S)
            tt(PT3, others, bc(wt[:], 2, S), ALU.is_equal, "eq")
            dve.wait_ge(ev["summed"], nth["summed"])
            tt(P3, others, bc(wt[:], 2, S), ALU.is_ge, "ge")
            dve.wait_ge(ev["ge"], nth["ge"])
            total(sb["count_ge"][:], P3, "count_ge")
            dve.wait_ge(ev["eq_masked"], nth["eq_masked"])
            total(sb["count_eq"][:], PT3, "count_eq")
            dve.wait_ge(ev["count_eq"], nth["count_eq"])
            dve.wait_ge(ev["count_ge"], nth["count_ge"])
            tt(rank[:], sb["count_ge"][:], sb["count_eq"][:], ALU.subtract, "rank")
            nc.vector.tensor_scalar(sb["factor"][:], sb["count_ge"][:], KC + 0.5, 1.0, ALU.is_gt, ALU.add)\
                .then_inc(ev["factor"], 1)
            dve.wait_ge(ev["rank"], nth["rank"])
            tt(sel[:], bc(rank[:], 2, TOP), bc(sb["iota"][:], 1, B), ALU.is_equal, "select")
            dve.wait_ge(ev["tables"], nth["tables"])
            prod = sb["cs_prod"]
            for t in range(NT):
                last = nc.vector.tensor_tensor(prod[:, t, :, :],
                                               banks[5][:, t * 64:(t + 1) * 64].rearrange("p (m c) -> p m c", m=MB),
                                               bc(sb["mbatch"][:, t, :], 2, 16), ALU.mult)
            last.then_inc(ev["cs_prod"], 1)
            dve.wait_ge(ev["cs_prod"], nth["cs_prod"])
            total(sb["cs"][:], prod[:].rearrange("p t m c -> p t c m"), "cs_ready")
            dve.wait_ge(ev["tokens"], nth["tokens"])
            tokens = sb["tokens"]
            nc.vector.tensor_copy(tokens[:].rearrange("p t d -> p (t d)"), banks[7][:, 0:SLOTS])\
                .then_inc(ev["tokens_ready"], 1)
            dve.wait_ge(ev["tokens_ready"], nth["tokens_ready"])
            tt(sb["sq"][:], tokens[:], tokens[:], ALU.mult, "squares")
            dve.wait_ge(ev["squares"], nth["squares"])
            total(sb["ss"][:], sb["sq"][:], "square_sum")
            dve.wait_ge(ev["square_sum"], nth["square_sum"])
            nc.vector.tensor_scalar(sb["ss"][:], sb["ss"][:], 1.0 / D, RMS_EPS, ALU.mult, ALU.add)\
                .then_inc(ev["mean_square"], 1)
            dve.wait_ge(ev["qkv"], nth["qkv"])
            nc.vector.tensor_scalar(sb["wsel"][:], banks[3][:, 0:NT], sb["c_rb"][:], sb["valid"][:],
                                    ALU.add, ALU.mult).then_inc(ev["wsel"], 1)
            dve.wait_ge(ev["dense_mask"], nth["dense_mask"])
            tt(sb["mprod"][:].rearrange("p t b r -> p (t b) r"),
               banks[6][:, 0:SLOTS].rearrange("p (x r) -> p x r", r=TOP),
               bc(sb["blocks2"][:].rearrange("p t b -> p (t b)"), 2, TOP), ALU.mult, "mask_prod")
            dve.wait_ge(ev["mask_prod"], nth["mask_prod"])
            total(sb["msel"][:], sb["mprod"][:].rearrange("p t b r -> p t r b"), "mask_ready")
            dve.wait_ge(ev["rstd"], nth["rstd"])
            tt(qkv[:], ps_all[:, 1:3, 0:3 * D], bc(sb["rms"][:], 2, 3 * D), ALU.mult, "qkv_ready")
            dve.wait_ge(ev["qkv_ready"], nth["qkv_ready"])
            dve.wait_ge(ev["cs_ready"], nth["cs_ready"])
            HH = HD // 2
            for t in range(NT):
                last = nc.vector.tensor_tensor(rot[:, t, :, 0:HH], qk[:, t, :, HH:HD],
                                               bc(sb["cs"][:, t, HD:HD + HH], 1, 2 * H), ALU.mult)
                last = nc.vector.tensor_tensor(rot[:, t, :, HH:HD], qk[:, t, :, 0:HH],
                                               bc(sb["cs"][:, t, HD + HH:2 * HD], 1, 2 * H), ALU.mult)
            last.then_inc(ev["rot_sin"], 1)
            for t in range(NT):
                last = nc.vector.tensor_tensor(roped[:, t, :, :], qk[:, t, :, :],
                                               bc(sb["cs"][:, t, 0:HD], 1, 2 * H), ALU.mult)
            last.then_inc(ev["rot_cos"], 1)
            dve.wait_ge(ev["rot_sin"], nth["rot_sin"])
            dve.wait_ge(ev["rot_cos"], nth["rot_cos"])
            tt(sb["roped"][:], sb["roped"][:], sb["rot"][:], ALU.add, "roped")
            dve.wait_ge(ev["roped"], nth["roped"])
            for part, src in ((0, scores4), (1, upper4)):
                n = min(8, KC - 8 * part)
                js = slice(8 * part, 8 * part + n)
                dve.wait_ge(ev[f"k{part}"], nth[f"k{part}"])
                flat = src.rearrange("p a (j t c) -> p (a j) t c", j=2, t=NT)
                for t in range(NT):
                    last = nc.vector.tensor_tensor(keys[:, js, t * D:(t + 1) * D], flat[:, 0:n, t, :],
                                                   bc(sb["roped"][:, t, 0:D], 1, n), ALU.mult)
                last.then_inc(ev[f"k{part}_prod"], 1)
                dve.wait_ge(ev[f"k{part}_prod"], nth[f"k{part}_prod"])
                total(att[:, :, js].rearrange("p x j -> p j x"),
                      keys[:, js, :].rearrange("p j (x c) -> p j x c", c=HD), f"k{part}_sum")
            dve.wait_ge(ev["k0_sum"], nth["k0_sum"])
            dve.wait_ge(ev["k1_sum"], nth["k1_sum"])
            dve.wait_ge(ev["mask_ready"], nth["mask_ready"])
            for t in range(NT):
                rows = att[:, t * H:(t + 1) * H, :]
                last = nc.vector.tensor_tensor(rows, rows, bc(sb["msel"][:, t, 0:KC], 1, H), ALU.add)
            last.then_inc(ev["masked"], 1)
            dve.wait_ge(ev["masked"], nth["masked"])
            total(sb["rmax"][:], att[:], "row_max", ALU.max)
            dve.wait_ge(ev["row_max"], nth["row_max"])
            tt(att[:], att[:], bc(sb["rmax"][:], 2, KC), ALU.subtract, "shifted")
            dve.wait_ge(ev["exps"], nth["exps"])
            total(sb["rsum32"][:], att[:], "row_sum")
            dve.wait_ge(ev["row_sum"], nth["row_sum"])
            nc.vector.reciprocal(sb["rmax"][:], sb["rsum32"][:]).then_inc(ev["row_inv"], 1)
            for part, src in ((0, scores4), (1, upper4)):
                n = min(8, KC - 8 * part)
                js = slice(8 * part, 8 * part + n)
                dve.wait_ge(ev[f"v{part}"], nth[f"v{part}"])
                nc.vector.tensor_tensor(keys[:, js, :].rearrange("p j (x c) -> p j x c", c=HD),
                                        src.rearrange("p a (j x c) -> p (a j) x c", j=2, c=HD)[:, 0:n, :, :],
                                        bc(att[:, :, js].rearrange("p x j -> p j x"), 3, HD), ALU.mult)\
                    .then_inc(ev[f"v{part}_prod"], 1)
            dve.wait_ge(ev["v0_prod"], nth["v0_prod"])
            dve.wait_ge(ev["v1_prod"], nth["v1_prod"])
            total(sb["vsum"][:], keys[:, 0:KC, :].rearrange("p j c -> p c j"), "v_sum")
            dve.wait_ge(ev["v_sum"], nth["v_sum"])
            dve.wait_ge(ev["row_inv"], nth["row_inv"])
            tt(sb["attended"][:].rearrange("p (x c) -> p x c", c=HD), sb["vsum"][:].rearrange("p (x c) -> p x c", c=HD),
               bc(sb["rmax"][:], 2, HD), ALU.mult, "attended")
            dve.wait_ge(ev["projected"], nth["projected"])
            x1 = sb["x1"]
            tt(x1[:].rearrange("p t d -> p (t d)"), banks[1][:, 0:SLOTS],
               tokens[:].rearrange("p t d -> p (t d)"), ALU.add, "x1")
            dve.wait_ge(ev["x1"], nth["x1"])
            tt(sb["sq"][:], x1[:], x1[:], ALU.mult, "squares2")
            dve.wait_ge(ev["squares2"], nth["squares2"])
            total(sb["ss2"][:], sb["sq"][:], "square_sum2")
            dve.wait_ge(ev["square_sum2"], nth["square_sum2"])
            nc.vector.tensor_scalar(sb["ss2"][:], sb["ss2"][:], 1.0 / D, RMS_EPS, ALU.mult, ALU.add)\
                .then_inc(ev["mean_square2"], 1)
            dve.wait_ge(ev["rstd2"], nth["rstd2"])
            dve.wait_ge(ev["attended_t"], nth["attended_t"])
            tt(sb["attended"][:].rearrange("p (t d) -> p t d", t=NT), x1[:], bc(sb["rms2"][:], 2, D), ALU.mult, "x1n")
            dve.wait_ge(ev["hidden_sb"], nth["hidden_sb"])
            nc.vector.scalar_tensor_tensor(out=gate, in0=hid, scalar=0.044715, in1=hid,
                                           op0=ALU.mult, op1=ALU.mult).then_inc(ev["cubed"], 1)
            dve.wait_ge(ev["cubed"], nth["cubed"])
            nc.vector.scalar_tensor_tensor(out=gate, in0=gate, scalar=1.0, in1=hid,
                                           op0=ALU.add, op1=ALU.mult).then_inc(ev["inner"], 1)
            dve.wait_ge(ev["tanhs"], nth["tanhs"])
            nc.vector.scalar_tensor_tensor(out=gate, in0=gate, scalar=1.0, in1=hid,
                                           op0=ALU.add, op1=ALU.mult).then_inc(ev["gated"], 1)
            for t in range(NT):
                last = nc.vector.tensor_scalar(sb["slot_w"][:, t, :], sb["blocks2"][:, t, :], sb["wsel"][:, t:t + 1],
                                               None, ALU.mult)
            last.then_inc(ev["slot_w"], 1)
            dve.wait_ge(ev["ff"], nth["ff"])
            tt(x1[:].rearrange("p t d -> p (t d)"), banks[1][:, 0:SLOTS], x1[:].rearrange("p t d -> p (t d)"),
               ALU.add, "x2")
            dve.wait_ge(ev["x2"], nth["x2"])
            dve.wait_ge(ev["slot_w"], nth["slot_w"])
            spread = big[:, 0:SB].rearrange("p (t b d) -> p t b d", t=NT, b=NB)
            for t in range(NT):
                last = nc.vector.tensor_tensor(spread[:, t, :, :], bc(x1[:, t, :], 1, NB), bc(sb["slot_w"][:, t, :], 2, D),
                                               ALU.mult)
            last.then_inc(ev["spread_x2"], 1)
            dve.wait_ge(ev["scattered"], nth["scattered"])
            dve.wait_ge(ev["scaled_x"], nth["scaled_x"])
            dve.wait_ge(ev["count_eq"], nth["count_eq"])
            tt(PT3, upper4.rearrange("p a (b d) -> p (a b) d", d=D), P3, ALU.add, "y")
            dve.wait_ge(ev["y"], nth["y"])
            for b in range(B):
                nc.vector.bn_stats(sb["bn16"][:, b, :], PT3[:, b, :])
            nc.vector.drain()
            for b in range(B):
                last = nc.vector.bn_aggr(sb["mv16"][:, b, :], sb["bn16"][:, b, :])
            last.then_inc(ev["aggregated"], 1)
            dve.wait_ge(ev["aggregated"], nth["aggregated"])
            nc.vector.tensor_scalar(sb["ve16"][:], sb["mv16"][:, :, 1], LN_EPS, None, ALU.add)\
                .then_inc(ev["var_eps"], 1)
            tt(PT3, PT3, bc(sb["mv16"][:, :, 0], 2, D), ALU.subtract, "centred")
            dve.wait_ge(ev["rstd3"], nth["rstd3"])
            dve.wait_ge(ev["centred"], nth["centred"])
            tt(X3, PT3, bc(sb["ln16"][:], 2, D), ALU.mult, "x_new")
            dve.wait_ge(ev["x_new"], nth["x_new"])


def wide_head_attention(nc, ps, sb, X, xs):
    S_ps, PT_ps, O_ps, M_ps = ps
    with ExitStack() as ctx:
        def sem(what):
            return ctx.enter_context(nc.semaphore(f"wide_{what}"))

        x_loaded = [sem("x_loaded0"), sem("x_loaded1")]
        xt_done, xt_ready = sem("xt_done"), sem("xt_ready")
        q_done, q_ready, k_done, k_ready = sem("q_done"), sem("q_ready"), sem("k_done"), sem("k_ready")
        v_done, v_ready = sem("v_done"), sem("v_ready")
        s_done, max_ready, sub_ready, exp_ready = sem("s_done"), sem("max_ready"), sem("sub_ready"), sem("exp_ready")
        sum_ready, inv_ready, p_ready = sem("sum_ready"), sem("inv_ready"), sem("p_ready")
        pt_done, pt_ready, pv_done, o_ready = sem("pt_done"), sem("pt_ready"), sem("pv_done"), sem("o_ready")
        out_done, xb_ready, y_ready = sem("out_done"), sem("xb_ready"), sem("y_ready")
        var1_ready, rstd1_ready, yn_ready, y2_ready = (
            sem("var1_ready"), sem("rstd1_ready"), sem("yn_ready"), sem("y2_ready"))
        var2_ready, rstd2_ready, x_new, pool_step = sem("var2_ready"), sem("rstd2_ready"), sem("x_new"), sem("pool_step")
        block = ctx.enter_context(nc.Block())
        HP = PAIRS // 2
        PW = 3 * HW

        @block.sync
        def _(sp):
            def slot(i, p, half):
                b = i + LEAD
                if has(b):
                    after(sp, xt_done, b - 1)
                    sp.dma_start(xs[:, p, :], one(X, b)).then_inc(x_loaded[p], 16)
            slots(sp, slot)

        @block.tensor
        def _(pe):
            def scores(b, u, p, g):
                if g == 0:
                    pe.wait_ge(q_ready, 2 * b + u + 1)
                    pe.wait_ge(k_ready, 2 * b + u + 1)
                    after(pe, sub_ready, 2 * b + u - 1)
                for e in range(2):
                    pair = HP * u + 2 * g + e
                    last = nc.tensor.matmul(S_ps[:, 2 * u + g, e * 2 * S:(e + 1) * 2 * S], sb["QW"][:, p, pair, :],
                                            sb["KW"][:, p, pair, :, :].rearrange("p e k -> p (e k)"),
                                            start=True, stop=True)
                if g == 1:
                    last.then_inc(s_done, 1)

            def transpose_probs(b, u):
                pe.wait_ge(p_ready, 2 * b + u + 1)
                after(pe, pt_ready, 2 * b + u)
                for h in range(UH):
                    last = nc.tensor.transpose(PT_ps[:, h // 4, (h % 4) * S:(h % 4 + 1) * S],
                                               sb["P"][:, u, h, :], sb["ident"][:])
                last.then_inc(pt_done, 1)

            def values(b, u, p, g):
                if g == 0:
                    pe.wait_ge(pt_ready, 2 * b + u + 1)
                    pe.wait_ge(v_ready, 2 * b + u + 1)
                    after(pe, o_ready, 2 * b + u)
                for e in range(4):
                    h = 4 * g + e
                    at = (HP * u + h // 2) * PW + (h % 2) * HW
                    last = nc.tensor.matmul(O_ps[:, (h // 2) * S:(h // 2 + 1) * S], sb["VW"][:, p, at:at + 128],
                                            sb["PT"][:, u, h, :], start=(h % 2 == 0), stop=(h % 2 == 1))
                if g == 1:
                    last.then_inc(pv_done, 1)

            def project(weight, n, q, c, done):
                for e in range(HP):
                    pair = HP * c + e
                    last = nc.tensor.matmul(M_ps[:, e * S:(e + 1) * S], weight[:, pair * 128:(pair + 1) * 128],
                                            sb["xT"][:, q, :], start=True, stop=True)
                last.then_inc(done, 1)

            def slot(i, p, half):
                q = 1 - p
                b, n, r, z = i + LEAD, i + 1, i - 1, i - LAG
                if has(z):
                    if has(n):
                        pe.wait_ge(xt_ready, n + 1)
                    if has(r):
                        pe.wait_ge(v_ready, 2 * i)
                    after(pe, y_ready, z)
                    pe.wait_ge(o_ready, 2 * z + 2)
                    for c in range(PAIRS):
                        last = nc.tensor.matmul(M_ps[:, 0:D], sb["OT"][:, c // HP, (c % HP) * S:(c % HP + 1) * S],
                                                sb["d_o"][:, c * D:(c + 1) * D], start=(c == 0), stop=(c == PAIRS - 1))
                    last.then_inc(out_done, 1)
                if has(i):
                    scores(i, 1, p, 0)
                if has(n):
                    pe.wait_ge(xt_ready, n + 1)
                    after(pe, y_ready, i - 1)
                    project(sb["d_q"], n, q, 0, q_done)
                if has(i):
                    scores(i, 1, p, 1)
                if has(n):
                    pe.wait_ge(q_ready, 2 * n + 1)
                    project(sb["d_q"], n, q, 1, q_done)
                if has(r):
                    transpose_probs(r, 1)
                if has(n):
                    pe.wait_ge(q_ready, 2 * n + 2)
                    project(sb["d_k"], n, q, 0, k_done)
                if has(r):
                    values(r, 0, q, 0)
                if has(n):
                    pe.wait_ge(k_ready, 2 * n + 1)
                    project(sb["d_k"], n, q, 1, k_done)
                if has(r):
                    values(r, 0, q, 1)
                if has(n):
                    scores(n, 0, q, 0)
                if has(i):
                    if has(n):
                        pe.wait_ge(k_ready, 2 * n + 2)
                    after(pe, y_ready, i - 1)
                    nc.tensor.matmul(M_ps[:], sb["xT"][:, p, :], sb["d_v"][:, 0:512], start=True, stop=True)\
                        .then_inc(v_done, 1)
                if has(n):
                    scores(n, 0, q, 1)
                if has(i):
                    pe.wait_ge(v_ready, 2 * i + 1)
                    nc.tensor.matmul(M_ps[:], sb["xT"][:, p, :], sb["d_v"][:, 512:1024], start=True, stop=True)\
                        .then_inc(v_done, 1)
                    transpose_probs(i, 0)
                if has(r):
                    values(r, 1, q, 0)
                if has(b):
                    pe.wait_ge(x_loaded[p], (half + 2) * 16)
                    if has(i):
                        pe.wait_ge(v_ready, 2 * i + 2)
                    elif has(n):
                        pe.wait_ge(k_ready, 2 * n + 2)
                    nc.tensor.transpose(M_ps[:, 0:S], xs[:, p, :], sb["ident"][:]).then_inc(xt_done, 1)
                if has(r):
                    values(r, 1, q, 1)
            slots(pe, slot)

        @block.scalar
        def _(act):
            def exps(b, u):
                act.wait_ge(sub_ready, 2 * b + u + 1)
                nc.scalar.activation(sb["P"][:, u, :, :], sb["P"][:, u, :, :], ACT.Exp).then_inc(exp_ready, 1)

            def probs_out(b, u):
                act.wait_ge(pt_done, 2 * b + u + 1)
                after(act, pv_done, 2 * b + u - 1)
                nc.scalar.activation(sb["PT"][:, u, :, :].rearrange("p h q -> p (h q)"),
                                     PT_ps[:].rearrange("p a c -> p (a c)"), ACT.Copy).then_inc(pt_ready, 1)

            def queries_out(n, q, c):
                act.wait_ge(q_done, 2 * n + c + 1)
                after(act, s_done, 2 * (n - 2) + c + 1)
                for e in range(HP):
                    pair = HP * c + e
                    last = nc.scalar.activation(sb["QW"][:, q, pair, :], M_ps[:, e * S:(e + 1) * S], ACT.Identity,
                                                bias=sb["d_qbs"][:, pair:pair + 1], scale=sb["d_qs"][:, pair:pair + 1])
                last.then_inc(q_ready, 1)

            def values_out(b, p, c):
                act.wait_ge(v_done, 2 * b + c + 1)
                after(act, pv_done, 2 * (b - 2) + c + 1)
                pairs = sb["VW"][:, p, c * HP * PW:(c + 1) * HP * PW].rearrange("p (a w) -> p a w", a=HP)
                for e in range(2):
                    last = nc.scalar.activation(pairs[:, :, 2 * e * HW:(2 * e + 1) * HW],
                                                M_ps[:].rearrange("p (a e w) -> p a e w", a=HP, e=2)[:, :, e, :],
                                                ACT.Copy)
                last.then_inc(v_ready, 1)

            def output_out(b, u):
                act.wait_ge(pv_done, 2 * b + u + 1)
                after(act, out_done, b)
                nc.scalar.activation(sb["OT"][:, u, :], O_ps[:], ACT.Copy).then_inc(o_ready, 1)

            def slot(i, p, half):
                b, n, r = i + LEAD, i + 1, i - 1
                if has(n):
                    queries_out(n, 1 - p, 0)
                    queries_out(n, 1 - p, 1)
                if has(r):
                    probs_out(r, 1)
                if has(i):
                    exps(i, 1)
                if has(r):
                    output_out(r, 0)
                if has(i):
                    values_out(i, p, 0)
                    values_out(i, p, 1)
                    probs_out(i, 0)
                if has(b):
                    act.wait_ge(xt_done, b + 1)
                    after(act, v_done, 2 * i + 2)
                    nc.scalar.activation(sb["xT"][:, p, :], M_ps[:, 0:S], ACT.Copy).then_inc(xt_ready, 1)
                if has(n):
                    exps(n, 0)
                if has(r):
                    output_out(r, 1)
            slots(act, slot)

        @block.vector
        def _(dve):
            def shift(b, u):
                unit = S_ps[:, 2 * u:2 * u + 2, :].rearrange("p a (h k) -> p (a h) k", k=S)
                dve.wait_ge(s_done, 2 * b + u + 1)
                after(dve, sub_ready, 2 * b + u)
                nc.vector.tensor_reduce(sb["mx"][:], unit, op=ALU.max, axis=AX.X).then_inc(max_ready, 1)
                dve.wait_ge(max_ready, 2 * b + u + 1)
                after(dve, pt_done, 2 * b + u - 1)
                nc.vector.tensor_tensor(sb["P"][:, u, :, :], unit, bc(sb["mx"][:], 2, S), ALU.subtract)\
                    .then_inc(sub_ready, 1)

            def inverse_sums(b, u):
                dve.wait_ge(exp_ready, 2 * b + u + 1)
                nc.vector.tensor_reduce(sb["rsum"][:, u, :], sb["P"][:, u, :, :], op=ALU.add, axis=AX.X)\
                    .then_inc(sum_ready, 1)
                dve.wait_ge(sum_ready, 2 * b + u + 1)
                after(dve, p_ready, 2 * b + u - 1)
                nc.vector.reciprocal(sb["rinv"][:, u, :], sb["rsum"][:, u, :]).then_inc(inv_ready, 1)

            def keys_out(n, q, c):
                dve.wait_ge(k_done, 2 * n + c + 1)
                after(dve, s_done, 2 * (n - 2) + c + 1)
                pairs = slice(c * HP, (c + 1) * HP)
                for e in range(2):
                    rows = slice(e * HW, (e + 1) * HW)
                    last = nc.vector.tensor_tensor(sb["KW"][rows, q, pairs, e, :],
                                                   M_ps[rows, :].rearrange("p (a k) -> p a k", a=HP),
                                                   bc(sb["d_kb"][rows, pairs], 2, S), ALU.add)
                last.then_inc(k_ready, 1)

            def slot(i, p, half):
                n, z = i + 1, i - LAG
                if has(i):
                    inverse_sums(i, 0)
                if has(z):
                    dve.wait_ge(out_done, z + 1)
                    dve.wait_ge(xb_ready, z + 1)
                    after(dve, yn_ready, z)
                    nc.vector.tensor_tensor(sb["Y"][:], M_ps[:, 0:D], sb["XB"][:, p, :], ALU.add).then_inc(y_ready, 1)
                    dve.wait_ge(y_ready, z + 1)
                    nc.vector.bn_stats(sb["bn"][:], sb["Y"][:])
                    nc.vector.drain()
                    nc.vector.bn_aggr(sb["mv"][:], sb["bn"][:]).then_inc(var1_ready, 1)
                if has(i):
                    shift(i, 1)
                if has(z):
                    dve.wait_ge(rstd1_ready, z + 1)
                    after(dve, y2_ready, z)
                    nc.vector.tensor_scalar(sb["YN"][:], sb["Y"][:], sb["mv"][:, 0:1], sb["rstd"][:],
                                            ALU.subtract, ALU.mult).then_inc(yn_ready, 1)
                if has(n):
                    keys_out(n, 1 - p, 0)
                    keys_out(n, 1 - p, 1)
                if has(i):
                    inverse_sums(i, 1)
                if has(z):
                    dve.wait_ge(y2_ready, z + 1)
                    nc.vector.bn_stats(sb["bn2"][:], sb["Y2"][:])
                    nc.vector.drain()
                    nc.vector.bn_aggr(sb["mv2"][:], sb["bn2"][:]).then_inc(var2_ready, 1)
                if has(n):
                    shift(n, 0)
                if has(z):
                    dve.wait_ge(rstd2_ready, z + 1)
                    nc.vector.tensor_scalar(one(X, z), sb["Y2"][:], sb["mv2"][:, 0:1], sb["rstd2"][:],
                                            ALU.subtract, ALU.mult).then_inc(x_new, 1)
            slots(dve, slot)

        @block.gpsimd
        def _(pool):
            def normalise(b, u):
                pool.wait_ge(inv_ready, 2 * b + u + 1)
                nc.gpsimd.tensor_tensor(sb["P"][:, u, :, :], sb["P"][:, u, :, :], bc(sb["rinv"][:, u, :], 2, S),
                                        ALU.mult).then_inc(p_ready, 1)

            def rstd(z, k, var, mv, out, ready):
                pool.wait_ge(var, z + 1)
                nc.gpsimd.tensor_tensor(sb["ve"][:], sb[mv][:, 1:2], sb["eps"][:], ALU.add).then_inc(pool_step, 1)
                pool.wait_ge(pool_step, 3 * z + k)
                nc.gpsimd.tensor_tensor(sb[out][:], sb["ve"][:], sb["mhalf"][:], ALU.pow).then_inc(ready, 1)

            def slot(i, p, half):
                r, z = i - 1, i - LAG
                if has(i):
                    normalise(i, 0)
                if has(z):
                    rstd(z, 1, var1_ready, "mv", "rstd", rstd1_ready)
                    pool.wait_ge(yn_ready, z + 1)
                    after(pool, x_new, z)
                    nc.gpsimd.tensor_tensor(sb["Y2"][:], sb["YN"][:], sb["gamma"][:], ALU.mult).then_inc(pool_step, 1)
                    pool.wait_ge(pool_step, 3 * z + 2)
                    nc.gpsimd.tensor_tensor(sb["Y2"][:], sb["Y2"][:], sb["XG"][:, p, :], ALU.add)\
                        .then_inc(y2_ready, 1)
                if has(r):
                    after(pool, y_ready, r - 1)
                    after(pool, y2_ready, r - 1)
                    nc.gpsimd.tensor_tensor(sb["XB"][:, 1 - p, :], one(X, r), sb["d_bias"][:], ALU.add)\
                        .then_inc(xb_ready, 1)
                    nc.gpsimd.tensor_tensor(sb["XG"][:, 1 - p, :], one(X, r), sb["beta"][:], ALU.add)
                if has(i):
                    normalise(i, 1)
                if has(z):
                    rstd(z, 3, var2_ready, "mv2", "rstd2", rstd2_ready)
            slots(pool, slot)


def recurrent_ffn(nc, ps_all, sb, X, out):
    with ExitStack() as ctx:
        ev, nth = counted(nc, ctx, "rec", tensor="xt_done own_done carried", scalar="xt_ready", vector="carried_sb")
        f_ready, g_ready, kept, added, c_ready = (
            ctx.enter_context(nc.semaphore(f"rec_{n}")) for n in ("f_ready", "g_ready", "kept", "added", "c_ready"))
        gates = ctx.enter_context(nc.semaphore("rec_gates"))
        tail = {n: ctx.enter_context(nc.semaphore(f"rec_{n}"))
                for n in ("pre", "act", "residual", "stats", "var", "rstd", "shift", "normed", "stored")}
        block = ctx.enter_context(nc.Block())
        XT = sb["P"][:].rearrange("p u h k -> p (u h) k")
        hid = sb["PT"][:].rearrange("p u h k -> p (u h) k")
        CH = 4
        chunks = [slice(c * CH, (c + 1) * CH) for c in range(B // CH)]
        gate = [[ps_all[:, p, 0:S], ps_all[:, 6 + p, 0:S], ps_all[:, 6 + p, S:2 * S]] for p in range(2)]
        own = ps_all[:, 2:6, :].rearrange("p a (b d) -> p (a b) d", d=D)
        c2, f, i, g = sb["c2"], sb["fg"], sb["ig"], sb["gg"]

        @block.tensor
        def _(pe):
            for b in range(B):
                last = nc.tensor.transpose(own[:, b, :], X[:, b, :], sb["ident"][:])
            last.then_inc(ev["xt_done"], 1)

            def from_input(t, p):
                for n in range(3):
                    nc.tensor.matmul(gate[p][n], sb["r_w"][:, n * D:(n + 1) * D], one(XT, t),
                                     start=(n < 2), stop=False, skip_group_check=True)

            def from_state(p, done):
                for n in range(3):
                    nc.tensor.matmul(gate[p][n], sb["r_u"][:, n * D:(n + 1) * D], c2[:, p, :],
                                     start=False, stop=True, skip_group_check=True).then_inc(done, 1)

            pe.wait_ge(ev["xt_ready"], nth["xt_ready"])
            from_input(0, 0)
            pe.wait_ge(c_ready, 1)
            from_state(0, gates)
            for b in range(B):
                last = nc.tensor.matmul(own[:, b, :], XT[:, b, :], sb["r_wo"][:], start=True, stop=True)
            last.then_inc(ev["own_done"], 1)
            from_input(1, 1)
            pe.wait_ge(c_ready, 2)
            from_state(1, gates)
            with pe.Fori(1, B // 2) as j:
                for p in range(2):
                    t = j * 2 + p
                    pe.wait_ge(g_ready, t - 1)
                    from_input(t, p)
                    pe.wait_ge(c_ready, t + 1)
                    from_state(p, gates)
            pe.wait_ge(c_ready, B + 1)
            pe.wait_ge(g_ready, B - 1)
            nc.tensor.matmul(gate[0][0], c2[:, 0, :], sb["r_uo"][:], start=True, stop=True)\
                .then_inc(ev["carried"], 1)

        @block.scalar
        def _(act):
            act.wait_ge(ev["xt_done"], nth["xt_done"])
            nc.scalar.activation(XT.rearrange("p b s -> p (b s)"), own.rearrange("p b s -> p (b s)"), ACT.Copy)\
                .then_inc(ev["xt_ready"], 1)

            def step(t, p, first):
                act.wait_ge(gates, t * 3 + 1)
                if not first:
                    act.wait_ge(kept, t)
                nc.scalar.activation(f[:], gate[p][0], ACT.Tanh, bias=sb["r_bf"][:], scale=0.5)\
                    .then_inc(f_ready, 1)
                act.wait_ge(gates, t * 3 + 3)
                if not first:
                    act.wait_ge(added, t)
                nc.scalar.activation(i[:], gate[p][1], ACT.Tanh, bias=sb["r_bi"][:], scale=0.5)
                nc.scalar.activation(g[:], gate[p][2], ACT.Tanh, bias=sb["r_bc"][:])\
                    .then_inc(g_ready, 1)

            step(0, 0, True)
            step(1, 1, False)
            with act.Fori(1, B // 2) as j:
                for p in range(2):
                    step(j * 2 + p, p, False)
            for c, steps in enumerate(chunks):
                act.wait_ge(tail["pre"], c + 1)
                nc.scalar.activation(hid[:, steps, :], hid[:, steps, :], ACT.Tanh).then_inc(tail["act"], 1)
            for c, steps in enumerate(chunks):
                act.wait_ge(tail["shift"], c + 1)
                for b in range(c * CH, (c + 1) * CH):
                    last = nc.scalar.activation(hid[:, b, :], hid[:, b, :], ACT.Identity,
                                                bias=sb["nshift"][:, b:b + 1], scale=sb["ln16"][:, b:b + 1])
                last.then_inc(tail["normed"], 1)

        @block.vector
        def _(dve):
            nc.vector.tensor_copy(c2[:, 0, :], sb["r_c0"][:].to_broadcast([D, S])).then_inc(c_ready, 1)

            def step(t, p):
                dve.wait_ge(f_ready, t + 1)
                nc.vector.scalar_tensor_tensor(out=sb["ca"][:], in0=f[:], scalar=1.0, in1=c2[:, p, :],
                                               op0=ALU.add, op1=ALU.mult).then_inc(kept, 1)
                dve.wait_ge(g_ready, t + 1)
                nc.vector.scalar_tensor_tensor(out=sb["cb"][:], in0=i[:], scalar=1.0, in1=g[:],
                                               op0=ALU.add, op1=ALU.mult).then_inc(added, 1)
                dve.wait_ge(added, t + 1)
                dve.wait_ge(kept, t + 1)
                nc.vector.scalar_tensor_tensor(out=c2[:, 1 - p, :], in0=sb["ca"][:], scalar=0.5, in1=sb["cb"][:],
                                               op0=ALU.mult, op1=ALU.add).then_inc(c_ready, 1)

            dve.wait_ge(c_ready, 1)
            step(0, 0)
            with dve.Fori(0, B // 2 - 1) as j:
                for p in (1, 0):
                    t = j * 2 + (2 - p)
                    dve.wait_ge(c_ready, t + 1)
                    dve.wait_ge(gates, t * 3)
                    step(t, p)
            dve.wait_ge(c_ready, B)
            dve.wait_ge(gates, 3 * B - 3)
            step(B - 1, 1)
            dve.wait_ge(ev["carried"], nth["carried"])
            nc.vector.tensor_tensor(sb["cu"][:], gate[0][0], sb["r_bo"][:], ALU.add)\
                .then_inc(ev["carried_sb"], 1)
            dve.wait_ge(ev["carried_sb"], nth["carried_sb"])
            dve.wait_ge(ev["own_done"], nth["own_done"])
            for c, steps in enumerate(chunks):
                nc.vector.tensor_tensor(hid[:, steps, :], own[:, steps, :], bc(sb["cu"][:], 1, CH), ALU.add)\
                    .then_inc(tail["pre"], 1)
            for c, steps in enumerate(chunks):
                dve.wait_ge(tail["residual"], c + 1)
                for b in range(c * CH, (c + 1) * CH):
                    nc.vector.bn_stats(sb["bn16"][:, b, :], hid[:, b, :])
                nc.vector.drain()
                for b in range(c * CH, (c + 1) * CH):
                    last = nc.vector.bn_aggr(sb["mv16"][:, b, :], sb["bn16"][:, b, :])
                last.then_inc(tail["stats"], 1)
                dve.wait_ge(tail["stats"], c + 1)
                nc.vector.tensor_scalar(sb["ve16"][:, steps], sb["mv16"][:, steps, 1], LN_EPS, None, ALU.add)\
                    .then_inc(tail["var"], 1)
            for c, steps in enumerate(chunks):
                dve.wait_ge(tail["rstd"], c + 1)
                nc.vector.scalar_tensor_tensor(out=sb["nshift"][:, steps], in0=sb["mv16"][:, steps, 0], scalar=-1.0,
                                               in1=sb["ln16"][:, steps], op0=ALU.mult, op1=ALU.mult)\
                    .then_inc(tail["shift"], 1)

        @block.gpsimd
        def _(pool):
            for c, steps in enumerate(chunks):
                pool.wait_ge(tail["act"], c + 1)
                nc.gpsimd.tensor_tensor(hid[:, steps, :], hid[:, steps, :], X[:, steps, :], ALU.add)\
                    .then_inc(tail["residual"], 1)
            for c, steps in enumerate(chunks):
                pool.wait_ge(tail["var"], c + 1)
                nc.gpsimd.tensor_tensor(sb["ln16"][:, steps], sb["ve16"][:, steps],
                                        sb["mhalf"][:].to_broadcast([S, CH]), ALU.pow).then_inc(tail["rstd"], 1)

        @block.sync
        def _(sp):
            for c, steps in enumerate(chunks):
                sp.wait_ge(tail["normed"], c + 1)
                sp.dma_start(out[steps, :, :].rearrange("b s d -> s b d"), hid[:, steps, :]).then_inc(tail["stored"], 16)
            sp.wait_ge(tail["stored"], 16 * len(chunks))


def decoder(nc, dram, out, layers=(1, 2, 3, 4, 5, 6)):
    with ExitStack() as ctx:
        def buf(name, shape, dt=F32):
            return ctx.enter_context(nc.sbuf_tensor(name, shape, dt))

        banks = ctx.enter_context(nc.psum_tensor("banks", [128, 8, 512], F32))
        ps = [banks[:, 0:4, :], banks[:, 4:6, :], banks[:, 6, :], banks[:, 7, :]]
        X = buf("X", [S, B, D])
        xs = buf("xs", [S, 2, D])
        width = {}
        for name, at, _, rows, columns in WEIGHTS:
            width[name] = (rows, at + columns)
        sb = {name: buf(name, list(shape)) for name, shape in width.items()}
        for name, shape in dict(
                a_k=[D, D], a_v=[D, D], a_kb=[D, 1], a_vb=[D, 1], a_qb=[D, 1], a_bl=[LAT, 1], a_bk=[D, 1],
                a_bv=[D, 1], a_bo=[S, D], a_bias=[S, D], b_qr=[D, D], b_kr=[D, D], b_bias=[S, D],
                e_qb=[D, 1], e_kb=[D, 1], e_bv=[D, 1], e_bp=[S, D], e_bias=[S, D],
                ident=[128, 128], headmask=[D, H], causalf=[S, S], inv=[D, 1], pos=[D, S], ones=[128, 128],
                spread=[D, PAIRS * D], turns=[D, S + 4 * MB], angle=[D, S + 4 * MB], ang=[D, 2, S + 4 * MB],
                trig=[D, 2, S + 4 * MB], rope=[D, 4, S],
                kmask=[D, B, S], mhalf=[S, 1], eps=[S, 1], a_qbs=[D, 1], e_qbs=[D, 1],
                xT=[D, 2, S], cT=[D, 2, S], QT=[D, 2, S], KT=[D, S], RP=[D, 4 * S], Kx=[128, 2, H, S],
                Vx=[S, 2, H * SLOT * 9 // 1], P=[S, 2, UH, S], PT=[S, 2, UH, S], mx=[S, UH], O=[128, 2 * S],
                rden=[S, H], ON=[S, D], ONT=[D, S], XB=[S, 2, D], Y=[S, D], bn=[S, 6], mv=[S, 2], ve=[S, 1],
                rstd=[S, 1], d_as=[128, PAIRS], d_qs=[128, PAIRS], d_qbs=[128, PAIRS], d_bo=[S, D], d_bias=[S, D],
                gamma=[S, D], beta=[S, D], QW=[128, 2, PAIRS, S], KW=[128, 2, PAIRS, 2, S],
                VW=[S, 2, PAIRS * 3 * HW], OT=[128, 2, PAIRS // 2 * S], rsum=[S, 2, UH], rinv=[S, 2, UH],
                YN=[S, D],
                upper=[S, S], iota=[S, TOP], valid=[128, 1], blocks2=[128, NT, NB], mbatch=[128, NT, MB],
                inv4=[S, 4], pos4=[S, MB], cs_table=[S, MB, 2 * HD], amask=[S, MB, S],
                c_ln1=[D, 1], c_ln2=[D, 1],
                c_rw_row=[S, D], c_rb=[S, 1], wt=[S, B], rank=[S, B], sel=[S, B, TOP], count_ge=[S, B],
                count_eq=[S, B], factor=[S, B], xsT=[D, NT * 128], umask=[S, NT * 128], selT=[128, NT * 128],
                cs_prod=[128, NT, MB, 2 * HD], cs=[128, NT, 2 * HD], tokens=[128, NT, D], sq=[128, NT, D],
                ss=[128, NT], rms=[128, NT], ss2=[128, NT], rms2=[128, NT], wsel=[128, NT],
                mprod=[128, NT, NB, TOP], msel=[128, NT, TOP], qkv=[128, NT, 3 * D], roped=[128, NT, 2 * D],
                rot=[128, NT, 2 * D], att=[128, NT * H, KC], rmax=[128, NT * H], rsum32=[128, NT * H],
                vsum=[128, NT * D], attended=[128, NT * D], fT=[D, NT * 128], x1=[128, NT, D], x1nT=[D, NT * 128],
                slot_w=[128, NT, NB], bn16=[S, B, 6], mv16=[S, B, 2],
                ve16=[S, B], r_bf=[D, 1], r_bi=[D, 1], r_c0=[D, 1], r_bf0=[D, 1], r_bi0=[D, 1], r_bc=[D, 1],
                r_c00=[D, 1], r_bo=[S, D], c2=[D, 2, S], fg=[D, S], ig=[D, S], gg=[D, S],
                ca=[D, S], cb=[D, S], cu=[S, D], nshift=[S, B], ln16=[S, B], Y2=[S, D], XG=[S, 2, D], bn2=[S, 6], mv2=[S, 2], rstd2=[S, 1]).items():
            sb[name] = buf(name, shape)
        for name, shape, dt in (("pos_i", [D, S], I32), ("pos4_i", [S, MB], I32), ("identb", [128, 128], BF16),
                                ("causal", [S, 4, S], BF16)):
            sb[name] = buf(name, shape, dt)
        setup_small_heads(nc, ps, sb, X, dram)
        small_heads = ps, sb, X, xs
        if 1 in layers:
            small_head_attention(nc, "self0", *small_heads, None, dict(
                q=sb["a_q"], k=sb["a_k"], v=sb["a_v"], o=sb["a_o"], qb=sb["a_qbs"], kb=sb["a_kb"],
                qs=float(HD) ** -0.5, bias=sb["a_bias"]))
        if 2 in layers:
            small_head_attention(nc, "cross0", *small_heads, dram["ctxT"], dict(
                q=sb["b_q"], qr=sb["b_qr"], k=sb["b_k"], kr=sb["b_kr"], v=sb["b_v"], o=sb["b_o"],
                bias=sb["b_bias"]), rope=sb["rope"][:].rearrange("p n s -> p (n s)"), causal=sb["causal"])
        if 3 in layers:
            routed_ffn(nc, banks, sb, X)
        if 4 in layers:
            wide_head_attention(nc, ps, sb, X, xs)
        if 5 in layers:
            small_head_attention(nc, "cross1", *small_heads, dram["ctxT"], dict(
                q=sb["e_q"], k=sb["e_k"], v=sb["e_v"], o=sb["e_o"], qb=sb["e_qbs"], kb=sb["e_kb"],
                qs=float(HD) ** -0.5, bias=sb["e_bias"]), key_mask=sb["kmask"])
        if 6 in layers:
            recurrent_ffn(nc, banks, sb, X, out)
        else:
            with nc.semaphore("stored") as stored, nc.Block() as block:
                @block.sync
                def _(sp):
                    sp.dma_start(out.rearrange("b s d -> s b d"), X[:]).then_inc(stored, 16)
                    sp.wait_ge(stored, 16)


def constants():
    part = np.arange(128)
    ident = np.eye(128, dtype=np.float32)
    headmask = (part[:, None] // HD == np.arange(H)[None]).astype(np.float32)
    causal = np.where(part[None, :] > part[:, None], np.float32(NEG), np.float32(0))
    inv = 1.0 / np.float32(ROPE_BASE) ** (np.arange(0, HD, 2, dtype=np.float32) / np.float32(HD))
    blocks = (part[:, None] // TOP == np.arange(NB)[None]).astype(np.float32)
    mbatch = np.stack([(np.minimum(t * NB + part // TOP, MB - 1)[:, None] == np.arange(MB)[None]) for t in range(NT)], 1)
    repeat = (part[:, None, None] // TOP == part[None, None, :] // TOP) \
        & (part[:, None, None] % TOP == np.arange(TOP)[None, :, None])
    return {"upper": (part[None, :] >= part[:, None]).astype(np.float32),
            "iota": np.tile(np.arange(TOP, dtype=np.float32), (S, 1)),
            "valid": (part % TOP < KC).astype(np.float32)[:, None].copy(),
            "blocks2": np.concatenate([blocks, blocks], 1), "mbatch": mbatch.astype(np.float32).reshape(128, -1),
            "repeat": repeat.astype(np.float32).reshape(128, -1),
            "inv4": np.tile(inv.astype(np.float32), (S, 1)),
            "ident": ident, "headmask": headmask, "causal": causal.astype(np.float32),
            "inv_freq": np.tile(inv.astype(np.float32), 2 * H)[:, None].copy()}


def laid_out(inputs):
    arrays = {}
    for name in ("x", "pos_S2", "mask_BxS2_ik0", "L0_attn_Wq", "L0_attn_bq", "L0_attn_bl", "L0_attn_Wk", "L0_attn_bk",
                 "L0_attn_Wv", "L0_attn_bv", "L0_attn_Wo", "L0_attn_bo", "L0_xattn_wo_b", "L0_ffn_attention_mask",
                 "L0_ffn_router_w", "L0_ffn_router_b", "L0_ffn_wq", "L0_ffn_wk", "L0_ffn_wv", "L0_ffn_wo", "L0_ffn_w1",
                 "L0_ffn_ln1", "L0_ffn_ln2", "L1_attn_bo", "L1_attn_gamma", "L1_attn_beta", "L1_xattn_bq",
                 "L1_xattn_bk", "L1_xattn_bv", "L1_xattn_bp", "L1_ffn_bf", "L1_ffn_bi", "L1_ffn_bc", "L1_ffn_bo",
                 "L1_ffn_in_c"):
        arrays[name] = inputs[name]
    for name in ("L0_attn_Wl", "L0_xattn_wq", "L0_xattn_wk", "L0_xattn_wv", "L0_xattn_wo_w", "L1_xattn_Wq",
                 "L1_xattn_Wk", "L1_xattn_Wv", "L1_xattn_Wp", "L1_attn_Wq", "L1_attn_Wk", "L1_attn_Wv", "L1_ffn_wf",
                 "L1_ffn_uf", "L1_ffn_wi", "L1_ffn_ui", "L1_ffn_wc", "L1_ffn_uc", "L1_ffn_wo", "L1_ffn_uo"):
        arrays[name + "T"] = inputs[name].T
    arrays["ctxT"] = inputs["ctx_1024"].transpose(2, 0, 1).reshape(D, B * S)
    arrays["L1_attn_Wo_pairs"] = inputs["L1_attn_Wo"].T.reshape(PAIRS, 128, D).transpose(1, 0, 2).reshape(128, -1)
    for name in ("bq", "bk", "bv"):
        arrays[f"L1_attn_{name}_pairs"] = inputs["L1_attn_" + name].reshape(PAIRS, 128).T
    arrays["L1_attn_scale_pairs"] = inputs["L1_attn_adaptive_scale"].reshape(PAIRS, 2).T
    arrays["L0_ffn_w2_chunks"] = inputs["L0_ffn_w2"].reshape(FF // 128, 128, D).transpose(1, 0, 2).reshape(128, -1)
    arrays["L0_ffn_router_w_row"] = inputs["L0_ffn_router_w"].reshape(D)
    arrays["L0_ffn_position_ids_t"] = inputs["L0_ffn_position_ids"].T
    arrays.update(constants())
    return {name: np.ascontiguousarray(a) for name, a in arrays.items()}


def kernel(**inputs):
    import numpy as _np
    import concourse.bacc as _bacc
    from concourse import mybir as _mybir
    from concourse.bass_utils import run_bass_kernel_spmd as _run

    nc = _bacc.Bacc("TRN2", target_bir_lowering=False, num_devices=1)
    arrays = laid_out({name: _np.asarray(a) for name, a in inputs.items()})
    dram = {name: nc.dram_tensor(f"in_{name}_dram", a.shape, _mybir.dt.from_np(a.dtype), kind="ExternalInput").ap()
            for name, a in arrays.items()}
    out = nc.dram_tensor("out_0_dram", (B, S, D), F32, kind="ExternalOutput").ap()
    decoder(nc, dram, out)
    r = _run(nc, [{f"in_{name}_dram": a for name, a in arrays.items()}], core_ids=[0])
    return r.results[0]["out_0_dram"]
```

```python
from contextlib import ExitStack

import concourse.bass as bass
import numpy as np
from concourse import mybir

ALU = mybir.AluOpType
ACT = mybir.ActivationFunctionType
AX = mybir.AxisListType
F32 = mybir.dt.float32
BF16 = mybir.dt.bfloat16
I32 = mybir.dt.int32

B, S, D = 16, 128, 128
H = 16
HD = D // H
LAT = D // 4
FF = 512
HW = 64
PAIRS = H // 2
SLOT = 2 * HD
UH = H // 2
UC = UH * S
TOP = S // 8
KC = TOP - 1
NB = 128 // TOP
NT = B // NB
MB = 4
LEAD, LAG = 2, 2
EDGE = 3
TERMS = 6
LN_EPS = 1e-5
RMS_EPS = 1e-6
ROPE_BASE = 10000.0
TWO_PI = 2 * np.pi
NEG = -1e30


def bc(ap, axis, n):
    shape = list(ap.shape)
    shape.insert(axis, n)
    return ap.unsqueeze(axis).to_broadcast(shape)


def after(eng, sem, count):
    if isinstance(count, int) and count <= 0:
        return
    eng.wait_ge(sem, count)


def has(b, stages=1):
    return not isinstance(b, int) or 0 <= b < B * stages


def slots(eng, slot, stages=1):
    for i in range(-EDGE, EDGE):
        slot(i, i % 2, i // 2, 0)
    for stage in range(stages):
        with eng.Fori(0, (B - 2 * EDGE) // 2) as j:
            for p in range(2):
                slot(j * 2 + (B * stage + EDGE + p), (EDGE + p) % 2, j + (B * stage + EDGE + p) // 2, stage)
        for i in range(B * (stage + 1) - EDGE, B * (stage + 1) + EDGE):
            slot(i, i % 2, i // 2, stage)


def one(t, i):
    return t[:, bass.ds(i, 1), :].rearrange("p o d -> p (o d)")


FIRST = [
    ("a_q", "L0_attn_Wq_by_feature", D, D), ("a_lT", "L0_attn_WlT", LAT, D), ("a_k0", "L0_attn_Wk_by_feature", LAT, D),
    ("a_v0", "L0_attn_Wv", LAT, D), ("a_o", "L0_attn_Wo", D, D),
    ("a_qb", "L0_attn_bq_by_feature", D, 1), ("a_bl", "L0_attn_bl", LAT, 1), ("a_bk", "L0_attn_bk_by_feature", D, 1),
    ("a_bv", "L0_attn_bv", D, 1), ("e_qb", "L1_xattn_bq_by_feature", D, 1), ("e_kb", "L1_xattn_bk_by_feature", D, 1),
    ("e_bv", "L1_xattn_bv", D, 1), ("d_qb", "L1_attn_bq_pairs", 128, PAIRS), ("d_kb", "L1_attn_bk_pairs", 128, PAIRS),
    ("d_vb", "L1_attn_bv_pairs", 128, PAIRS), ("d_as", "L1_attn_scale_pairs", 128, PAIRS),
]
SECOND = [
    ("b_q", "L0_xattn_wqT_by_feature", D, D), ("b_k", "L0_xattn_wkT_by_feature", D, D), ("b_v", "L0_xattn_wvT", D, D),
    ("b_o", "L0_xattn_wo_wT", D, D),
    ("e_q", "L1_xattn_WqT_by_feature", D, D), ("e_k", "L1_xattn_WkT_by_feature", D, D), ("e_v", "L1_xattn_WvT", D, D),
    ("e_o", "L1_xattn_WpT", D, D), ("d_o", "L1_attn_Wo_pairs", 128, PAIRS * D),
]
LATE = [
    ("c_qkv", "L0_ffn_wqkv", D, 3 * D), ("c_o", "L0_ffn_wo", D, D), ("c_w1", "L0_ffn_w1", D, FF),
    ("c_w2", "L0_ffn_w2_chunks", 128, FF), ("c_rw", "L0_ffn_router_w", D, 1),
    ("c_ln1", "L0_ffn_ln1", D, 1), ("c_ln2", "L0_ffn_ln2", D, 1),
    ("r_w", "L1_ffn_w", D, 3 * D), ("r_u", "L1_ffn_u", D, 3 * D), ("r_wo", "L1_ffn_woT", D, D),
    ("r_uo", "L1_ffn_uoT", D, D), ("r_bf0", "L1_ffn_bf", D, 1), ("r_bi0", "L1_ffn_bi", D, 1),
    ("r_bc", "L1_ffn_bc", D, 1), ("r_c00", "L1_ffn_in_c", D, 1),
]
LAST = [
    ("d_q", "L1_attn_WqT", D, H * HW), ("d_k", "L1_attn_WkT", D, H * HW), ("d_v", "L1_attn_WvT", D, H * HW),
]
CONSTANTS = [
    ("ident", "ident", 128, 128), ("inv", "inv_freq", D, 1), ("inv4", "inv4", S, 4),
    ("causalf", "causal", S, S), ("upper", "upper", S, S), ("iota", "iota", S, TOP), ("valid", "valid", 128, 1),
    ("blocks2", "blocks2", 128, NT * NB), ("mbatch", "mbatch", 128, NT * MB),
]
PACKS = {"first": FIRST, "second": SECOND, "late": LATE, "last": LAST, "constants": CONSTANTS}
ROWS = [("a_bo", "L0_attn_bo", D), ("b_bias", "L0_xattn_wo_b", D), ("e_bp", "L1_xattn_bp", D),
        ("d_bo", "L1_attn_bo", D), ("gamma", "L1_attn_gamma", D), ("beta", "L1_attn_beta", D),
        ("c_rw_row", "L0_ffn_router_w_row", D), ("c_rb", "L0_ffn_router_b", 1), ("r_bo", "L1_ffn_bo", D)]


def width(entries):
    return sum(entry[-1] for entry in entries)


def fold_value_bias(nc, sems, k, sb, vb, wo, n, bias_row, out, psum_bank):
    spread, product, done = sems

    def on_vector_spread():
        for c in range(n):
            last = nc.vector.tensor_scalar(sb["spread"][:, c * D:(c + 1) * D], sb["ones"][:], vb[:, c:c + 1], None,
                                           ALU.mult)
        last.then_inc(spread, 1)

    def on_tensor():
        nc.tensor.wait_ge(spread, k)
        for c in range(n):
            last = nc.tensor.matmul(psum_bank[:, 0:D], sb["spread"][:, c * D:(c + 1) * D],
                                    wo[:, c * D:(c + 1) * D], start=(c == 0), stop=(c == n - 1))
        last.then_inc(product, 1)

    def on_vector_add():
        nc.vector.wait_ge(product, k)
        nc.vector.tensor_tensor(out[:], psum_bank[:, 0:D], bias_row[:], ALU.add).then_inc(done, 1)

    return on_vector_spread, on_tensor, on_vector_add


LATE_LOADS = 6


def setup_small_heads(nc, ps, sb, packs, X, dram, late_loaded):
    S_ps, PT_ps, O_ps, M_ps = ps
    with ExitStack() as ctx:
        def sem(what):
            return ctx.enter_context(nc.semaphore(f"setup_{what}"))

        loaded, loaded_c, filled = sem("loaded"), sem("loaded_constants"), sem("filled")
        prepared = sem("prepared")
        products_a, copied_a = sem("products_a"), sem("copied_a")
        rope_step = sem("rope_step")
        sin_done, table_ready, mask_ready = sem("sin_done"), sem("table_ready"), sem("mask_ready")
        fold = sem("fold_spread"), sem("fold_product"), sem("fold_done")
        block = ctx.enter_context(nc.Block())
        d_steps = fold_value_bias(nc, fold, 3, sb, sb["d_vb"], sb["d_o"], PAIRS, sb["d_bo"], sb["d_bias"], O_ps)
        a_steps = fold_value_bias(nc, fold, 1, sb, sb["a_vb"], sb["a_o"], 1, sb["a_bo"], sb["a_bias"], O_ps)
        e_steps = fold_value_bias(nc, fold, 2, sb, sb["e_bv"], sb["e_o"], 1, sb["e_bp"], sb["e_bias"], M_ps)
        EARLY, EARLY_CONSTANTS = 4, 3

        @block.sync
        def _(sp):
            sp.dma_start(packs["first"][:], dram["first"]).then_inc(loaded, 16)
            sp.dma_start(X[:], dram["x"].rearrange("b s d -> s b d")).then_inc(loaded, 16)
            sp.dma_start(packs["rows"][:], bc(dram["rows"], 0, S)).then_inc(loaded, 16)
            sp.dma_start(packs["second"][:], dram["second"]).then_inc(loaded, 16)
            sp.dma_start(packs["late"][:], dram["late"]).then_inc(late_loaded, 16)
            sp.dma_start(sb["QW"][:].rearrange("p u h k -> p (u h k)"), dram["repeat"]).then_inc(late_loaded, 16)
            sp.dma_start(sb["amask"][:], dram["L0_ffn_attention_mask"][:, 0, 0:S, 0:S].rearrange("m t k -> t m k"))\
                .then_inc(late_loaded, 16)
            sp.dma_start(sb["kmask"][:].rearrange("p b k -> p (b k)").bitcast(I32),
                         bc(dram["mask_BxS2_ik0"].rearrange("b k -> (b k)"), 0, D)).then_inc(late_loaded, 16)
            half = 3 * H * HW // 2
            sp.dma_start(packs["last"][:, 0:half], dram["last"][:, 0:half]).then_inc(late_loaded, 16)
            sp.dma_start(packs["last"][:, half:], dram["last"][:, half:]).then_inc(late_loaded, 16)

        @block.scalar
        def _(act):
            act.dma_start(sb["pos_i"][:], bc(dram["pos_S2"], 0, D)).then_inc(loaded_c, 16)
            act.dma_start(sb["pos4_i"][:], dram["L0_ffn_position_ids_t"][0:S, :]).then_inc(loaded_c, 16)
            act.dma_start(packs["constants"][:], dram["constants"]).then_inc(loaded_c, 16)
            for half in range(2):
                act.wait_ge(rope_step, 6 * half + 6)
                nc.scalar.activation(sb["trig"][:, half, :], sb["ang"][:, half, :], ACT.Sin).then_inc(sin_done, 1)

        @block.gpsimd
        def _(pool):
            nc.gpsimd.memset(sb["Vx"][:], 0.0).then_inc(mask_ready, 1)
            nc.gpsimd.memset(sb["KW"][:], 0.0).then_inc(mask_ready, 1)
            nc.gpsimd.memset(sb["VW"][:], 0.0).then_inc(mask_ready, 1)
            pool.wait_ge(mask_ready, 3)

        @block.tensor
        def _(pe):
            pe.wait_ge(loaded, 16 * EARLY)
            nc.tensor.matmul(M_ps[:, 0:D], sb["a_lT"][:], sb["a_k0"][:], start=True, stop=True)
            nc.tensor.matmul(M_ps[:, D:2 * D], sb["a_lT"][:], sb["a_v0"][:], start=True, stop=True)
            nc.tensor.matmul(M_ps[:, 2 * D:2 * D + 1], sb["a_k0"][:], sb["a_bl"][:], start=True, stop=True)
            nc.tensor.matmul(M_ps[:, 2 * D + 1:2 * D + 2], sb["a_v0"][:], sb["a_bl"][:], start=True, stop=True)\
                .then_inc(products_a, 1)
            a_steps[1]()
            pe.wait_ge(copied_a, 4)
            e_steps[1]()
            d_steps[1]()

        @block.vector
        def _(dve):
            nc.vector.memset(sb["ones"][:], 1.0).then_inc(filled, 1)
            nc.vector.memset(sb["mhalf"][:], -0.5).then_inc(filled, 1)
            nc.vector.memset(sb["eps"][:], LN_EPS).then_inc(filled, 1)
            dve.wait_ge(mask_ready, 1)
            for p in range(2):
                nc.vector.memset(sb["Vx"][:, p, :].rearrange("p (h c) -> p h c", h=H)[:, :, HD], 1.0)\
                    .then_inc(filled, 1)
            dve.wait_ge(filled, 5)
            dve.wait_ge(loaded_c, 16 * EARLY_CONSTANTS)
            nc.vector.tensor_copy(sb["pos"][:], sb["pos_i"][:]).then_inc(filled, 1)
            nc.vector.tensor_copy(sb["pos4"][:], sb["pos4_i"][:]).then_inc(filled, 1)
            dve.wait_ge(filled, 7)
            turns, angle, rounding = sb["turns"], sb["angle"], 1.5 * 2.0 ** 23
            c1 = float(np.float32(6.28125))
            c2 = float(np.float32(np.floor((TWO_PI - c1) * 2 ** 22) / 2 ** 22))
            c3 = float(TWO_PI - c1 - c2)
            nc.vector.tensor_scalar(angle[:, 0:S], sb["pos"][:], sb["inv"][:], None, ALU.mult).then_inc(table_ready, 1)
            nc.vector.tensor_tensor(angle[:, S:S + 4 * MB].rearrange("p (m c) -> p m c", m=MB), bc(sb["pos4"][:], 2, 4),
                                    bc(sb["inv4"][:], 1, MB), ALU.mult).then_inc(table_ready, 1)
            dve.wait_ge(table_ready, 2)
            step = [0]

            def link(instruction):
                step[0] += 1
                instruction.then_inc(rope_step, 1)
                dve.wait_ge(rope_step, step[0])

            for half, (quarter, shift_) in enumerate(((0.25, np.pi / 2), (0.0, 0.0))):
                a = sb["ang"][:, half, :]
                link(nc.vector.tensor_scalar(turns[:], angle[:], float(1 / TWO_PI), quarter, ALU.mult, ALU.add))
                link(nc.vector.tensor_scalar(turns[:], turns[:], rounding, rounding, ALU.add, ALU.subtract))
                link(nc.vector.scalar_tensor_tensor(out=a, in0=turns[:], scalar=-c1, in1=angle[:],
                                                    op0=ALU.mult, op1=ALU.add))
                link(nc.vector.scalar_tensor_tensor(out=a, in0=turns[:], scalar=-c2, in1=a,
                                                    op0=ALU.mult, op1=ALU.add))
                link(nc.vector.scalar_tensor_tensor(out=a, in0=turns[:], scalar=-c3, in1=a,
                                                    op0=ALU.mult, op1=ALU.add))
                if half == 0:
                    link(nc.vector.tensor_scalar(a, a, float(shift_), 3.1415925, ALU.add, ALU.min))
                else:
                    link(nc.vector.tensor_scalar(a, a, -3.1415925, 3.1415925, ALU.max, ALU.min))
            dve.wait_ge(sin_done, 2)
            nc.vector.tensor_scalar(sb["rope"][:, 0:2, :], sb["trig"][:, :, 0:S], float(HD) ** -0.5, None, ALU.mult)\
                .then_inc(table_ready, 1)
            nc.vector.tensor_copy(sb["rope"][:, 2:4, :], sb["trig"][:, :, 0:S]).then_inc(table_ready, 1)
            for at, which, sign in ((0, 0, 1.0), (4, 0, 1.0), (8, 1, -1.0), (12, 1, 1.0)):
                nc.vector.tensor_scalar(sb["cs_table"][:, :, at:at + 4],
                                        sb["trig"][:, which, S:].rearrange("p (m c) -> p m c", m=MB), sign, None,
                                        ALU.mult).then_inc(table_ready, 1)
            nc.vector.tensor_copy(sb["identb"][:], sb["ident"][:]).then_inc(prepared, 1)
            nc.vector.tensor_copy(sb["causal"][:], bc(sb["causalf"][:], 1, 4)).then_inc(prepared, 1)
            dve.wait_ge(prepared, 2)
            dve.wait_ge(loaded, 16 * EARLY)
            for src, dst in (("b_q", "b_qr"), ("b_k", "b_kr")):
                nc.vector.tensor_scalar(sb[dst][:, 0:D // 2], sb[src][:, D // 2:D], -1.0, None, ALU.mult)\
                    .then_inc(prepared, 1)
                nc.vector.tensor_copy(sb[dst][:, D // 2:D], sb[src][:, 0:D // 2]).then_inc(prepared, 1)
            dve.wait_ge(prepared, 6)
            dve.wait_ge(products_a, 1)
            nc.vector.tensor_copy(sb["a_k"][:], M_ps[:, 0:D]).then_inc(copied_a, 1)
            nc.vector.tensor_copy(sb["a_v"][:], M_ps[:, D:2 * D]).then_inc(copied_a, 1)
            nc.vector.tensor_tensor(sb["a_kb"][:], M_ps[:, 2 * D:2 * D + 1], sb["a_bk"][:], ALU.add)\
                .then_inc(copied_a, 1)
            nc.vector.tensor_tensor(sb["a_vb"][:], M_ps[:, 2 * D + 1:2 * D + 2], sb["a_bv"][:], ALU.add)\
                .then_inc(copied_a, 1)
            dve.wait_ge(copied_a, 4)
            a_steps[0]()
            a_steps[2]()
            dve.wait_ge(fold[2], 1)
            e_steps[0]()
            e_steps[2]()
            dve.wait_ge(fold[2], 2)
            d_steps[0]()
            d_steps[2]()
            dve.wait_ge(fold[2], 3)
            nc.vector.tensor_scalar(sb["d_qs"][:], sb["d_as"][:], float(HW) ** -0.5, None, ALU.mult)\
                .then_inc(prepared, 1)
            dve.wait_ge(prepared, 7)
            nc.vector.tensor_tensor(sb["d_qbs"][:], sb["d_qb"][:], sb["d_qs"][:], ALU.mult).then_inc(prepared, 1)
            dve.wait_ge(prepared, 8)
            for name in ("a_qb", "e_qb"):
                nc.vector.tensor_scalar(sb[name + "s"][:], sb[name][:], float(HD) ** -0.5, None, ALU.mult)\
                    .then_inc(prepared, 1)
            dve.wait_ge(prepared, 10)
            dve.wait_ge(table_ready, 8)


TERM_PARTS = ((0, 0), (0, 1), (1, 0), (1, 1), (0, 2), (2, 0))
TERMS_OF_PART = ((0,), (1, 2, 3), (4, 5))


def small_head_attention(nc, name, ps, sb, X, xs, stages, own_outputs=None):
    S_ps, PT_ps, O_ps, M_ps = ps
    N = len(stages)
    steps = own_outputs is not None
    unit_bank = (0, 0) if steps else (0, 2)
    f_bank, ig_bank = S_ps[:, 2, :], S_ps[:, 3, :]

    def at(b, stage):
        s = b // B if isinstance(b, int) else stage
        return stages[s], b - B * s, s

    def loads(s):
        return 2 if "context" in stages[s] else 1

    def parts(p, which):
        return sb["parts"][:, p, which:which + 4:3, :]

    def source(w):
        return sb["cT"] if "context" in w else sb["xT"]

    with ExitStack() as ctx:
        def sem(what):
            return ctx.enter_context(nc.semaphore(f"{name}_{what}"))

        x_loaded = [sem("x_loaded0"), sem("x_loaded1")]
        xt_done, xt_ready = sem("xt_done"), sem("xt_ready")
        qk_done, q_ready, k_ready = sem("qk_done"), sem("q_ready"), sem("k_ready")
        rope_prod = sem("rope_prod")
        high_ready, rest_ready, middle_ready, split_ready = (
            sem("high_ready"), sem("rest_ready"), sem("middle_ready"), sem("split_ready"))
        stacked = [sem("stacked0"), sem("stacked1")]
        s_done, max_ready, sub_ready, exp_ready = sem("s_done"), sem("max_ready"), sem("sub_ready"), sem("exp_ready")
        pt_done, pt_ready, pv_done = sem("pt_done"), sem("pt_ready"), sem("pv_done")
        o_ready, ot_done, v_ready = sem("o_ready"), sem("ot_done"), sem("v_ready")
        rden_ready, on_ready = sem("rden_ready"), sem("on_ready")
        ont_done, ont_ready, out_done = sem("ont_done"), sem("ont_ready"), sem("out_done")
        xb_ready, y_ready, var_ready, rstd_ready, x_new = (
            sem("xb_ready"), sem("y_ready"), sem("var_ready"), sem("rstd_ready"), sem("x_new"))
        ve_ready = sem("ve_ready")
        if steps:
            xr_done, xr_ready, gates_done, gates_ready, terms, c_ready, x_kept = (
                sem(n) for n in ("xr_done", "xr_ready", "gates_done", "gates_ready", "terms", "c_ready", "x_kept"))
        block = ctx.enter_context(nc.Block())

        @block.sync
        def _(sp):
            def slot(i, p, half, stage):
                b, m = i + LEAD, i + LEAD + 1
                if has(m, N):
                    w, own, s = at(m, stage)
                    after(sp, xt_done, m - 1)
                    if s > 0:
                        sp.wait_ge(x_new, m - B + 1 if isinstance(m, int) else B * s)
                    sp.dma_start(xs[:, 1 - p, :], one(X, own)).then_inc(x_loaded[1 - p], 16)
                if has(m, N) and "context" in at(m, stage)[0]:
                    after(sp, ot_done, i + 2)
                    sp.dma_start(sb["cT"][:, 1 - p, :], one(at(m, stage)[0]["context"], at(m, stage)[1]))\
                        .then_inc(x_loaded[1 - p], 16)
                if has(b, N):
                    for part_ready, terms_of in ((high_ready, TERMS_OF_PART[0]), (middle_ready, TERMS_OF_PART[1]),
                                                 (split_ready, TERMS_OF_PART[2])):
                        sp.wait_ge(part_ready, b + 1)
                        for t in terms_of:
                            q_part, k_part = TERM_PARTS[t]
                            sp.dma_start(sb["stacked"][t * HD:(t + 1) * HD, p, :, :, :],
                                         sb["parts"][:, p, q_part:3 + k_part + 1:3 + k_part - q_part, :])\
                                .then_inc(stacked[p], 16)
            slots(sp, slot, N)

        @block.tensor
        def _(pe):
            def scores(b, u, p, pairs, causal):
                pe.wait_ge(stacked[p], pairs * (16 * TERMS))
                after(pe, sub_ready, 2 * b + u - (0 if steps else 1))
                for g in range(2):
                    bank = S_ps[:, unit_bank[u] + g, :]
                    if causal is not None:
                        nc.tensor.matmul(bank, sb["identb"][:], causal[:].rearrange("p h k -> p (h k)"),
                                         start=True, stop=False, skip_group_check=True)
                    for e in range(4):
                        head = sb["stacked"][0:TERMS * HD, p, UH * u + 4 * g + e, :, :]
                        last = nc.tensor.matmul(bank[:, e * S:(e + 1) * S], head[:, 0, :], head[:, 1, :],
                                                start=causal is None, stop=True,
                                                skip_group_check=causal is not None)
                last.then_inc(s_done, 1)

            def transpose_probs(b, u):
                pe.wait_ge(exp_ready, 2 * b + u + 1)
                after(pe, pt_ready, 2 * b + u)
                for h in range(UH):
                    last = nc.tensor.transpose(PT_ps[:, h // 4, (h % 4) * S:(h % 4 + 1) * S],
                                               sb["P"][:, u, h, :], sb["ident"][:])
                last.then_inc(pt_done, 1)

            def values(b, u, p):
                pe.wait_ge(pt_ready, 2 * b + u + 1)
                if u == 0:
                    pe.wait_ge(v_ready, b + 1)
                    after(pe, o_ready, b)
                for h in range(UH):
                    at = u * UH * (SLOT * (UH + 1)) + h * SLOT * UH
                    last = nc.tensor.matmul(O_ps[:, u * S:(u + 1) * S], sb["Vx"][:, p, at:at + S],
                                            sb["PT"][:, u, h, :], start=(h == 0), stop=(h == UH - 1))
                last.then_inc(pv_done, 1)

            def slot(i, p, half, stage):
                q = 1 - p
                b, n, r, z = i + LEAD, i + 1, i - 1, i - LAG

                def gates():
                    pe.wait_ge(xr_ready, z + 1)
                    pe.wait_ge(c_ready, z + 1)
                    for k, gate in enumerate((f_bank[:, 0:S], ig_bank[:, 0:S], ig_bank[:, S:2 * S])):
                        nc.tensor.matmul(gate, sb["r_w"][:, k * D:(k + 1) * D], sb["xr"][:], start=True, stop=False)
                        nc.tensor.matmul(gate, sb["r_u"][:, k * D:(k + 1) * D], sb["c2"][:], start=False, stop=True)
                    nc.tensor.matmul(ig_bank[:, 2 * S:3 * S], sb["xr"][:], sb["r_wo"][:], start=True, stop=True)\
                        .then_inc(gates_done, 1)

                if has(i, N):
                    scores(i, 1, p, half + 1, at(i, stage)[0].get("causal"))
                if has(b, N):
                    w, _, s = at(b, stage)
                    before = sum(B // 2 * loads(t) for t in range(s))
                    pe.wait_ge(x_loaded[p], (half + (2 - s * B // 2)) * (16 * loads(s)) + 16 * before)
                    after(pe, y_ready, i - 1)
                    after(pe, v_ready, i + 1)
                    nc.tensor.transpose(M_ps[:, 0:S], xs[:, p, :], sb["ident"][:]).then_inc(xt_done, 1)
                if has(r, N):
                    values(r, 1, q)
                if has(b, N):
                    pe.wait_ge(xt_ready, b + 1)
                    for m, which in enumerate(("q", "qr", "k", "kr") if "rope" in w else ("q", "k")):
                        src = sb["xT"] if which[0] == "q" else source(w)
                        last = nc.tensor.matmul(M_ps[:, m * S:(m + 1) * S], w[which][:], src[:, p, :],
                                                start=True, stop=True)
                    last.then_inc(qk_done, 1)
                if has(i, N):
                    transpose_probs(i, 0)
                if has(n, N):
                    scores(n, 0, q, half + 1 + p, at(n, stage)[0].get("causal"))
                if not has(b, N):
                    if has(r, N) or has(n, N):
                        after(pe, y_ready, i - 1)
                elif "rope" in at(b, stage)[0]:
                    pe.wait_ge(rope_prod, at(b, stage)[1] + 1)
                else:
                    pe.wait_ge(q_ready, b + 1)
                    pe.wait_ge(k_ready, b + 1)
                if has(r, N) or has(n, N):
                    if has(r, N):
                        pe.wait_ge(o_ready, r + 1)
                        for t in range(2):
                            last = nc.tensor.transpose(M_ps[:, t * S:(t + 1) * S], sb["O"][:, t * S:(t + 1) * S],
                                                       sb["ident"][:])
                    if has(n, N):
                        last = nc.tensor.matmul(M_ps[:, 2 * S:3 * S], source(at(n, stage)[0])[:, q, :],
                                                at(n, stage)[0]["v"][:],
                                                start=True, stop=True)
                    last.then_inc(ot_done, 1)
                if steps and has(z):
                    pe.wait_ge(x_new, z + 1)
                    after(pe, gates_ready, z)
                    nc.tensor.transpose(f_bank[:, S:2 * S], sb["YN"][:], sb["ident"][:]).then_inc(xr_done, 1)
                if has(i, N):
                    values(i, 0, p)
                if steps and has(z):
                    gates()
                if has(r, N):
                    pe.wait_ge(on_ready, r + 1)
                    if has(n, N):
                        pe.wait_ge(v_ready, n + 1)
                    nc.tensor.transpose(M_ps[:, 0:S], sb["ON"][:], sb["ident"][:]).then_inc(ont_done, 1)
                if has(i, N):
                    transpose_probs(i, 1)
                if has(r, N):
                    pe.wait_ge(ont_ready, r + 1)
                    nc.tensor.matmul(M_ps[:, S:2 * S], sb["ONT"][:], at(r, stage)[0]["o"][:], start=True, stop=True)\
                        .then_inc(out_done, 1)
            slots(pe, slot, N)

        @block.scalar
        def _(act):
            def exps(b, u):
                act.wait_ge(sub_ready, 2 * b + u + 1)
                nc.scalar.activation(sb["P"][:, u, :, :], sb["P"][:, u, :, :], ACT.Exp).then_inc(exp_ready, 1)

            def probs_out(b, u):
                act.wait_ge(pt_done, 2 * b + u + 1)
                after(act, pv_done, 2 * b + u - 1)
                nc.scalar.activation(sb["PT"][:, u, :, :].rearrange("p h q -> p (h q)"),
                                     PT_ps[:].rearrange("p a c -> p (a c)"), ACT.Copy).then_inc(pt_ready, 1)

            def slot(i, p, half, stage):
                b, n, r, z = i + LEAD, i + 1, i - 1, i - LAG
                if has(i, N):
                    exps(i, 0)
                if has(b, N):
                    act.wait_ge(xt_done, b + 1)
                    after(act, ot_done, b - 1)
                    nc.scalar.activation(sb["xT"][:, p, :], M_ps[:, 0:S], ACT.Copy).then_inc(xt_ready, 1)
                if has(b, N) and "rope" not in at(b, stage)[0]:
                    w = at(b, stage)[0]
                    act.wait_ge(qk_done, b + 1)
                    after(act, rest_ready, b)
                    after(act, high_ready, b)
                    if "key_mask" not in w:
                        nc.scalar.activation(sb["QK"][:, 1, :], M_ps[:, S:2 * S], ACT.Identity, bias=w["kb"][:])\
                            .then_inc(k_ready, 1)
                    nc.scalar.activation(sb["QK"][:, 0, :], M_ps[:, 0:S], ACT.Identity, bias=w["qb"][:],
                                         scale=w["qs"]).then_inc(q_ready, 1)
                if has(i, N):
                    probs_out(i, 0)
                if has(b, N):
                    if "rope" not in at(b, stage)[0]:
                        act.wait_ge(k_ready, b + 1)
                    act.wait_ge(q_ready, b + 1)
                    after(act, s_done, 2 * i + 2)
                    nc.scalar.activation(parts(p, 0), sb["QK"][:], ACT.Copy).then_inc(high_ready, 1)
                if has(i, N):
                    exps(i, 1)
                if steps and has(z):
                    act.wait_ge(xr_done, z + 1)
                    after(act, gates_done, z)
                    nc.scalar.activation(sb["xr"][:], f_bank[:, S:2 * S], ACT.Copy).then_inc(xr_ready, 1)
                if has(n, N):
                    act.wait_ge(ot_done, n + 1)
                    after(act, pv_done, 2 * i)
                    after(act, on_ready, r + 1)
                    nc.scalar.activation(sb["Vx"][:, 1 - p, :].rearrange("p (h c) -> p h c", h=H)[:, :, 0:HD],
                                         M_ps[:, 2 * S:3 * S].rearrange("p (h c) -> p h c", h=H), ACT.Copy)\
                        .then_inc(v_ready, 1)
                if has(b, N):
                    act.wait_ge(rest_ready, b + 1)
                    nc.scalar.activation(parts(p, 1), sb["rest"][:], ACT.Copy)\
                        .then_inc(middle_ready, 1)
                if has(r, N):
                    act.wait_ge(ont_done, r + 1)
                    after(act, out_done, r)
                    nc.scalar.activation(sb["ONT"][:], M_ps[:, 0:S], ACT.Copy).then_inc(ont_ready, 1)
                if steps and has(z):
                    act.wait_ge(gates_done, z + 1)
                    act.wait_ge(c_ready, z + 1)
                    for gate, bank, bias, scale in (
                            ("fg", f_bank[:, 0:S], "r_bf", 0.5), ("ig", ig_bank[:, 0:S], "r_bi", 0.5),
                            ("gg", ig_bank[:, S:2 * S], "r_bc", 1.0)):
                        nc.scalar.activation(sb[gate][:], bank, ACT.Tanh, bias=sb[bias][:], scale=scale)
                    nc.scalar.activation(one(own_outputs, z), ig_bank[:, 2 * S:3 * S], ACT.Copy)\
                        .then_inc(gates_ready, 1)
                if has(i, N):
                    probs_out(i, 1)
            slots(act, slot, N)

        @block.vector
        def _(dve):
            def shift(b, u):
                unit = S_ps[:, unit_bank[u]:unit_bank[u] + 2, :].rearrange("p a (h k) -> p (a h) k", k=S)
                dve.wait_ge(s_done, 2 * b + u + 1)
                after(dve, sub_ready, 2 * b + u)
                nc.vector.tensor_reduce(sb["mx"][:, 0:UH], unit, op=ALU.max, axis=AX.X).then_inc(max_ready, 1)
                dve.wait_ge(max_ready, 2 * b + u + 1)
                after(dve, pt_done, 2 * b + u - 1)
                nc.vector.tensor_tensor(sb["P"][:, u, :, :], unit, bc(sb["mx"][:, 0:UH], 2, S), ALU.subtract)\
                    .then_inc(sub_ready, 1)

            def slot(i, p, half, stage):
                b, n, r, z = i + LEAD, i + 1, i - 1, i - LAG
                if has(z, N):
                    dve.wait_ge(out_done, z + 1)
                    dve.wait_ge(xb_ready, z + 1)
                    after(dve, x_new, z)
                    nc.vector.tensor_tensor(sb["Y"][:], M_ps[:, S:2 * S], sb["XB"][:, p, :], ALU.add)\
                        .then_inc(y_ready, 1)
                if has(i, N):
                    shift(i, 1)
                if has(r, N):
                    dve.wait_ge(pv_done, 2 * r + 2)
                    after(dve, ot_done, i + 1)
                    nc.vector.tensor_copy(sb["O"][:], O_ps[:, 0:2 * S]).then_inc(o_ready, 1)
                if has(z, N):
                    dve.wait_ge(y_ready, z + 1)
                    nc.vector.bn_stats(sb["bn"][:], sb["Y"][:])
                    nc.vector.drain()
                    nc.vector.bn_aggr(sb["mv"][:], sb["bn"][:]).then_inc(var_ready, 1)
                if has(b, N):
                    w, own, _ = at(b, stage)
                    if "rope" in w:
                        dve.wait_ge(qk_done, b + 1)
                        after(dve, q_ready, b)
                        nc.vector.tensor_tensor(sb["RP"][:], M_ps[:, 0:4 * S], w["rope"], ALU.mult)\
                            .then_inc(rope_prod, 1)
                    elif "key_mask" in w:
                        after(dve, rest_ready, b)
                        dve.wait_ge(q_ready, b + 1)
                        nc.vector.scalar_tensor_tensor(out=sb["QK"][:, 1, :], in0=M_ps[:, S:2 * S], scalar=w["kb"][:],
                                                       in1=one(w["key_mask"], own), op0=ALU.add, op1=ALU.mult)\
                            .then_inc(k_ready, 1)
                if has(z, N):
                    dve.wait_ge(rstd_ready, z + 1)
                    if steps:
                        after(dve, xr_done, z)
                        after(dve, x_kept, z)
                    nc.vector.tensor_scalar(sb["YN"][:] if steps else one(X, at(z, stage)[1]), sb["Y"][:],
                                            sb["mv"][:, 0:1], sb["rstd"][:], ALU.subtract, ALU.mult)\
                        .then_inc(x_new, 1)
                if has(r, N):
                    heads = M_ps[:, 0:2 * S].rearrange("p (h c) -> p h c", h=H)
                    dve.wait_ge(ot_done, i + 2)
                    nc.vector.reciprocal(sb["rden"][:], heads[:, :, HD]).then_inc(rden_ready, 1)
                    dve.wait_ge(rden_ready, r + 1)
                    after(dve, ont_done, r)
                    nc.vector.tensor_tensor(sb["ON"][:].rearrange("p (h c) -> p h c", h=H), heads[:, :, 0:HD],
                                            bc(sb["rden"][:], 2, HD), ALU.mult).then_inc(on_ready, 1)
                if has(n, N):
                    shift(n, 0)
                if steps and has(z):
                    dve.wait_ge(gates_ready, z + 1)
                    nc.vector.scalar_tensor_tensor(out=sb["ca"][:], in0=sb["fg"][:], scalar=1.0, in1=sb["c2"][:],
                                                   op0=ALU.add, op1=ALU.mult).then_inc(terms, 1)
                    nc.vector.scalar_tensor_tensor(out=sb["cb"][:], in0=sb["ig"][:], scalar=1.0, in1=sb["gg"][:],
                                                   op0=ALU.add, op1=ALU.mult).then_inc(terms, 1)
                    dve.wait_ge(terms, z * 2 + 2)
                    nc.vector.scalar_tensor_tensor(out=sb["c2"][:], in0=sb["ca"][:], scalar=0.5, in1=sb["cb"][:],
                                                   op0=ALU.mult, op1=ALU.add).then_inc(c_ready, 1)
            if steps:
                nc.vector.tensor_copy(sb["c2"][:], sb["r_c0"][:].to_broadcast([D, S])).then_inc(c_ready, 1)
            slots(dve, slot, N)
            if steps:
                dve.wait_ge(c_ready, B + 1)

        @block.gpsimd
        def _(pool):
            def slot(i, p, half, stage):
                b, r, z = i + LEAD, i - 1, i - LAG
                if has(z, N):
                    pool.wait_ge(var_ready, z + 1)
                    nc.gpsimd.tensor_tensor(sb["ve"][:], sb["mv"][:, 1:2], sb["eps"][:], ALU.add)\
                        .then_inc(ve_ready, 1)
                    pool.wait_ge(ve_ready, z + 1)
                    nc.gpsimd.tensor_tensor(sb["rstd"][:], sb["ve"][:], sb["mhalf"][:], ALU.pow)\
                        .then_inc(rstd_ready, 1)
                if has(r, N):
                    w, own, s = at(r, stage)
                    after(pool, y_ready, r - 1)
                    if s > 0:
                        pool.wait_ge(x_new, r - B + 1 if isinstance(r, int) else B * s)
                    nc.gpsimd.tensor_tensor(sb["XB"][:, 1 - p, :], one(X, own), w["bias"][:], ALU.add)\
                        .then_inc(xb_ready, 1)
                if has(b, N):
                    if "rope" in at(b, stage)[0]:
                        pool.wait_ge(rope_prod, at(b, stage)[1] + 1)
                        after(pool, high_ready, b)
                        products = sb["RP"][:].rearrange("p (n e s) -> p n e s", n=2, e=2)
                        nc.gpsimd.tensor_tensor(sb["QK"][:], products[:, :, 0, :], products[:, :, 1, :], ALU.add)\
                            .then_inc(q_ready, 1)
                    pool.wait_ge(high_ready, b + 1)
                    after(pool, split_ready, b)
                    after(pool, middle_ready, b)
                    nc.gpsimd.tensor_tensor(sb["rest"][:], sb["QK"][:], parts(p, 0), ALU.subtract)\
                        .then_inc(rest_ready, 1)
                    pool.wait_ge(middle_ready, b + 1)
                    if steps and has(z):
                        pool.wait_ge(x_new, z + 1)
                    nc.gpsimd.tensor_tensor(parts(p, 2), sb["rest"][:], parts(p, 1),
                                            ALU.subtract).then_inc(split_ready, 1)
                if steps and has(z):
                    if not has(b, N):
                        pool.wait_ge(x_new, z + 1)
                    nc.gpsimd.tensor_tensor(one(X, z), sb["YN"][:], sb["ones"][:], ALU.mult).then_inc(x_kept, 1)
            slots(pool, slot, N)
            if steps:
                pool.wait_ge(x_kept, B)


GELU_C = float(np.sqrt(2 / np.pi))


def counted(nc, ctx, prefix, **engines):
    sems, counts = {}, {}
    for engine, names in engines.items():
        sem = ctx.enter_context(nc.semaphore(f"{prefix}_{engine}_events"))
        for n, name in enumerate(names.split()):
            sems[name], counts[name] = sem, n + 1
    return sems, counts


def routed_ffn(nc, ps_all, sb, X, late_loaded):
    SB, SLOTS = 2048, NT * 128
    with ExitStack() as ctx:
        ev, nth = counted(
            nc, ctx, "ffn",
            tensor="spread_t gathered masks_u tables selected_t tokens qkv dense_mask k0 k1 v0 v1 attended_t "
                   "projected x1n_t hidden ff scattered",
            scalar="qkv_scaled weights_scaled xsT u_ready selT_ready exps attended_sb x1n_sb hidden_sb tanhs",
            pool="key_mask eq_masked rstd scaled_x rstd2 rstd3",
            vector="weighed summed weights spread eq ge count_ge count_eq rank factor select cs_prod cs_ready "
                   "tokens_ready squares square_sum mean_square wsel mask_prod mask_ready qkv_ready rot_sin rot_cos "
                   "roped k0_prod k0_sum k1_prod k1_sum masked row_max shifted row_sum row_inv v0_prod v1_prod "
                   "v_sum attended x1 squares2 square_sum2 mean_square2 x1n cubed inner gated slot_w x2 spread_x2 "
                   "y aggregated var_eps centred x_new")

        block = ctx.enter_context(nc.Block())
        banks = [ps_all[:, n, :] for n in range(8)]
        scores4, upper4 = ps_all[:, 0:4, :], ps_all[:, 4:8, :]
        P, PT = (sb[n][:].rearrange("p u h k -> p (u h k)") for n in ("P", "PT"))
        big = sb["big"][:]
        wide = sb["QW"][:].rearrange("p u h k -> p (u h k)")
        hid, gate = wide[:, 0:NT * FF], wide[:, NT * FF:2 * NT * FF]
        repeat = wide.rearrange("p (j c) -> p j c", j=TOP)
        P3, PT3 = (t.rearrange("p (b d) -> p b d", b=B) for t in (P, PT))
        wt, sel, rank = sb["wt"], sb["sel"], sb["rank"]
        sel_flat = sel[:].rearrange("p b r -> p (b r)")
        qkv = sb["qkv"]
        qk = qkv[:, :, 0:2 * D].rearrange("p t (h c) -> p t h c", c=HD)
        roped = sb["roped"][:].rearrange("p t (h c) -> p t h c", c=HD)
        rot = sb["rot"][:].rearrange("p t (h c) -> p t h c", c=HD)
        keys = big.rearrange("p (j c) -> p j c", c=SLOTS)
        att = sb["att"]
        X3 = X[:]

        @block.tensor
        def _(pe):
            pe.wait_ge(ev["spread"], nth["spread"])
            for b in range(B):
                last = nc.tensor.transpose(banks[b // 4][:, (b % 4) * S:(b % 4 + 1) * S],
                                           big[:, b * S:(b + 1) * S], sb["ident"][:])
            last.then_inc(ev["spread_t"], 1)
            pe.wait_ge(ev["select"], nth["select"])
            for b in range(B):
                last = nc.tensor.matmul(banks[6][:, b * TOP:(b + 1) * TOP], X3[:, b, :], sel[:, b, :],
                                        start=True, stop=True)
            last.then_inc(ev["gathered"], 1)
            pe.wait_ge(late_loaded, 16 * LATE_LOADS)
            pe.wait_ge(ev["weights_scaled"], nth["weights_scaled"])
            for m in range(MB):
                end = B if m == MB - 1 else m + 1
                last = nc.tensor.matmul(banks[4][:, m * TOP:end * TOP], sb["amask"][:, m, :],
                                        sel_flat[:, m * TOP:end * TOP], start=True, stop=True)
            last.then_inc(ev["masks_u"], 1)
            for t in range(NT):
                last = nc.tensor.matmul(banks[5][:, t * 64:(t + 1) * 64], sel_flat[:, t * 128:(t + 1) * 128],
                                        sb["cs_table"][:].rearrange("p m c -> p (m c)"), start=True, stop=True)
            last.then_inc(ev["tables"], 1)
            pe.wait_ge(ev["eq"], nth["eq"])
            for t in range(NT):
                last = nc.tensor.transpose(banks[0][:, t * 128:(t + 1) * 128], sel_flat[:, t * 128:(t + 1) * 128],
                                           sb["ident"][:])
            last.then_inc(ev["selected_t"], 1)
            pe.wait_ge(ev["xsT"], nth["xsT"])
            for t in range(NT):
                last = nc.tensor.transpose(banks[7][:, t * 128:(t + 1) * 128], sb["xsT"][:, t * 128:(t + 1) * 128],
                                           sb["ident"][:])
            last.then_inc(ev["tokens"], 1)
            for t in range(NT):
                tile = sb["xsT"][:, t * 128:(t + 1) * 128]
                nc.tensor.matmul(banks[1 + t][:, 0:3 * D], tile, sb["c_qkv"][:], start=True, stop=True)
                last = nc.tensor.matmul(banks[3][:, t:t + 1], tile, sb["c_rw"][:], start=True, stop=True)
            last.then_inc(ev["qkv"], 1)
            pe.wait_ge(ev["u_ready"], nth["u_ready"])
            pe.wait_ge(ev["xsT"], nth["xsT"])
            for t in range(NT):
                last = nc.tensor.matmul(banks[6][:, t * 128:(t + 1) * 128], sb["umask"][:, t * 128:(t + 1) * 128],
                                        sel_flat[:, t * 128:(t + 1) * 128], start=True, stop=True)
            last.then_inc(ev["dense_mask"], 1)
            pe.wait_ge(ev["roped"], nth["roped"])
            pe.wait_ge(ev["selT_ready"], nth["selT_ready"])
            pe.wait_ge(ev["tokens_ready"], nth["tokens_ready"])
            pe.wait_ge(ev["mask_prod"], nth["mask_prod"])
            pe.wait_ge(ev["wsel"], nth["wsel"])
            pe.wait_ge(ev["cs_prod"], nth["cs_prod"])
            for what, source, done in (("k", sb["roped"][:, :, D:2 * D], ("k0", "k1")),
                                       ("v", qkv[:, :, 2 * D:3 * D], ("v0", "v1"))):
                for part in range(2):
                    if what == "v":
                        pe.wait_ge(ev[f"k{part}_prod"], nth[f"k{part}_prod"])
                    for j in range(8 * part, min(8 * part + 8, KC)):
                        at = j % 8
                        last = nc.tensor.matmul(banks[4 * part + at // 2][:, (at % 2) * SLOTS:(at % 2 + 1) * SLOTS]
                                                .rearrange("p (t c) -> p t c", t=NT),
                                                repeat[:, j, :], source, start=True, stop=True)
                    last.then_inc(ev[done[part]], 1)
            pe.wait_ge(ev["attended"], nth["attended"])
            for t in range(NT):
                last = nc.tensor.transpose(banks[0][:, t * 128:(t + 1) * 128], sb["attended"][:, t * D:(t + 1) * D],
                                           sb["ident"][:])
            last.then_inc(ev["attended_t"], 1)
            pe.wait_ge(ev["attended_sb"], nth["attended_sb"])
            for t in range(NT):
                last = nc.tensor.matmul(banks[1][:, t * D:(t + 1) * D], sb["fT"][:, t * 128:(t + 1) * 128],
                                        sb["c_o"][:], start=True, stop=True)
            last.then_inc(ev["projected"], 1)
            pe.wait_ge(ev["x1n"], nth["x1n"])
            for t in range(NT):
                last = nc.tensor.transpose(banks[0][:, t * 128:(t + 1) * 128], sb["attended"][:, t * D:(t + 1) * D],
                                           sb["ident"][:])
            last.then_inc(ev["x1n_t"], 1)
            pe.wait_ge(ev["x1n_sb"], nth["x1n_sb"])
            for c in range(FF // 128):
                last = nc.tensor.matmul(banks[2 + c // 2][:, (c % 2) * SLOTS:(c % 2 + 1) * SLOTS],
                                        sb["c_w1"][:, c * 128:(c + 1) * 128], sb["x1nT"][:], start=True, stop=True)
            last.then_inc(ev["hidden"], 1)
            pe.wait_ge(ev["gated"], nth["gated"])
            for t in range(NT):
                for c in range(FF // 128):
                    last = nc.tensor.matmul(banks[1][:, t * D:(t + 1) * D],
                                            gate[:, c * SLOTS + t * 128:c * SLOTS + (t + 1) * 128],
                                            sb["c_w2"][:, c * D:(c + 1) * D], start=(c == 0), stop=(c == FF // 128 - 1))
            last.then_inc(ev["ff"], 1)
            pe.wait_ge(ev["spread_x2"], nth["spread_x2"])
            for t in range(NT):
                for g in range(2):
                    last = nc.tensor.matmul(banks[4 + 2 * t + g], sb["selT"][:, t * 128:(t + 1) * 128],
                                            big[:, (2 * t + g) * 512:(2 * t + g + 1) * 512], start=True, stop=True)
            last.then_inc(ev["scattered"], 1)

        @block.scalar
        def _(act):
            def out_of(event, bank, dst, ready):
                act.wait_ge(ev[event], nth[event])
                nc.scalar.activation(dst, bank, ACT.Copy).then_inc(ev[ready], 1)

            act.wait_ge(late_loaded, 16 * LATE_LOADS)
            nc.scalar.activation(sb["c_qkv"][:, 0:D], sb["c_qkv"][:, 0:D], ACT.Copy, scale=float(HD) ** -0.5)\
                .then_inc(ev["qkv_scaled"], 1)
            act.wait_ge(ev["qkv_scaled"], nth["qkv_scaled"])
            nc.scalar.activation(sb["c_qkv"][:], sb["c_qkv"][:], ACT.Identity, scale=sb["c_ln1"][:])
            nc.scalar.activation(sb["c_w1"][:], sb["c_w1"][:], ACT.Identity, scale=sb["c_ln2"][:])
            nc.scalar.activation(sb["c_w2"][:], sb["c_w2"][:], ACT.Copy, scale=0.5)
            for dst, src, scale in (("r_u", "r_u", 0.5), ("r_uo", "r_uo", 0.5), ("r_bf", "r_bf0", 0.5),
                                    ("r_bi", "r_bi0", 0.5), ("r_c0", "r_c00", 2.0)):
                last = nc.scalar.activation(sb[dst][:], sb[src][:], ACT.Copy, scale=scale)
            last.then_inc(ev["weights_scaled"], 1)
            out_of("gathered", banks[6][:, 0:SLOTS], sb["xsT"][:], "xsT")
            out_of("masks_u", banks[4][:, 0:SLOTS], sb["umask"][:], "u_ready")
            out_of("selected_t", banks[0][:, 0:SLOTS], sb["selT"][:], "selT_ready")
            act.wait_ge(ev["shifted"], nth["shifted"])
            nc.scalar.activation(att[:], att[:], ACT.Exp).then_inc(ev["exps"], 1)
            out_of("attended_t", banks[0][:, 0:SLOTS], sb["fT"][:], "attended_sb")
            out_of("x1n_t", banks[0][:, 0:SLOTS], sb["x1nT"][:], "x1n_sb")
            act.wait_ge(ev["hidden"], nth["hidden"])
            nc.scalar.activation(hid, ps_all[:, 2:4, :].rearrange("p a c -> p (a c)"), ACT.Copy)\
                .then_inc(ev["hidden_sb"], 1)
            act.wait_ge(ev["inner"], nth["inner"])
            nc.scalar.activation(gate, gate, ACT.Tanh, scale=GELU_C).then_inc(ev["tanhs"], 1)

        @block.gpsimd
        def _(pool):
            pool.wait_ge(late_loaded, 16 * LATE_LOADS)
            key_mask = sb["kmask"][:].rearrange("p b k -> p (b k)")
            nc.gpsimd.tensor_copy(key_mask, key_mask.bitcast(I32)).then_inc(ev["key_mask"], 1)
            pool.wait_ge(ev["eq"], nth["eq"])
            nc.gpsimd.tensor_tensor(PT3, PT3, bc(sb["upper"][:], 1, B), ALU.mult).then_inc(ev["eq_masked"], 1)
            pool.wait_ge(ev["mean_square"], nth["mean_square"])
            nc.gpsimd.tensor_tensor(sb["rms"][:], sb["ss"][:], sb["mhalf"][:].to_broadcast([128, NT]), ALU.pow)\
                .then_inc(ev["rstd"], 1)
            pool.wait_ge(ev["factor"], nth["factor"])
            pool.wait_ge(ev["count_ge"], nth["count_ge"])
            nc.gpsimd.tensor_tensor(P3, X3, bc(sb["factor"][:], 2, D), ALU.mult).then_inc(ev["scaled_x"], 1)
            pool.wait_ge(ev["mean_square2"], nth["mean_square2"])
            nc.gpsimd.tensor_tensor(sb["rms2"][:], sb["ss2"][:], sb["mhalf"][:].to_broadcast([128, NT]), ALU.pow)\
                .then_inc(ev["rstd2"], 1)
            pool.wait_ge(ev["var_eps"], nth["var_eps"])
            nc.gpsimd.tensor_tensor(sb["ln16"][:], sb["ve16"][:], sb["mhalf"][:].to_broadcast([128, B]), ALU.pow)\
                .then_inc(ev["rstd3"], 1)

        @block.vector
        def _(dve):
            def tt(out, a, b_, op, done):
                nc.vector.tensor_tensor(out, a, b_, op).then_inc(ev[done], 1)

            def total(out, in_, done, op=ALU.add):
                nc.vector.tensor_reduce(out, in_, op=op, axis=AX.X).then_inc(ev[done], 1)

            tt(P3, X3, bc(sb["c_rw_row"][:], 1, B), ALU.mult, "weighed")
            dve.wait_ge(ev["weighed"], nth["weighed"])
            total(wt[:], P3, "summed")
            dve.wait_ge(ev["summed"], nth["summed"])
            nc.vector.tensor_scalar(wt[:], wt[:], sb["c_rb"][:], None, ALU.add).then_inc(ev["weights"], 1)
            dve.wait_ge(ev["weights"], nth["weights"])
            nc.vector.tensor_copy(big[:, 0:SB].rearrange("p (b t) -> p b t", b=B), bc(wt[:], 2, S))\
                .then_inc(ev["spread"], 1)
            dve.wait_ge(ev["spread_t"], nth["spread_t"])
            others = scores4.rearrange("p a (b j) -> p (a b) j", j=S)
            tt(PT3, others, bc(wt[:], 2, S), ALU.is_equal, "eq")
            dve.wait_ge(ev["summed"], nth["summed"])
            tt(P3, others, bc(wt[:], 2, S), ALU.is_ge, "ge")
            dve.wait_ge(ev["ge"], nth["ge"])
            total(sb["count_ge"][:], P3, "count_ge")
            dve.wait_ge(ev["eq_masked"], nth["eq_masked"])
            total(sb["count_eq"][:], PT3, "count_eq")
            dve.wait_ge(ev["count_eq"], nth["count_eq"])
            dve.wait_ge(ev["count_ge"], nth["count_ge"])
            tt(rank[:], sb["count_ge"][:], sb["count_eq"][:], ALU.subtract, "rank")
            nc.vector.tensor_scalar(sb["factor"][:], sb["count_ge"][:], KC + 0.5, 1.0, ALU.is_gt, ALU.add)\
                .then_inc(ev["factor"], 1)
            dve.wait_ge(ev["rank"], nth["rank"])
            tt(sel[:], bc(rank[:], 2, TOP), bc(sb["iota"][:], 1, B), ALU.is_equal, "select")
            dve.wait_ge(ev["tables"], nth["tables"])
            prod = sb["cs_prod"]
            for t in range(NT):
                last = nc.vector.tensor_tensor(prod[:, t, :, :],
                                               banks[5][:, t * 64:(t + 1) * 64].rearrange("p (m c) -> p m c", m=MB),
                                               bc(sb["mbatch"][:, t, :], 2, 16), ALU.mult)
            last.then_inc(ev["cs_prod"], 1)
            dve.wait_ge(ev["cs_prod"], nth["cs_prod"])
            total(sb["cs"][:], prod[:].rearrange("p t m c -> p t c m"), "cs_ready")
            dve.wait_ge(ev["tokens"], nth["tokens"])
            tokens = sb["tokens"]
            nc.vector.tensor_copy(tokens[:].rearrange("p t d -> p (t d)"), banks[7][:, 0:SLOTS])\
                .then_inc(ev["tokens_ready"], 1)
            dve.wait_ge(ev["tokens_ready"], nth["tokens_ready"])
            tt(sb["sq"][:], tokens[:], tokens[:], ALU.mult, "squares")
            dve.wait_ge(ev["squares"], nth["squares"])
            total(sb["ss"][:], sb["sq"][:], "square_sum")
            dve.wait_ge(ev["square_sum"], nth["square_sum"])
            nc.vector.tensor_scalar(sb["ss"][:], sb["ss"][:], 1.0 / D, RMS_EPS, ALU.mult, ALU.add)\
                .then_inc(ev["mean_square"], 1)
            dve.wait_ge(ev["qkv"], nth["qkv"])
            nc.vector.tensor_scalar(sb["wsel"][:], banks[3][:, 0:NT], sb["c_rb"][:], sb["valid"][:],
                                    ALU.add, ALU.mult).then_inc(ev["wsel"], 1)
            dve.wait_ge(ev["dense_mask"], nth["dense_mask"])
            tt(sb["mprod"][:].rearrange("p t b r -> p (t b) r"),
               banks[6][:, 0:SLOTS].rearrange("p (x r) -> p x r", r=TOP),
               bc(sb["blocks2"][:].rearrange("p t b -> p (t b)"), 2, TOP), ALU.mult, "mask_prod")
            dve.wait_ge(ev["mask_prod"], nth["mask_prod"])
            total(sb["msel"][:], sb["mprod"][:].rearrange("p t b r -> p t r b"), "mask_ready")
            dve.wait_ge(ev["rstd"], nth["rstd"])
            tt(qkv[:], ps_all[:, 1:3, 0:3 * D], bc(sb["rms"][:], 2, 3 * D), ALU.mult, "qkv_ready")
            dve.wait_ge(ev["qkv_ready"], nth["qkv_ready"])
            dve.wait_ge(ev["cs_ready"], nth["cs_ready"])
            HH = HD // 2
            for t in range(NT):
                last = nc.vector.tensor_tensor(rot[:, t, :, 0:HH], qk[:, t, :, HH:HD],
                                               bc(sb["cs"][:, t, HD:HD + HH], 1, 2 * H), ALU.mult)
                last = nc.vector.tensor_tensor(rot[:, t, :, HH:HD], qk[:, t, :, 0:HH],
                                               bc(sb["cs"][:, t, HD + HH:2 * HD], 1, 2 * H), ALU.mult)
            last.then_inc(ev["rot_sin"], 1)
            for t in range(NT):
                last = nc.vector.tensor_tensor(roped[:, t, :, :], qk[:, t, :, :],
                                               bc(sb["cs"][:, t, 0:HD], 1, 2 * H), ALU.mult)
            last.then_inc(ev["rot_cos"], 1)
            dve.wait_ge(ev["rot_sin"], nth["rot_sin"])
            dve.wait_ge(ev["rot_cos"], nth["rot_cos"])
            tt(sb["roped"][:], sb["roped"][:], sb["rot"][:], ALU.add, "roped")
            dve.wait_ge(ev["roped"], nth["roped"])
            for part, src in ((0, scores4), (1, upper4)):
                n = min(8, KC - 8 * part)
                js = slice(8 * part, 8 * part + n)
                dve.wait_ge(ev[f"k{part}"], nth[f"k{part}"])
                flat = src.rearrange("p a (j t c) -> p (a j) t c", j=2, t=NT)
                for t in range(NT):
                    last = nc.vector.tensor_tensor(keys[:, js, t * D:(t + 1) * D], flat[:, 0:n, t, :],
                                                   bc(sb["roped"][:, t, 0:D], 1, n), ALU.mult)
                last.then_inc(ev[f"k{part}_prod"], 1)
                dve.wait_ge(ev[f"k{part}_prod"], nth[f"k{part}_prod"])
                total(att[:, :, js].rearrange("p x j -> p j x"),
                      keys[:, js, :].rearrange("p j (x c) -> p j x c", c=HD), f"k{part}_sum")
            dve.wait_ge(ev["k0_sum"], nth["k0_sum"])
            dve.wait_ge(ev["k1_sum"], nth["k1_sum"])
            dve.wait_ge(ev["mask_ready"], nth["mask_ready"])
            for t in range(NT):
                rows = att[:, t * H:(t + 1) * H, :]
                last = nc.vector.tensor_tensor(rows, rows, bc(sb["msel"][:, t, 0:KC], 1, H), ALU.add)
            last.then_inc(ev["masked"], 1)
            dve.wait_ge(ev["masked"], nth["masked"])
            total(sb["rmax"][:], att[:], "row_max", ALU.max)
            dve.wait_ge(ev["row_max"], nth["row_max"])
            tt(att[:], att[:], bc(sb["rmax"][:], 2, KC), ALU.subtract, "shifted")
            dve.wait_ge(ev["exps"], nth["exps"])
            total(sb["rsum32"][:], att[:], "row_sum")
            dve.wait_ge(ev["row_sum"], nth["row_sum"])
            nc.vector.reciprocal(sb["rmax"][:], sb["rsum32"][:]).then_inc(ev["row_inv"], 1)
            for part, src in ((0, scores4), (1, upper4)):
                n = min(8, KC - 8 * part)
                js = slice(8 * part, 8 * part + n)
                dve.wait_ge(ev[f"v{part}"], nth[f"v{part}"])
                nc.vector.tensor_tensor(keys[:, js, :].rearrange("p j (x c) -> p j x c", c=HD),
                                        src.rearrange("p a (j x c) -> p (a j) x c", j=2, c=HD)[:, 0:n, :, :],
                                        bc(att[:, :, js].rearrange("p x j -> p j x"), 3, HD), ALU.mult)\
                    .then_inc(ev[f"v{part}_prod"], 1)
            dve.wait_ge(ev["v0_prod"], nth["v0_prod"])
            dve.wait_ge(ev["v1_prod"], nth["v1_prod"])
            total(sb["vsum"][:], keys[:, 0:KC, :].rearrange("p j c -> p c j"), "v_sum")
            dve.wait_ge(ev["v_sum"], nth["v_sum"])
            dve.wait_ge(ev["row_inv"], nth["row_inv"])
            tt(sb["attended"][:].rearrange("p (x c) -> p x c", c=HD), sb["vsum"][:].rearrange("p (x c) -> p x c", c=HD),
               bc(sb["rmax"][:], 2, HD), ALU.mult, "attended")
            dve.wait_ge(ev["projected"], nth["projected"])
            x1 = sb["x1"]
            tt(x1[:].rearrange("p t d -> p (t d)"), banks[1][:, 0:SLOTS],
               tokens[:].rearrange("p t d -> p (t d)"), ALU.add, "x1")
            dve.wait_ge(ev["x1"], nth["x1"])
            tt(sb["sq"][:], x1[:], x1[:], ALU.mult, "squares2")
            dve.wait_ge(ev["squares2"], nth["squares2"])
            total(sb["ss2"][:], sb["sq"][:], "square_sum2")
            dve.wait_ge(ev["square_sum2"], nth["square_sum2"])
            nc.vector.tensor_scalar(sb["ss2"][:], sb["ss2"][:], 1.0 / D, RMS_EPS, ALU.mult, ALU.add)\
                .then_inc(ev["mean_square2"], 1)
            dve.wait_ge(ev["rstd2"], nth["rstd2"])
            dve.wait_ge(ev["attended_t"], nth["attended_t"])
            tt(sb["attended"][:].rearrange("p (t d) -> p t d", t=NT), x1[:], bc(sb["rms2"][:], 2, D), ALU.mult, "x1n")
            dve.wait_ge(ev["hidden_sb"], nth["hidden_sb"])
            nc.vector.scalar_tensor_tensor(out=gate, in0=hid, scalar=0.044715, in1=hid,
                                           op0=ALU.mult, op1=ALU.mult).then_inc(ev["cubed"], 1)
            dve.wait_ge(ev["cubed"], nth["cubed"])
            nc.vector.scalar_tensor_tensor(out=gate, in0=gate, scalar=1.0, in1=hid,
                                           op0=ALU.add, op1=ALU.mult).then_inc(ev["inner"], 1)
            dve.wait_ge(ev["tanhs"], nth["tanhs"])
            nc.vector.scalar_tensor_tensor(out=gate, in0=gate, scalar=1.0, in1=hid,
                                           op0=ALU.add, op1=ALU.mult).then_inc(ev["gated"], 1)
            for t in range(NT):
                last = nc.vector.tensor_scalar(sb["slot_w"][:, t, :], sb["blocks2"][:, t, :], sb["wsel"][:, t:t + 1],
                                               None, ALU.mult)
            last.then_inc(ev["slot_w"], 1)
            dve.wait_ge(ev["ff"], nth["ff"])
            tt(x1[:].rearrange("p t d -> p (t d)"), banks[1][:, 0:SLOTS], x1[:].rearrange("p t d -> p (t d)"),
               ALU.add, "x2")
            dve.wait_ge(ev["x2"], nth["x2"])
            dve.wait_ge(ev["slot_w"], nth["slot_w"])
            spread = big[:, 0:SB].rearrange("p (t b d) -> p t b d", t=NT, b=NB)
            for t in range(NT):
                last = nc.vector.tensor_tensor(spread[:, t, :, :], bc(x1[:, t, :], 1, NB), bc(sb["slot_w"][:, t, :], 2, D),
                                               ALU.mult)
            last.then_inc(ev["spread_x2"], 1)
            dve.wait_ge(ev["scattered"], nth["scattered"])
            dve.wait_ge(ev["scaled_x"], nth["scaled_x"])
            dve.wait_ge(ev["count_eq"], nth["count_eq"])
            tt(PT3, upper4.rearrange("p a (b d) -> p (a b) d", d=D), P3, ALU.add, "y")
            dve.wait_ge(ev["y"], nth["y"])
            for b in range(B):
                nc.vector.bn_stats(sb["bn16"][:, b, :], PT3[:, b, :])
            nc.vector.drain()
            for b in range(B):
                last = nc.vector.bn_aggr(sb["mv16"][:, b, :], sb["bn16"][:, b, :])
            last.then_inc(ev["aggregated"], 1)
            dve.wait_ge(ev["aggregated"], nth["aggregated"])
            nc.vector.tensor_scalar(sb["ve16"][:], sb["mv16"][:, :, 1], LN_EPS, None, ALU.add)\
                .then_inc(ev["var_eps"], 1)
            tt(PT3, PT3, bc(sb["mv16"][:, :, 0], 2, D), ALU.subtract, "centred")
            dve.wait_ge(ev["rstd3"], nth["rstd3"])
            dve.wait_ge(ev["centred"], nth["centred"])
            tt(X3, PT3, bc(sb["ln16"][:], 2, D), ALU.mult, "x_new")
            dve.wait_ge(ev["x_new"], nth["x_new"])


def wide_head_attention(nc, ps, sb, X, xs, late_loaded):
    S_ps, PT_ps, O_ps, M_ps = ps
    A, BB, C = S_ps[:, 2, :], S_ps[:, 3, :], M_ps
    with ExitStack() as ctx:
        def sem(what):
            return ctx.enter_context(nc.semaphore(f"wide_{what}"))

        x_loaded = [sem("x_loaded0"), sem("x_loaded1")]
        xt_done, xt_ready = sem("xt_done"), sem("xt_ready")
        q_done, q_ready, k_done, k_ready = sem("q_done"), sem("q_ready"), sem("k_done"), sem("k_ready")
        v_done, v_ready = sem("v_done"), sem("v_ready")
        s_done, max_ready, sub_ready, exp_ready = sem("s_done"), sem("max_ready"), sem("sub_ready"), sem("exp_ready")
        sum_ready, inv_ready, p_ready = sem("sum_ready"), sem("inv_ready"), sem("p_ready")
        pt_done, pt_ready, pv_done, o_ready = sem("pt_done"), sem("pt_ready"), sem("pv_done"), sem("o_ready")
        out_done, xb_ready, y_ready = sem("out_done"), sem("xb_ready"), sem("y_ready")
        var1_ready, rstd1_ready, yn_ready, y2_ready = (
            sem("var1_ready"), sem("rstd1_ready"), sem("yn_ready"), sem("y2_ready"))
        var2_ready, rstd2_ready, x_new, pool_step = sem("var2_ready"), sem("rstd2_ready"), sem("x_new"), sem("pool_step")
        block = ctx.enter_context(nc.Block())
        HP = PAIRS // 2
        PW = 3 * HW

        @block.sync
        def _(sp):
            def slot(i, p, half, stage):
                b = i + LEAD
                if has(b):
                    after(sp, xt_done, b - 1)
                    sp.dma_start(xs[:, p, :], one(X, b)).then_inc(x_loaded[p], 16)
            slots(sp, slot)

        @block.tensor
        def _(pe):
            pe.wait_ge(late_loaded, 16 * LATE_LOADS)
            def scores(b, u, p):
                pe.wait_ge(q_ready, 2 * b + u + 1)
                pe.wait_ge(k_ready, 2 * b + u + 1)
                after(pe, sub_ready, 2 * b + u)
                for e in range(HP):
                    pair = HP * u + e
                    last = nc.tensor.matmul(S_ps[:, e // 2, (e % 2) * 2 * S:(e % 2 + 1) * 2 * S], sb["QW"][:, p, pair, :],
                                            sb["KW"][:, p, pair, :, :].rearrange("p e k -> p (e k)"),
                                            start=True, stop=True)
                last.then_inc(s_done, 1)

            def transpose_probs(b, u):
                pe.wait_ge(p_ready, 2 * b + u + 1)
                after(pe, pt_ready, 2 * b + u)
                for h in range(UH):
                    last = nc.tensor.transpose(PT_ps[:, h // 4, (h % 4) * S:(h % 4 + 1) * S],
                                               sb["P"][:, u, h, :], sb["ident"][:])
                last.then_inc(pt_done, 1)

            def values(b, u, p):
                pe.wait_ge(pt_ready, 2 * b + u + 1)
                pe.wait_ge(v_ready, 2 * b + u + 1)
                after(pe, o_ready, 2 * b + u)
                for h in range(UH):
                    at = (HP * u + h // 2) * PW + (h % 2) * HW
                    last = nc.tensor.matmul(O_ps[:, (h // 2) * S:(h // 2 + 1) * S], sb["VW"][:, p, at:at + 128],
                                            sb["PT"][:, u, h, :], start=(h % 2 == 0), stop=(h % 2 == 1))
                last.then_inc(pv_done, 1)

            def project(weight, n, q, c, bank, done):
                for e in range(HP):
                    pair = HP * c + e
                    last = nc.tensor.matmul(bank[:, e * S:(e + 1) * S], weight[:, pair * 128:(pair + 1) * 128],
                                            sb["xT"][:, q, :], start=True, stop=True)
                last.then_inc(done, 1)

            def slot(i, p, half, stage):
                q = 1 - p
                b, n, r, z = i + LEAD, i + 1, i - 1, i - LAG
                if has(i):
                    scores(i, 1, p)
                if has(n):
                    pe.wait_ge(xt_ready, n + 1)
                    project(sb["d_q"], n, q, 0, A, q_done)
                if has(z):
                    if has(r):
                        pe.wait_ge(v_ready, 2 * r + 1)
                    after(pe, y_ready, z)
                    pe.wait_ge(o_ready, 2 * z + 2)
                    for c in range(PAIRS):
                        last = nc.tensor.matmul(BB[:, 0:D], sb["OT"][:, c // HP, (c % HP) * S:(c % HP + 1) * S],
                                                sb["d_o"][:, c * D:(c + 1) * D], start=(c == 0), stop=(c == PAIRS - 1))
                    last.then_inc(out_done, 1)
                if has(n):
                    if has(r):
                        pe.wait_ge(v_ready, 2 * r + 2)
                    project(sb["d_k"], n, q, 0, C, k_done)
                if has(r):
                    transpose_probs(r, 1)
                if has(n):
                    after(pe, y_ready, i - 1)
                    project(sb["d_q"], n, q, 1, BB, q_done)
                    pe.wait_ge(q_ready, 2 * n + 1)
                    project(sb["d_k"], n, q, 1, A, k_done)
                if has(r):
                    values(r, 0, q)
                if has(i):
                    if has(n):
                        pe.wait_ge(q_ready, 2 * n + 2)
                    else:
                        pe.wait_ge(y_ready, i - 1)
                    nc.tensor.matmul(BB[:], sb["xT"][:, p, :], sb["d_v"][:, 0:512], start=True, stop=True)\
                        .then_inc(v_done, 1)
                    if has(n):
                        pe.wait_ge(k_ready, 2 * n + 1)
                    else:
                        pe.wait_ge(v_ready, 2 * i)
                    nc.tensor.matmul(C[:], sb["xT"][:, p, :], sb["d_v"][:, 512:1024], start=True, stop=True)\
                        .then_inc(v_done, 1)
                if has(n):
                    scores(n, 0, q)
                if has(i):
                    transpose_probs(i, 0)
                if has(b):
                    pe.wait_ge(x_loaded[p], (half + 2) * 16)
                    if has(n):
                        pe.wait_ge(k_ready, 2 * n + 2)
                    nc.tensor.transpose(A[:, 0:S], xs[:, p, :], sb["ident"][:]).then_inc(xt_done, 1)
                if has(r):
                    values(r, 1, q)
            slots(pe, slot)

        @block.scalar
        def _(act):
            def exps(b, u):
                act.wait_ge(sub_ready, 2 * b + u + 1)
                nc.scalar.activation(sb["P"][:, u, :, :], sb["P"][:, u, :, :], ACT.Exp).then_inc(exp_ready, 1)

            def probs_out(b, u):
                act.wait_ge(pt_done, 2 * b + u + 1)
                after(act, pv_done, 2 * b + u - 1)
                nc.scalar.activation(sb["PT"][:, u, :, :].rearrange("p h q -> p (h q)"),
                                     PT_ps[:].rearrange("p a c -> p (a c)"), ACT.Copy).then_inc(pt_ready, 1)

            def queries_out(n, q, c):
                act.wait_ge(q_done, 2 * n + c + 1)
                after(act, s_done, 2 * (n - 2) + c + 1)
                for e in range(HP):
                    pair = HP * c + e
                    last = nc.scalar.activation(sb["QW"][:, q, pair, :], (A, BB)[c][:, e * S:(e + 1) * S], ACT.Identity,
                                                bias=sb["d_qbs"][:, pair:pair + 1], scale=sb["d_qs"][:, pair:pair + 1])
                last.then_inc(q_ready, 1)

            def values_out(b, p, c):
                act.wait_ge(v_done, 2 * b + c + 1)
                after(act, pv_done, 2 * (b - 2) + c + 1)
                pairs = sb["VW"][:, p, c * HP * PW:(c + 1) * HP * PW].rearrange("p (a w) -> p a w", a=HP)
                for e in range(2):
                    last = nc.scalar.activation(pairs[:, :, 2 * e * HW:(2 * e + 1) * HW],
                                                (BB, C)[c].rearrange("p (a e w) -> p a e w", a=HP, e=2)[:, :, e, :],
                                                ACT.Copy)
                last.then_inc(v_ready, 1)

            def output_out(b, u):
                act.wait_ge(pv_done, 2 * b + u + 1)
                after(act, out_done, b)
                nc.scalar.activation(sb["OT"][:, u, :], O_ps[:], ACT.Copy).then_inc(o_ready, 1)

            def slot(i, p, half, stage):
                b, n, r = i + LEAD, i + 1, i - 1
                if has(n):
                    queries_out(n, 1 - p, 0)
                if has(r):
                    probs_out(r, 1)
                if has(n):
                    queries_out(n, 1 - p, 1)
                if has(i):
                    exps(i, 1)
                if has(r):
                    output_out(r, 0)
                if has(i):
                    values_out(i, p, 0)
                    values_out(i, p, 1)
                    probs_out(i, 0)
                if has(b):
                    act.wait_ge(xt_done, b + 1)
                    after(act, v_done, 2 * i + 2)
                    nc.scalar.activation(sb["xT"][:, p, :], A[:, 0:S], ACT.Copy).then_inc(xt_ready, 1)
                if has(n):
                    exps(n, 0)
                if has(r):
                    output_out(r, 1)
            slots(act, slot)

        @block.vector
        def _(dve):
            def shift(b, u):
                unit = S_ps[:, 0:2, :].rearrange("p a (h k) -> p (a h) k", k=S)
                dve.wait_ge(s_done, 2 * b + u + 1)
                after(dve, sub_ready, 2 * b + u)
                nc.vector.tensor_reduce(sb["mx"][:], unit, op=ALU.max, axis=AX.X).then_inc(max_ready, 1)
                dve.wait_ge(max_ready, 2 * b + u + 1)
                after(dve, pt_done, 2 * b + u - 1)
                nc.vector.tensor_tensor(sb["P"][:, u, :, :], unit, bc(sb["mx"][:], 2, S), ALU.subtract)\
                    .then_inc(sub_ready, 1)

            def inverse_sums(b, u):
                dve.wait_ge(exp_ready, 2 * b + u + 1)
                nc.vector.tensor_reduce(sb["rsum"][:, u, :], sb["P"][:, u, :, :], op=ALU.add, axis=AX.X)\
                    .then_inc(sum_ready, 1)
                dve.wait_ge(sum_ready, 2 * b + u + 1)
                after(dve, p_ready, 2 * b + u - 1)
                nc.vector.reciprocal(sb["rinv"][:, u, :], sb["rsum"][:, u, :]).then_inc(inv_ready, 1)

            def keys_out(n, q, c):
                dve.wait_ge(k_done, 2 * n + c + 1)
                after(dve, s_done, 2 * (n - 2) + c + 1)
                pairs = slice(c * HP, (c + 1) * HP)
                for e in range(2):
                    rows = slice(e * HW, (e + 1) * HW)
                    last = nc.vector.tensor_tensor(sb["KW"][rows, q, pairs, e, :],
                                                   (C, A)[c][rows, :].rearrange("p (a k) -> p a k", a=HP),
                                                   bc(sb["d_kb"][rows, pairs], 2, S), ALU.add)
                last.then_inc(k_ready, 1)

            def slot(i, p, half, stage):
                n, z = i + 1, i - LAG
                if has(i):
                    inverse_sums(i, 0)
                if has(z):
                    dve.wait_ge(out_done, z + 1)
                    dve.wait_ge(xb_ready, z + 1)
                    after(dve, yn_ready, z)
                    nc.vector.tensor_tensor(sb["Y"][:], BB[:, 0:D], sb["XB"][:, p, :], ALU.add).then_inc(y_ready, 1)
                    dve.wait_ge(y_ready, z + 1)
                    nc.vector.bn_stats(sb["bn"][:], sb["Y"][:])
                    nc.vector.drain()
                    nc.vector.bn_aggr(sb["mv"][:], sb["bn"][:]).then_inc(var1_ready, 1)
                if has(i):
                    shift(i, 1)
                if has(z):
                    dve.wait_ge(rstd1_ready, z + 1)
                    after(dve, y2_ready, z)
                    nc.vector.tensor_scalar(sb["YN"][:], sb["Y"][:], sb["mv"][:, 0:1], sb["rstd"][:],
                                            ALU.subtract, ALU.mult).then_inc(yn_ready, 1)
                if has(n):
                    keys_out(n, 1 - p, 0)
                    keys_out(n, 1 - p, 1)
                if has(i):
                    inverse_sums(i, 1)
                if has(z):
                    dve.wait_ge(y2_ready, z + 1)
                    nc.vector.bn_stats(sb["bn2"][:], sb["Y2"][:])
                    nc.vector.drain()
                    nc.vector.bn_aggr(sb["mv2"][:], sb["bn2"][:]).then_inc(var2_ready, 1)
                if has(n):
                    shift(n, 0)
                if has(z):
                    dve.wait_ge(rstd2_ready, z + 1)
                    nc.vector.tensor_scalar(one(X, z), sb["Y2"][:], sb["mv2"][:, 0:1], sb["rstd2"][:],
                                            ALU.subtract, ALU.mult).then_inc(x_new, 1)
            slots(dve, slot)

        @block.gpsimd
        def _(pool):
            def normalise(b, u):
                pool.wait_ge(inv_ready, 2 * b + u + 1)
                nc.gpsimd.tensor_tensor(sb["P"][:, u, :, :], sb["P"][:, u, :, :], bc(sb["rinv"][:, u, :], 2, S),
                                        ALU.mult).then_inc(p_ready, 1)

            def rstd(z, k, var, mv, out, ready):
                pool.wait_ge(var, z + 1)
                nc.gpsimd.tensor_tensor(sb["ve"][:], sb[mv][:, 1:2], sb["eps"][:], ALU.add).then_inc(pool_step, 1)
                pool.wait_ge(pool_step, 3 * z + k)
                nc.gpsimd.tensor_tensor(sb[out][:], sb["ve"][:], sb["mhalf"][:], ALU.pow).then_inc(ready, 1)

            def slot(i, p, half, stage):
                r, z = i - 1, i - LAG
                if has(i):
                    normalise(i, 0)
                if has(z):
                    rstd(z, 1, var1_ready, "mv", "rstd", rstd1_ready)
                    pool.wait_ge(yn_ready, z + 1)
                    after(pool, x_new, z)
                    nc.gpsimd.tensor_tensor(sb["Y2"][:], sb["YN"][:], sb["gamma"][:], ALU.mult).then_inc(pool_step, 1)
                    pool.wait_ge(pool_step, 3 * z + 2)
                    nc.gpsimd.tensor_tensor(sb["Y2"][:], sb["Y2"][:], sb["XG"][:, p, :], ALU.add)\
                        .then_inc(y2_ready, 1)
                if has(r):
                    after(pool, y_ready, r - 1)
                    after(pool, y2_ready, r - 1)
                    nc.gpsimd.tensor_tensor(sb["XB"][:, 1 - p, :], one(X, r), sb["d_bias"][:], ALU.add)\
                        .then_inc(xb_ready, 1)
                    nc.gpsimd.tensor_tensor(sb["XG"][:, 1 - p, :], one(X, r), sb["beta"][:], ALU.add)
                if has(i):
                    normalise(i, 1)
                if has(z):
                    rstd(z, 3, var2_ready, "mv2", "rstd2", rstd2_ready)
            slots(pool, slot)


def recurrence_output(nc, bank, sb, X, hid, out):
    with ExitStack() as ctx:
        carried, carried_sb = (ctx.enter_context(nc.semaphore(f"rec_{n}")) for n in ("carried", "carried_sb"))
        tail = {n: ctx.enter_context(nc.semaphore(f"rec_{n}"))
                for n in ("pre", "act", "residual", "stats", "var", "rstd", "shift", "normed", "stored")}
        block = ctx.enter_context(nc.Block())
        CH = 4
        chunks = [slice(c * CH, (c + 1) * CH) for c in range(B // CH)]

        @block.tensor
        def _(pe):
            nc.tensor.matmul(bank[:, 0:D], sb["c2"][:], sb["r_uo"][:], start=True, stop=True).then_inc(carried, 1)

        @block.scalar
        def _(act):
            for c, steps in enumerate(chunks):
                act.wait_ge(tail["pre"], c + 1)
                nc.scalar.activation(hid[:, steps, :], hid[:, steps, :], ACT.Tanh).then_inc(tail["act"], 1)
            for c, steps in enumerate(chunks):
                act.wait_ge(tail["shift"], c + 1)
                for b in range(c * CH, (c + 1) * CH):
                    last = nc.scalar.activation(hid[:, b, :], hid[:, b, :], ACT.Identity,
                                                bias=sb["nshift"][:, b:b + 1], scale=sb["ln16"][:, b:b + 1])
                last.then_inc(tail["normed"], 1)

        @block.vector
        def _(dve):
            dve.wait_ge(carried, 1)
            nc.vector.tensor_tensor(sb["cu"][:], bank[:, 0:D], sb["r_bo"][:], ALU.add).then_inc(carried_sb, 1)
            dve.wait_ge(carried_sb, 1)
            for c, steps in enumerate(chunks):
                nc.vector.tensor_tensor(hid[:, steps, :], hid[:, steps, :], bc(sb["cu"][:], 1, CH), ALU.add)\
                    .then_inc(tail["pre"], 1)
            for c, steps in enumerate(chunks):
                dve.wait_ge(tail["residual"], c + 1)
                for b in range(c * CH, (c + 1) * CH):
                    nc.vector.bn_stats(sb["bn16"][:, b, :], hid[:, b, :])
                nc.vector.drain()
                for b in range(c * CH, (c + 1) * CH):
                    last = nc.vector.bn_aggr(sb["mv16"][:, b, :], sb["bn16"][:, b, :])
                last.then_inc(tail["stats"], 1)
                dve.wait_ge(tail["stats"], c + 1)
                nc.vector.tensor_scalar(sb["ve16"][:, steps], sb["mv16"][:, steps, 1], LN_EPS, None, ALU.add)\
                    .then_inc(tail["var"], 1)
            for c, steps in enumerate(chunks):
                dve.wait_ge(tail["rstd"], c + 1)
                nc.vector.scalar_tensor_tensor(out=sb["nshift"][:, steps], in0=sb["mv16"][:, steps, 0], scalar=-1.0,
                                               in1=sb["ln16"][:, steps], op0=ALU.mult, op1=ALU.mult)\
                    .then_inc(tail["shift"], 1)

        @block.gpsimd
        def _(pool):
            for c, steps in enumerate(chunks):
                pool.wait_ge(tail["act"], c + 1)
                nc.gpsimd.tensor_tensor(hid[:, steps, :], hid[:, steps, :], X[:, steps, :], ALU.add)\
                    .then_inc(tail["residual"], 1)
            for c, steps in enumerate(chunks):
                pool.wait_ge(tail["var"], c + 1)
                nc.gpsimd.tensor_tensor(sb["ln16"][:, steps], sb["ve16"][:, steps],
                                        sb["mhalf"][:].to_broadcast([S, CH]), ALU.pow).then_inc(tail["rstd"], 1)

        @block.sync
        def _(sp):
            for c, steps in enumerate(chunks):
                sp.wait_ge(tail["normed"], c + 1)
                sp.dma_start(out[steps, :, :].rearrange("b s d -> s b d"), hid[:, steps, :]).then_inc(tail["stored"], 16)
            sp.wait_ge(tail["stored"], 16 * len(chunks))


def decoder(nc, dram, out, layers=(1, 2, 3, 4, 5, 6)):
    with ExitStack() as ctx:
        def buf(name, shape, dt=F32):
            return ctx.enter_context(nc.sbuf_tensor(name, shape, dt))

        banks = ctx.enter_context(nc.psum_tensor("banks", [128, 8, 512], F32))
        ps = [banks[:, 0:4, :], banks[:, 4:6, :], banks[:, 6, :], banks[:, 7, :]]
        X = buf("X", [S, B, D])
        xs = buf("xs", [S, 2, D])
        sb, packs = {}, {}
        for pack, entries in PACKS.items():
            packs[pack] = buf("loaded_" + pack, [128, width(entries)])
            at = 0
            for name, _, rows, columns in entries:
                sb[name] = packs[pack][0:rows, at:at + columns]
                at += columns
        packs["rows"], at = buf("loaded_rows", [S, width(ROWS)]), 0
        for name, _, columns in ROWS:
            sb[name] = packs["rows"][:, at:at + columns]
            at += columns
        sb["blocks2"] = sb["blocks2"].rearrange("p (t b) -> p t b", t=NT)
        sb["mbatch"] = sb["mbatch"].rearrange("p (t m) -> p t m", t=NT)
        for name, shape in dict(
                a_k=[D, D], a_v=[D, D], a_kb=[D, 1], a_vb=[D, 1],                 a_bias=[S, D], b_qr=[D, D], b_kr=[D, D],                 e_bias=[S, D],
                pos=[D, S], ones=[128, 128],
                spread=[D, PAIRS * D], turns=[D, S + 4 * MB], angle=[D, S + 4 * MB], ang=[D, 2, S + 4 * MB],
                trig=[D, 2, S + 4 * MB], rope=[D, 4, S],
                kmask=[D, B, S], mhalf=[S, 1], eps=[S, 1], a_qbs=[D, 1], e_qbs=[D, 1],
                xT=[D, 2, S], cT=[D, 2, S], QK=[D, 2, S], rest=[D, 2, S], RP=[D, 4 * S], big=[128, 2 * H * S],
                Vx=[S, 2, H * SLOT * 9 // 1], P=[S, 2, UH, S], PT=[S, 2, UH, S], mx=[S, UH], O=[128, 2 * S],
                rden=[S, H], ON=[S, D], ONT=[D, S], XB=[S, 2, D], Y=[S, D], bn=[S, 6], mv=[S, 2], ve=[S, 1],
                rstd=[S, 1], d_qs=[128, PAIRS], d_qbs=[128, PAIRS], d_bias=[S, D],
                QW=[128, 2, PAIRS, S], KW=[128, 2, PAIRS, 2, S],
                VW=[S, 2, PAIRS * 3 * HW], OT=[128, 2, PAIRS // 2 * S], rsum=[S, 2, UH], rinv=[S, 2, UH],
                YN=[S, D],
                                pos4=[S, MB], cs_table=[S, MB, 2 * HD], amask=[S, MB, S],
                                wt=[S, B], rank=[S, B], sel=[S, B, TOP], count_ge=[S, B],
                count_eq=[S, B], factor=[S, B], xsT=[D, NT * 128], umask=[S, NT * 128], selT=[128, NT * 128],
                cs_prod=[128, NT, MB, 2 * HD], cs=[128, NT, 2 * HD], tokens=[128, NT, D], sq=[128, NT, D],
                ss=[128, NT], rms=[128, NT], ss2=[128, NT], rms2=[128, NT], wsel=[128, NT],
                mprod=[128, NT, NB, TOP], msel=[128, NT, TOP], qkv=[128, NT, 3 * D], roped=[128, NT, 2 * D],
                rot=[128, NT, 2 * D], att=[128, NT * H, KC], rmax=[128, NT * H], rsum32=[128, NT * H],
                vsum=[128, NT * D], attended=[128, NT * D], fT=[D, NT * 128], x1=[128, NT, D], x1nT=[D, NT * 128],
                slot_w=[128, NT, NB], bn16=[S, B, 6], mv16=[S, B, 2],
                ve16=[S, B], r_bf=[D, 1], r_bi=[D, 1], r_c0=[D, 1],                 c2=[D, S], xr=[D, S], fg=[D, S], ig=[D, S], gg=[D, S],
                ca=[D, S], cb=[D, S], cu=[S, D], nshift=[S, B], ln16=[S, B], Y2=[S, D], XG=[S, 2, D], bn2=[S, 6], mv2=[S, 2], rstd2=[S, 1]).items():
            sb[name] = buf(name, shape)
        for name, shape, dt in (("pos_i", [D, S], I32), ("pos4_i", [S, MB], I32), ("identb", [128, 128], BF16),
                                ("causal", [S, 4, S], BF16),
                                ("parts", [D, 2, 2 * 3, S], BF16)):
            sb[name] = buf(name, shape, dt)
        sb["stacked"] = sb["big"][:].bitcast(BF16).rearrange("p (e h n x) -> p e h n x", e=2, h=H, n=2)
        late_loaded = ctx.enter_context(nc.semaphore("late_loaded"))
        setup_small_heads(nc, ps, sb, packs, X, dram, late_loaded)
        small_heads = ps, sb, X, xs
        context = dram["ctxT"].rearrange("d (b s) -> d b s", b=B)
        self0 = dict(q=sb["a_q"], k=sb["a_k"], v=sb["a_v"], o=sb["a_o"], qb=sb["a_qbs"], kb=sb["a_kb"],
                     qs=float(HD) ** -0.5, bias=sb["a_bias"])
        cross0 = dict(q=sb["b_q"], qr=sb["b_qr"], k=sb["b_k"], kr=sb["b_kr"], v=sb["b_v"], o=sb["b_o"],
                      bias=sb["b_bias"], context=context, causal=sb["causal"],
                      rope=sb["rope"][:].rearrange("p n s -> p (n s)"))
        cross1 = dict(q=sb["e_q"], k=sb["e_k"], v=sb["e_v"], o=sb["e_o"], qb=sb["e_qbs"], kb=sb["e_kb"],
                      qs=float(HD) ** -0.5, bias=sb["e_bias"], context=context, key_mask=sb["kmask"])
        first = [w for n, w in ((1, self0), (2, cross0)) if n in layers]
        if first:
            small_head_attention(nc, "layer0", *small_heads, first)
        if 3 in layers:
            routed_ffn(nc, banks, sb, X, late_loaded)
        if 4 in layers:
            wide_head_attention(nc, ps, sb, X, xs, late_loaded)
        own = sb["QW"][:].rearrange("p u h k -> p (u h) k")
        if 5 in layers:
            small_head_attention(nc, "layer1", *small_heads, [cross1], own)
        if 6 in layers:
            recurrence_output(nc, banks[:, 0, :], sb, X, own, out)
        else:
            with nc.semaphore("stored") as stored, nc.Block() as block:
                @block.sync
                def _(sp):
                    sp.dma_start(out.rearrange("b s d -> s b d"), X[:]).then_inc(stored, 16)
                    sp.wait_ge(stored, 16)


def constants():
    part = np.arange(128)
    ident = np.eye(128, dtype=np.float32)
    causal = np.where(part[None, :] > part[:, None], np.float32(NEG), np.float32(0))
    inv = 1.0 / np.float32(ROPE_BASE) ** (np.arange(0, HD, 2, dtype=np.float32) / np.float32(HD))
    blocks = (part[:, None] // TOP == np.arange(NB)[None]).astype(np.float32)
    mbatch = np.stack([(np.minimum(t * NB + part // TOP, MB - 1)[:, None] == np.arange(MB)[None]) for t in range(NT)], 1)
    repeat = (part[:, None, None] // TOP == part[None, None, :] // TOP) \
        & (part[:, None, None] % TOP == np.arange(TOP)[None, :, None])
    return {"upper": (part[None, :] >= part[:, None]).astype(np.float32),
            "iota": np.tile(np.arange(TOP, dtype=np.float32), (S, 1)),
            "valid": (part % TOP < KC).astype(np.float32)[:, None].copy(),
            "blocks2": np.concatenate([blocks, blocks], 1), "mbatch": mbatch.astype(np.float32).reshape(128, -1),
            "repeat": repeat.astype(np.float32).reshape(128, -1),
            "inv4": np.tile(inv.astype(np.float32), (S, 1)),
            "ident": ident, "causal": causal.astype(np.float32),
            "inv_freq": np.repeat(np.tile(inv.astype(np.float32), 2), H)[:, None].copy()}


def laid_out(inputs):
    pieces = dict(inputs, **constants())
    for name in ("L0_attn_Wl", "L0_xattn_wq", "L0_xattn_wk", "L0_xattn_wv", "L0_xattn_wo_w", "L1_xattn_Wq",
                 "L1_xattn_Wk", "L1_xattn_Wv", "L1_xattn_Wp", "L1_attn_Wq", "L1_attn_Wk", "L1_attn_Wv",
                 "L1_ffn_wo", "L1_ffn_uo"):
        pieces[name + "T"] = inputs[name].T
    for name in ("L0_attn_Wq", "L0_attn_Wk", "L0_attn_bq", "L0_attn_bk", "L0_xattn_wqT", "L0_xattn_wkT",
                 "L1_xattn_WqT", "L1_xattn_WkT", "L1_xattn_bq", "L1_xattn_bk"):
        piece = pieces[name]
        pieces[name + "_by_feature"] = piece.reshape(-1, H, HD).transpose(0, 2, 1).reshape(piece.shape)
    pieces["L0_ffn_wqkv"] = np.concatenate([inputs["L0_ffn_w" + n] for n in "qkv"], 1)
    pieces["L1_ffn_w"] = np.concatenate([inputs["L1_ffn_w" + n].T for n in "fic"], 1)
    pieces["L1_ffn_u"] = np.concatenate([inputs["L1_ffn_u" + n].T for n in "fic"], 1)
    pieces["L1_attn_Wo_pairs"] = inputs["L1_attn_Wo"].T.reshape(PAIRS, 128, D).transpose(1, 0, 2).reshape(128, -1)
    for name in ("bq", "bk", "bv"):
        pieces[f"L1_attn_{name}_pairs"] = inputs["L1_attn_" + name].reshape(PAIRS, 128).T
    pieces["L1_attn_scale_pairs"] = np.repeat(inputs["L1_attn_adaptive_scale"].reshape(PAIRS, 2).T, HW, axis=0)
    pieces["L0_ffn_w2_chunks"] = inputs["L0_ffn_w2"].reshape(FF // 128, 128, D).transpose(1, 0, 2).reshape(128, -1)
    pieces["L0_ffn_router_w_row"] = inputs["L0_ffn_router_w"].reshape(D)

    arrays = {name: pieces[name] for name in ("x", "pos_S2", "mask_BxS2_ik0", "L0_ffn_attention_mask", "repeat")}
    for pack, entries in PACKS.items():
        packed, at = np.zeros((128, width(entries)), np.float32), 0
        for _, name, rows, columns in entries:
            packed[0:rows, at:at + columns] = pieces[name].reshape(rows, columns)
            at += columns
        arrays[pack] = packed
    arrays["rows"] = np.concatenate([pieces[name].reshape(-1) for _, name, _ in ROWS])
    arrays["ctxT"] = inputs["ctx_1024"].transpose(2, 0, 1).reshape(D, B * S)
    arrays["L0_ffn_position_ids_t"] = inputs["L0_ffn_position_ids"].T
    return {name: np.ascontiguousarray(a) for name, a in arrays.items()}


def kernel(**inputs):
    import numpy as _np
    import concourse.bacc as _bacc
    from concourse import mybir as _mybir
    from concourse.bass_utils import run_bass_kernel_spmd as _run

    nc = _bacc.Bacc("TRN2", target_bir_lowering=False, num_devices=1)
    arrays = laid_out({name: _np.asarray(a) for name, a in inputs.items()})
    dram = {name: nc.dram_tensor(f"in_{name}_dram", a.shape, _mybir.dt.from_np(a.dtype), kind="ExternalInput").ap()
            for name, a in arrays.items()}
    out = nc.dram_tensor("out_0_dram", (B, S, D), F32, kind="ExternalOutput").ap()
    decoder(nc, dram, out)
    r = _run(nc, [{f"in_{name}_dram": a for name, a in arrays.items()}], core_ids=[0])
    return r.results[0]["out_0_dram"]
```

```python
from contextlib import ExitStack

import concourse.bass as bass
import numpy as np
from concourse import mybir

ALU = mybir.AluOpType
ACT = mybir.ActivationFunctionType
AX = mybir.AxisListType
F32 = mybir.dt.float32
BF16 = mybir.dt.bfloat16
I32 = mybir.dt.int32

B, S, D = 16, 128, 128
H = 16
HD = D // H
LAT = D // 4
FF = 512
HW = 64
PAIRS = H // 2
SLOT = 2 * HD
UH = H // 2
UC = UH * S
TOP = S // 8
KC = TOP - 1
NB = 128 // TOP
NT = B // NB
MB = 4
LEAD, LAG = 2, 2
EDGE = 3
LATE_LOADS = 7
TERMS = 6
LN_EPS = 1e-5
RMS_EPS = 1e-6
ROPE_BASE = 10000.0
TWO_PI = 2 * np.pi
NEG = -1e30


def bc(ap, axis, n):
    shape = list(ap.shape)
    shape.insert(axis, n)
    return ap.unsqueeze(axis).to_broadcast(shape)


def after(eng, sem, count):
    if isinstance(count, int) and count <= 0:
        return
    eng.wait_ge(sem, count)


def has(b, stages=1):
    return not isinstance(b, int) or 0 <= b < B * stages


def slots(eng, slot, stages=1):
    for i in range(-EDGE, EDGE):
        slot(i, i % 2, i // 2, 0)
    for stage in range(stages):
        with eng.Fori(0, (B - 2 * EDGE) // 2) as j:
            for p in range(2):
                slot(j * 2 + (B * stage + EDGE + p), (EDGE + p) % 2, j + (B * stage + EDGE + p) // 2, stage)
        for i in range(B * (stage + 1) - EDGE, B * (stage + 1) + EDGE):
            slot(i, i % 2, i // 2, stage)


def one(t, i):
    return t[:, bass.ds(i, 1), :].rearrange("p o d -> p (o d)")


FIRST = [
    ("a_q", "L0_attn_Wq_by_feature", D, D), ("a_lT", "L0_attn_WlT", LAT, D), ("a_k0", "L0_attn_Wk_by_feature", LAT, D),
    ("a_v0", "L0_attn_Wv", LAT, D), ("a_o", "L0_attn_Wo", D, D),
    ("a_qb", "L0_attn_bq_by_feature", D, 1), ("a_bl", "L0_attn_bl", LAT, 1), ("a_bk", "L0_attn_bk_by_feature", D, 1),
    ("a_bv", "L0_attn_bv", D, 1), ("e_qb", "L1_xattn_bq_by_feature", D, 1), ("e_kb", "L1_xattn_bk_by_feature", D, 1),
    ("e_bv", "L1_xattn_bv", D, 1), ("d_qb", "L1_attn_bq_pairs", 128, PAIRS), ("d_kb", "L1_attn_bk_pairs", 128, PAIRS),
    ("d_vb", "L1_attn_bv_pairs", 128, PAIRS), ("d_as", "L1_attn_scale_pairs", 128, PAIRS),
]
SECOND = [
    ("b_q", "L0_xattn_wqT_by_feature", D, D), ("b_k", "L0_xattn_wkT_by_feature", D, D), ("b_v", "L0_xattn_wvT", D, D),
    ("b_o", "L0_xattn_wo_wT", D, D),
]
LATE = [
    ("c_qkv", "L0_ffn_wqkv", D, 3 * D), ("c_o", "L0_ffn_wo", D, D), ("c_w1", "L0_ffn_w1", D, FF),
    ("c_w2", "L0_ffn_w2_chunks", 128, FF), ("c_rw", "L0_ffn_router_w", D, 1),
    ("c_ln1", "L0_ffn_ln1", D, 1), ("c_ln2", "L0_ffn_ln2", D, 1),
    ("r_w", "L1_ffn_w", D, 3 * D), ("r_u", "L1_ffn_u", D, 3 * D), ("r_wo", "L1_ffn_woT", D, D),
    ("r_uo", "L1_ffn_uoT", D, D), ("r_bf0", "L1_ffn_bf", D, 1), ("r_bi0", "L1_ffn_bi", D, 1),
    ("r_bc", "L1_ffn_bc", D, 1), ("r_c00", "L1_ffn_in_c", D, 1),
    ("e_q", "L1_xattn_WqT_by_feature", D, D), ("e_k", "L1_xattn_WkT_by_feature", D, D), ("e_v", "L1_xattn_WvT", D, D),
    ("e_o", "L1_xattn_WpT", D, D), ("d_o", "L1_attn_Wo_pairs", 128, PAIRS * D),
]
LAST = [
    ("d_q", "L1_attn_WqT", D, H * HW), ("d_k", "L1_attn_WkT", D, H * HW), ("d_v", "L1_attn_WvT", D, H * HW),
]
CONSTANTS = [
    ("ident", "ident", 128, 128), ("inv", "inv_freq", D, 1), ("inv4", "inv4", S, 4),
    ("causalf", "causal", S, S), ("upper", "upper", S, S), ("iota", "iota", S, TOP), ("valid", "valid", 128, 1),
    ("blocks2", "blocks2", 128, NT * NB), ("mbatch", "mbatch", 128, NT * MB),
]
PACKS = {"first": FIRST, "second": SECOND, "late": LATE, "last": LAST, "constants": CONSTANTS}
ROWS = [("a_bo", "L0_attn_bo", D), ("b_bias", "L0_xattn_wo_b", D), ("e_bp", "L1_xattn_bp", D),
        ("d_bo", "L1_attn_bo", D), ("gamma", "L1_attn_gamma", D), ("beta", "L1_attn_beta", D),
        ("c_rw_row", "L0_ffn_router_w_row", D), ("c_rb", "L0_ffn_router_b", 1), ("r_bo", "L1_ffn_bo", D)]


def width(entries):
    return sum(entry[-1] for entry in entries)


def setup_small_heads(nc, ps, sb, packs, X, dram):
    S_ps, PT_ps, O_ps, M_ps = ps
    with ExitStack() as ctx:
        def sem(what):
            return ctx.enter_context(nc.semaphore(f"setup_{what}"))

        loaded, loaded_c, filled = sem("loaded"), sem("loaded_constants"), sem("filled")
        prepared = sem("prepared")
        products_a, copied_a = sem("products_a"), sem("copied_a")
        rope_step = sem("rope_step")
        sin_done, table_ready, zeros_ready = sem("sin_done"), sem("table_ready"), sem("zeros_ready")
        bias_spread, bias_product = sem("bias_spread"), sem("bias_product")
        block = ctx.enter_context(nc.Block())
        EARLY, EARLY_CONSTANTS = 4, 3

        @block.sync
        def _(sp):
            sp.dma_start(packs["first"][:], dram["first"]).then_inc(loaded, 16)
            sp.dma_start(X[:], dram["x"].rearrange("b s d -> s b d")).then_inc(loaded, 16)
            sp.dma_start(packs["rows"][:], bc(dram["rows"], 0, S)).then_inc(loaded, 16)
            sp.dma_start(packs["second"][:], dram["second"]).then_inc(loaded, 16)

        @block.scalar
        def _(act):
            act.dma_start(sb["pos_i"][:], bc(dram["pos_S2"], 0, D)).then_inc(loaded_c, 16)
            act.dma_start(sb["pos4_i"][:], dram["L0_ffn_position_ids_t"][0:S, :]).then_inc(loaded_c, 16)
            act.dma_start(packs["constants"][:], dram["constants"]).then_inc(loaded_c, 16)
            for half in range(2):
                act.wait_ge(rope_step, 6 * half + 6)
                nc.scalar.activation(sb["trig"][:, half, :], sb["ang"][:, half, :], ACT.Sin).then_inc(sin_done, 1)

        @block.gpsimd
        def _(pool):
            nc.gpsimd.memset(sb["Vx"][:], 0.0).then_inc(zeros_ready, 1)
            nc.gpsimd.memset(sb["KW"][:], 0.0).then_inc(zeros_ready, 1)
            nc.gpsimd.memset(sb["VW"][:], 0.0).then_inc(zeros_ready, 1)
            pool.wait_ge(zeros_ready, 3)

        @block.tensor
        def _(pe):
            pe.wait_ge(loaded, 16 * EARLY)
            nc.tensor.matmul(M_ps[:, 0:D], sb["a_lT"][:], sb["a_k0"][:], start=True, stop=True)
            nc.tensor.matmul(M_ps[:, D:2 * D], sb["a_lT"][:], sb["a_v0"][:], start=True, stop=True)
            nc.tensor.matmul(M_ps[:, 2 * D:2 * D + 1], sb["a_k0"][:], sb["a_bl"][:], start=True, stop=True)
            nc.tensor.matmul(M_ps[:, 2 * D + 1:2 * D + 2], sb["a_v0"][:], sb["a_bl"][:], start=True, stop=True)\
                .then_inc(products_a, 1)
            pe.wait_ge(bias_spread, 1)
            nc.tensor.matmul(O_ps[:, 0:D], sb["spread"][:, 0:D], sb["a_o"][:], start=True, stop=True)\
                .then_inc(bias_product, 1)

        @block.vector
        def _(dve):
            nc.vector.memset(sb["ones"][:], 1.0).then_inc(filled, 1)
            nc.vector.memset(sb["mhalf"][:], -0.5).then_inc(filled, 1)
            nc.vector.memset(sb["eps"][:], LN_EPS).then_inc(filled, 1)
            dve.wait_ge(zeros_ready, 1)
            for p in range(2):
                nc.vector.memset(sb["Vx"][:, p, :].rearrange("p (h c) -> p h c", h=H)[:, :, HD], 1.0)\
                    .then_inc(filled, 1)
            dve.wait_ge(filled, 5)
            dve.wait_ge(loaded_c, 16 * EARLY_CONSTANTS)
            nc.vector.tensor_copy(sb["pos"][:], sb["pos_i"][:]).then_inc(filled, 1)
            nc.vector.tensor_copy(sb["pos4"][:], sb["pos4_i"][:]).then_inc(filled, 1)
            dve.wait_ge(filled, 7)
            turns, angle, rounding = sb["turns"], sb["angle"], 1.5 * 2.0 ** 23
            c1 = float(np.float32(6.28125))
            c2 = float(np.float32(np.floor((TWO_PI - c1) * 2 ** 22) / 2 ** 22))
            c3 = float(TWO_PI - c1 - c2)
            nc.vector.tensor_scalar(angle[:, 0:S], sb["pos"][:], sb["inv"][:], None, ALU.mult).then_inc(table_ready, 1)
            nc.vector.tensor_tensor(angle[:, S:S + 4 * MB].rearrange("p (m c) -> p m c", m=MB), bc(sb["pos4"][:], 2, 4),
                                    bc(sb["inv4"][:], 1, MB), ALU.mult).then_inc(table_ready, 1)
            dve.wait_ge(table_ready, 2)
            step = [0]

            def link(instruction):
                step[0] += 1
                instruction.then_inc(rope_step, 1)
                dve.wait_ge(rope_step, step[0])

            for half, (quarter, shift_) in enumerate(((0.25, np.pi / 2), (0.0, 0.0))):
                a = sb["ang"][:, half, :]
                link(nc.vector.tensor_scalar(turns[:], angle[:], float(1 / TWO_PI), quarter, ALU.mult, ALU.add))
                link(nc.vector.tensor_scalar(turns[:], turns[:], rounding, rounding, ALU.add, ALU.subtract))
                link(nc.vector.scalar_tensor_tensor(out=a, in0=turns[:], scalar=-c1, in1=angle[:],
                                                    op0=ALU.mult, op1=ALU.add))
                link(nc.vector.scalar_tensor_tensor(out=a, in0=turns[:], scalar=-c2, in1=a,
                                                    op0=ALU.mult, op1=ALU.add))
                link(nc.vector.scalar_tensor_tensor(out=a, in0=turns[:], scalar=-c3, in1=a,
                                                    op0=ALU.mult, op1=ALU.add))
                if half == 0:
                    link(nc.vector.tensor_scalar(a, a, float(shift_), 3.1415925, ALU.add, ALU.min))
                else:
                    link(nc.vector.tensor_scalar(a, a, -3.1415925, 3.1415925, ALU.max, ALU.min))
            dve.wait_ge(sin_done, 2)
            nc.vector.tensor_scalar(sb["rope"][:, 0:2, :], sb["trig"][:, :, 0:S], float(HD) ** -0.5, None, ALU.mult)\
                .then_inc(table_ready, 1)
            nc.vector.tensor_copy(sb["rope"][:, 2:4, :], sb["trig"][:, :, 0:S]).then_inc(table_ready, 1)
            for at, which, sign in ((0, 0, 1.0), (4, 0, 1.0), (8, 1, -1.0), (12, 1, 1.0)):
                nc.vector.tensor_scalar(sb["cs_table"][:, :, at:at + 4],
                                        sb["trig"][:, which, S:].rearrange("p (m c) -> p m c", m=MB), sign, None,
                                        ALU.mult).then_inc(table_ready, 1)
            nc.vector.tensor_copy(sb["identb"][:], sb["ident"][:]).then_inc(prepared, 1)
            nc.vector.tensor_copy(sb["causal"][:], bc(sb["causalf"][:], 1, 4)).then_inc(prepared, 1)
            dve.wait_ge(prepared, 2)
            dve.wait_ge(loaded, 16 * EARLY)
            for src, dst in (("b_q", "b_qr"), ("b_k", "b_kr")):
                nc.vector.tensor_scalar(sb[dst][:, 0:D // 2], sb[src][:, D // 2:D], -1.0, None, ALU.mult)\
                    .then_inc(prepared, 1)
                nc.vector.tensor_copy(sb[dst][:, D // 2:D], sb[src][:, 0:D // 2]).then_inc(prepared, 1)
            dve.wait_ge(prepared, 6)
            dve.wait_ge(products_a, 1)
            nc.vector.tensor_copy(sb["a_k"][:], M_ps[:, 0:D]).then_inc(copied_a, 1)
            nc.vector.tensor_copy(sb["a_v"][:], M_ps[:, D:2 * D]).then_inc(copied_a, 1)
            nc.vector.tensor_tensor(sb["a_kb"][:], M_ps[:, 2 * D:2 * D + 1], sb["a_bk"][:], ALU.add)\
                .then_inc(copied_a, 1)
            nc.vector.tensor_tensor(sb["a_vb"][:], M_ps[:, 2 * D + 1:2 * D + 2], sb["a_bv"][:], ALU.add)\
                .then_inc(copied_a, 1)
            dve.wait_ge(copied_a, 4)
            nc.vector.tensor_scalar(sb["spread"][:, 0:D], sb["ones"][:], sb["a_vb"][:], None, ALU.mult)\
                .then_inc(bias_spread, 1)
            dve.wait_ge(bias_product, 1)
            nc.vector.tensor_tensor(sb["a_bias"][:], O_ps[:, 0:D], sb["a_bo"][:], ALU.add).then_inc(prepared, 1)
            for name in ("a_qb", "e_qb"):
                nc.vector.tensor_scalar(sb[name + "s"][:], sb[name][:], float(HD) ** -0.5, None, ALU.mult)\
                    .then_inc(prepared, 1)
            dve.wait_ge(prepared, 9)
            dve.wait_ge(table_ready, 8)


TERM_PARTS = ((0, 0), (0, 1), (1, 0), (1, 1), (0, 2), (2, 0))
TERMS_OF_PART = ((0,), (1, 2, 3), (4, 5))


def small_head_attention(nc, name, ps, sb, X, xs, stages, own_outputs=None, later_loads=None):
    S_ps, PT_ps, O_ps, M_ps = ps
    N = len(stages)
    steps = own_outputs is not None
    unit_bank = (0, 0) if steps else (0, 2)
    f_bank, ig_bank = S_ps[:, 2, :], S_ps[:, 3, :]

    def at(b, stage):
        s = b // B if isinstance(b, int) else stage
        return stages[s], b - B * s, s

    def loads(s):
        return 2 if "context" in stages[s] else 1

    def parts(p, which):
        return sb["parts"][:, p, which:which + 4:3, :]

    def source(w):
        return sb["cT"] if "context" in w else sb["xT"]

    with ExitStack() as ctx:
        def sem(what):
            return ctx.enter_context(nc.semaphore(f"{name}_{what}"))

        x_loaded = [sem("x_loaded0"), sem("x_loaded1")]
        xt_done, xt_ready = sem("xt_done"), sem("xt_ready")
        qk_done, q_ready, k_ready = sem("qk_done"), sem("q_ready"), sem("k_ready")
        rope_prod = sem("rope_prod")
        high_ready, rest_ready, middle_ready, split_ready = (
            sem("high_ready"), sem("rest_ready"), sem("middle_ready"), sem("split_ready"))
        stacked = [sem("stacked0"), sem("stacked1")]
        s_done, max_ready, sub_ready, exp_ready = sem("s_done"), sem("max_ready"), sem("sub_ready"), sem("exp_ready")
        pt_done, pt_ready, pv_done = sem("pt_done"), sem("pt_ready"), sem("pv_done")
        o_ready, ot_done, v_ready = sem("o_ready"), sem("ot_done"), sem("v_ready")
        rden_ready, on_ready = sem("rden_ready"), sem("on_ready")
        ont_done, ont_ready, out_done = sem("ont_done"), sem("ont_ready"), sem("out_done")
        xb_ready, y_ready, var_ready, rstd_ready, x_new = (
            sem("xb_ready"), sem("y_ready"), sem("var_ready"), sem("rstd_ready"), sem("x_new"))
        ve_ready = sem("ve_ready")
        if steps:
            xr_done, xr_ready, gates_done, gates_ready, terms, c_ready, x_kept = (
                sem(n) for n in ("xr_done", "xr_ready", "gates_done", "gates_ready", "terms", "c_ready", "x_kept"))
        block = ctx.enter_context(nc.Block())

        @block.sync
        def _(sp):
            def slot(i, p, half, stage):
                b, m = i + LEAD, i + LEAD + 1
                if has(m, N):
                    w, own, s = at(m, stage)
                    after(sp, xt_done, m - 1)
                    if s > 0:
                        sp.wait_ge(x_new, m - B + 1 if isinstance(m, int) else B * s)
                    sp.dma_start(xs[:, 1 - p, :], one(X, own)).then_inc(x_loaded[1 - p], 16)
                if later_loads and isinstance(i, int) and B - EDGE <= i < B + EDGE:
                    pieces, loaded = later_loads
                    for dst, src in pieces[i - (B - EDGE)]:
                        sp.dma_start(dst, src).then_inc(loaded, 16)
                if has(m, N) and "context" in at(m, stage)[0]:
                    after(sp, ot_done, i + 2)
                    sp.dma_start(sb["cT"][:, 1 - p, :], one(at(m, stage)[0]["context"], at(m, stage)[1]))\
                        .then_inc(x_loaded[1 - p], 16)
                if has(b, N):
                    for part_ready, terms_of in ((high_ready, TERMS_OF_PART[0]), (middle_ready, TERMS_OF_PART[1]),
                                                 (split_ready, TERMS_OF_PART[2])):
                        sp.wait_ge(part_ready, b + 1)
                        for t in terms_of:
                            q_part, k_part = TERM_PARTS[t]
                            sp.dma_start(sb["stacked"][t * HD:(t + 1) * HD, p, :, :, :],
                                         sb["parts"][:, p, q_part:3 + k_part + 1:3 + k_part - q_part, :])\
                                .then_inc(stacked[p], 16)
            slots(sp, slot, N)

        @block.tensor
        def _(pe):
            def scores(b, u, p, pairs, causal):
                pe.wait_ge(stacked[p], pairs * (16 * TERMS))
                after(pe, sub_ready, 2 * b + u - (0 if steps else 1))
                for g in range(2):
                    bank = S_ps[:, unit_bank[u] + g, :]
                    if causal is not None:
                        nc.tensor.matmul(bank, sb["identb"][:], causal[:].rearrange("p h k -> p (h k)"),
                                         start=True, stop=False, skip_group_check=True)
                    for e in range(4):
                        head = sb["stacked"][0:TERMS * HD, p, UH * u + 4 * g + e, :, :]
                        last = nc.tensor.matmul(bank[:, e * S:(e + 1) * S], head[:, 0, :], head[:, 1, :],
                                                start=causal is None, stop=True,
                                                skip_group_check=causal is not None)
                last.then_inc(s_done, 1)

            def transpose_probs(b, u):
                pe.wait_ge(exp_ready, 2 * b + u + 1)
                for g in range(2):
                    after(pe, pt_ready, 4 * b + 2 * u + g - 1)
                    for e in range(4):
                        last = nc.tensor.transpose(PT_ps[:, g, e * S:(e + 1) * S], sb["P"][:, u, 4 * g + e, :],
                                                   sb["ident"][:])
                    last.then_inc(pt_done, 1)

            def values(b, u, p):
                if u == 0:
                    pe.wait_ge(v_ready, b + 1)
                    after(pe, o_ready, b)
                for h in range(UH):
                    if h % 4 == 0:
                        pe.wait_ge(pt_ready, 4 * b + 2 * u + h // 4 + 1)
                    at = u * UH * (SLOT * (UH + 1)) + h * SLOT * UH
                    last = nc.tensor.matmul(O_ps[:, u * S:(u + 1) * S], sb["Vx"][:, p, at:at + S],
                                            sb["PT"][:, u, h, :], start=(h == 0), stop=(h == UH - 1))
                last.then_inc(pv_done, 1)

            def slot(i, p, half, stage):
                q = 1 - p
                b, n, r, z = i + LEAD, i + 1, i - 1, i - LAG

                def gates():
                    pe.wait_ge(xr_ready, z + 1)
                    pe.wait_ge(c_ready, z + 1)
                    for k, gate in enumerate((f_bank[:, 0:S], ig_bank[:, 0:S], ig_bank[:, S:2 * S])):
                        nc.tensor.matmul(gate, sb["r_w"][:, k * D:(k + 1) * D], sb["xr"][:], start=True, stop=False)
                        nc.tensor.matmul(gate, sb["r_u"][:, k * D:(k + 1) * D], sb["c2"][:], start=False, stop=True)
                    nc.tensor.matmul(ig_bank[:, 2 * S:3 * S], sb["xr"][:], sb["r_wo"][:], start=True, stop=True)\
                        .then_inc(gates_done, 1)

                if has(i, N):
                    scores(i, 1, p, half + 1, at(i, stage)[0].get("causal"))
                if has(b, N):
                    w, _, s = at(b, stage)
                    before = sum(B // 2 * loads(t) for t in range(s))
                    pe.wait_ge(x_loaded[p], (half + (2 - s * B // 2)) * (16 * loads(s)) + 16 * before)
                    after(pe, y_ready, i - 1)
                    after(pe, v_ready, i + 1)
                    nc.tensor.transpose(M_ps[:, 0:S], xs[:, p, :], sb["ident"][:]).then_inc(xt_done, 1)
                if has(r, N):
                    values(r, 1, q)
                if has(b, N):
                    pe.wait_ge(xt_ready, b + 1)
                    for m, which in enumerate(("q", "qr", "k", "kr") if "rope" in w else ("q", "k")):
                        src = sb["xT"] if which[0] == "q" else source(w)
                        last = nc.tensor.matmul(M_ps[:, m * S:(m + 1) * S], w[which][:], src[:, p, :],
                                                start=True, stop=True)
                    last.then_inc(qk_done, 1)
                if has(i, N):
                    transpose_probs(i, 0)
                if steps and has(z):
                    pe.wait_ge(x_new, z + 1)
                    after(pe, gates_ready, z)
                    nc.tensor.transpose(f_bank[:, S:2 * S], sb["YN"][:], sb["ident"][:]).then_inc(xr_done, 1)
                if has(n, N):
                    scores(n, 0, q, half + 1 + p, at(n, stage)[0].get("causal"))
                if not has(b, N):
                    if has(r, N) or has(n, N):
                        after(pe, y_ready, i - 1)
                elif "rope" in at(b, stage)[0]:
                    pe.wait_ge(rope_prod, at(b, stage)[1] + 1)
                else:
                    pe.wait_ge(q_ready, b + 1)
                    pe.wait_ge(k_ready, b + 1)
                if has(r, N) or has(n, N):
                    if has(r, N):
                        pe.wait_ge(o_ready, r + 1)
                        for t in range(2):
                            last = nc.tensor.transpose(M_ps[:, t * S:(t + 1) * S], sb["O"][:, t * S:(t + 1) * S],
                                                       sb["ident"][:])
                    if has(n, N):
                        last = nc.tensor.matmul(M_ps[:, 2 * S:3 * S], source(at(n, stage)[0])[:, q, :],
                                                at(n, stage)[0]["v"][:],
                                                start=True, stop=True)
                    last.then_inc(ot_done, 1)
                if steps and has(z):
                    gates()
                if has(i, N):
                    values(i, 0, p)
                if has(r, N):
                    pe.wait_ge(on_ready, r + 1)
                    if has(n, N):
                        pe.wait_ge(v_ready, n + 1)
                    nc.tensor.transpose(M_ps[:, 0:S], sb["ON"][:], sb["ident"][:]).then_inc(ont_done, 1)
                if has(i, N):
                    transpose_probs(i, 1)
                if has(r, N):
                    pe.wait_ge(ont_ready, r + 1)
                    nc.tensor.matmul(M_ps[:, S:2 * S], sb["ONT"][:], at(r, stage)[0]["o"][:], start=True, stop=True)\
                        .then_inc(out_done, 1)
            slots(pe, slot, N)

        @block.scalar
        def _(act):
            def exps(b, u):
                act.wait_ge(sub_ready, 2 * b + u + 1)
                nc.scalar.activation(sb["P"][:, u, :, :], sb["P"][:, u, :, :], ACT.Exp).then_inc(exp_ready, 1)

            def probs_out(b, u):
                for g in range(2):
                    act.wait_ge(pt_done, 4 * b + 2 * u + g + 1)
                    if g == 0:
                        after(act, pv_done, 2 * b + u - 1)
                    nc.scalar.activation(sb["PT"][:, u, 4 * g:4 * g + 4, :].rearrange("p h q -> p (h q)"),
                                         PT_ps[:, g, :], ACT.Copy).then_inc(pt_ready, 1)

            def slot(i, p, half, stage):
                b, n, r, z = i + LEAD, i + 1, i - 1, i - LAG
                if has(i, N):
                    exps(i, 0)
                if has(b, N):
                    act.wait_ge(xt_done, b + 1)
                    after(act, ot_done, b - 1)
                    nc.scalar.activation(sb["xT"][:, p, :], M_ps[:, 0:S], ACT.Copy).then_inc(xt_ready, 1)
                if has(b, N) and "rope" not in at(b, stage)[0]:
                    w = at(b, stage)[0]
                    act.wait_ge(qk_done, b + 1)
                    after(act, rest_ready, b)
                    after(act, high_ready, b)
                    if "key_mask" not in w:
                        nc.scalar.activation(sb["QK"][:, 1, :], M_ps[:, S:2 * S], ACT.Identity, bias=w["kb"][:])\
                            .then_inc(k_ready, 1)
                    nc.scalar.activation(sb["QK"][:, 0, :], M_ps[:, 0:S], ACT.Identity, bias=w["qb"][:],
                                         scale=w["qs"]).then_inc(q_ready, 1)
                if steps and has(z):
                    act.wait_ge(xr_done, z + 1)
                    after(act, gates_done, z)
                    nc.scalar.activation(sb["xr"][:], f_bank[:, S:2 * S], ACT.Copy).then_inc(xr_ready, 1)
                if has(i, N):
                    probs_out(i, 0)
                if has(b, N):
                    if "rope" not in at(b, stage)[0]:
                        act.wait_ge(k_ready, b + 1)
                    act.wait_ge(q_ready, b + 1)
                    after(act, s_done, 2 * i + 2)
                    nc.scalar.activation(parts(p, 0), sb["QK"][:], ACT.Copy).then_inc(high_ready, 1)
                if has(i, N):
                    exps(i, 1)
                if has(n, N):
                    act.wait_ge(ot_done, n + 1)
                    after(act, pv_done, 2 * i)
                    after(act, on_ready, r + 1)
                    nc.scalar.activation(sb["Vx"][:, 1 - p, :].rearrange("p (h c) -> p h c", h=H)[:, :, 0:HD],
                                         M_ps[:, 2 * S:3 * S].rearrange("p (h c) -> p h c", h=H), ACT.Copy)\
                        .then_inc(v_ready, 1)
                if has(b, N):
                    act.wait_ge(rest_ready, b + 1)
                    nc.scalar.activation(parts(p, 1), sb["rest"][:], ACT.Copy)\
                        .then_inc(middle_ready, 1)
                if steps and has(z):
                    act.wait_ge(gates_done, z + 1)
                    act.wait_ge(c_ready, z + 1)
                    for gate, bank, bias, scale in (
                            ("fg", f_bank[:, 0:S], "r_bf", 0.5), ("ig", ig_bank[:, 0:S], "r_bi", 0.5),
                            ("gg", ig_bank[:, S:2 * S], "r_bc", 1.0)):
                        nc.scalar.activation(sb[gate][:], bank, ACT.Tanh, bias=sb[bias][:], scale=scale)
                    nc.scalar.activation(one(own_outputs, z), ig_bank[:, 2 * S:3 * S], ACT.Copy)\
                        .then_inc(gates_ready, 1)
                if has(r, N):
                    act.wait_ge(ont_done, r + 1)
                    after(act, out_done, r)
                    nc.scalar.activation(sb["ONT"][:], M_ps[:, 0:S], ACT.Copy).then_inc(ont_ready, 1)
                if has(i, N):
                    probs_out(i, 1)
            slots(act, slot, N)

        @block.vector
        def _(dve):
            def shift(b, u):
                unit = S_ps[:, unit_bank[u]:unit_bank[u] + 2, :].rearrange("p a (h k) -> p (a h) k", k=S)
                dve.wait_ge(s_done, 2 * b + u + 1)
                after(dve, sub_ready, 2 * b + u)
                nc.vector.tensor_reduce(sb["mx"][:, 0:UH], unit, op=ALU.max, axis=AX.X).then_inc(max_ready, 1)
                dve.wait_ge(max_ready, 2 * b + u + 1)
                after(dve, pt_done, 4 * b + 2 * u - 2)
                nc.vector.tensor_tensor(sb["P"][:, u, :, :], unit, bc(sb["mx"][:, 0:UH], 2, S), ALU.subtract)\
                    .then_inc(sub_ready, 1)

            def slot(i, p, half, stage):
                b, n, r, z = i + LEAD, i + 1, i - 1, i - LAG
                if has(z, N):
                    dve.wait_ge(out_done, z + 1)
                    dve.wait_ge(xb_ready, z + 1)
                    after(dve, x_new, z)
                    nc.vector.tensor_tensor(sb["Y"][:], M_ps[:, S:2 * S], sb["XB"][:, p, :], ALU.add)\
                        .then_inc(y_ready, 1)
                    dve.wait_ge(y_ready, z + 1)
                    nc.vector.bn_stats(sb["bn"][:], sb["Y"][:])
                    nc.vector.drain()
                    nc.vector.bn_aggr(sb["mv"][:], sb["bn"][:]).then_inc(var_ready, 1)
                if has(i, N):
                    shift(i, 1)
                if has(z, N):
                    dve.wait_ge(rstd_ready, z + 1)
                    if steps:
                        after(dve, xr_done, z)
                        after(dve, x_kept, z)
                    nc.vector.tensor_scalar(sb["YN"][:] if steps else one(X, at(z, stage)[1]), sb["Y"][:],
                                            sb["mv"][:, 0:1], sb["rstd"][:], ALU.subtract, ALU.mult)\
                        .then_inc(x_new, 1)
                if has(r, N):
                    dve.wait_ge(pv_done, 2 * r + 2)
                    after(dve, ot_done, i + 1)
                    nc.vector.tensor_copy(sb["O"][:], O_ps[:, 0:2 * S]).then_inc(o_ready, 1)
                if has(b, N):
                    w, own, _ = at(b, stage)
                    if "rope" in w:
                        dve.wait_ge(qk_done, b + 1)
                        after(dve, q_ready, b)
                        nc.vector.tensor_tensor(sb["RP"][:], M_ps[:, 0:4 * S], w["rope"], ALU.mult)\
                            .then_inc(rope_prod, 1)
                    elif "key_mask" in w:
                        after(dve, rest_ready, b)
                        dve.wait_ge(q_ready, b + 1)
                        nc.vector.scalar_tensor_tensor(out=sb["QK"][:, 1, :], in0=M_ps[:, S:2 * S], scalar=w["kb"][:],
                                                       in1=one(w["key_mask"], own), op0=ALU.add, op1=ALU.mult)\
                            .then_inc(k_ready, 1)
                if has(r, N):
                    heads = M_ps[:, 0:2 * S].rearrange("p (h c) -> p h c", h=H)
                    dve.wait_ge(ot_done, i + 2)
                    nc.vector.reciprocal(sb["rden"][:], heads[:, :, HD]).then_inc(rden_ready, 1)
                    dve.wait_ge(rden_ready, r + 1)
                    after(dve, ont_done, r)
                    nc.vector.tensor_tensor(sb["ON"][:].rearrange("p (h c) -> p h c", h=H), heads[:, :, 0:HD],
                                            bc(sb["rden"][:], 2, HD), ALU.mult).then_inc(on_ready, 1)
                if has(n, N):
                    shift(n, 0)
                if steps and has(z):
                    dve.wait_ge(gates_ready, z + 1)
                    nc.vector.scalar_tensor_tensor(out=sb["ca"][:], in0=sb["fg"][:], scalar=1.0, in1=sb["c2"][:],
                                                   op0=ALU.add, op1=ALU.mult).then_inc(terms, 1)
                    nc.vector.scalar_tensor_tensor(out=sb["cb"][:], in0=sb["ig"][:], scalar=1.0, in1=sb["gg"][:],
                                                   op0=ALU.add, op1=ALU.mult).then_inc(terms, 1)
                    dve.wait_ge(terms, z * 2 + 2)
                    nc.vector.scalar_tensor_tensor(out=sb["c2"][:], in0=sb["ca"][:], scalar=0.5, in1=sb["cb"][:],
                                                   op0=ALU.mult, op1=ALU.add).then_inc(c_ready, 1)
            if steps:
                nc.vector.tensor_copy(sb["c2"][:], sb["r_c0"][:].to_broadcast([D, S])).then_inc(c_ready, 1)
            slots(dve, slot, N)
            if steps:
                dve.wait_ge(c_ready, B + 1)

        @block.gpsimd
        def _(pool):
            def slot(i, p, half, stage):
                b, r, z = i + LEAD, i - 1, i - LAG
                if has(z, N):
                    pool.wait_ge(var_ready, z + 1)
                    nc.gpsimd.tensor_tensor(sb["ve"][:], sb["mv"][:, 1:2], sb["eps"][:], ALU.add)\
                        .then_inc(ve_ready, 1)
                    pool.wait_ge(ve_ready, z + 1)
                    nc.gpsimd.tensor_tensor(sb["rstd"][:], sb["ve"][:], sb["mhalf"][:], ALU.pow)\
                        .then_inc(rstd_ready, 1)
                if has(r, N):
                    w, own, s = at(r, stage)
                    after(pool, y_ready, r - 1)
                    if s > 0:
                        pool.wait_ge(x_new, r - B + 1 if isinstance(r, int) else B * s)
                    nc.gpsimd.tensor_tensor(sb["XB"][:, 1 - p, :], one(X, own), w["bias"][:], ALU.add)\
                        .then_inc(xb_ready, 1)
                if has(b, N):
                    if "rope" in at(b, stage)[0]:
                        pool.wait_ge(rope_prod, at(b, stage)[1] + 1)
                        after(pool, high_ready, b)
                        products = sb["RP"][:].rearrange("p (n e s) -> p n e s", n=2, e=2)
                        nc.gpsimd.tensor_tensor(sb["QK"][:], products[:, :, 0, :], products[:, :, 1, :], ALU.add)\
                            .then_inc(q_ready, 1)
                    pool.wait_ge(high_ready, b + 1)
                    after(pool, split_ready, b)
                    after(pool, middle_ready, b)
                    nc.gpsimd.tensor_tensor(sb["rest"][:], sb["QK"][:], parts(p, 0), ALU.subtract)\
                        .then_inc(rest_ready, 1)
                    pool.wait_ge(middle_ready, b + 1)
                    if steps and has(z):
                        pool.wait_ge(x_new, z + 1)
                    nc.gpsimd.tensor_tensor(parts(p, 2), sb["rest"][:], parts(p, 1),
                                            ALU.subtract).then_inc(split_ready, 1)
                if steps and has(z):
                    if not has(b, N):
                        pool.wait_ge(x_new, z + 1)
                    nc.gpsimd.tensor_tensor(one(X, z), sb["YN"][:], sb["ones"][:], ALU.mult).then_inc(x_kept, 1)
            slots(pool, slot, N)
            if steps:
                pool.wait_ge(x_kept, B)


GELU_C = float(np.sqrt(2 / np.pi))


def counted(nc, ctx, prefix, **engines):
    sems, counts = {}, {}
    for engine, names in engines.items():
        sem = ctx.enter_context(nc.semaphore(f"{prefix}_{engine}_events"))
        for n, name in enumerate(names.split()):
            sems[name], counts[name] = sem, n + 1
    return sems, counts


def routed_ffn(nc, ps_all, sb, X, late_loaded):
    SB, SLOTS = 2048, NT * 128
    with ExitStack() as ctx:
        ev, nth = counted(
            nc, ctx, "ffn",
            tensor="spread_t0 spread_t1 spread_t2 spread_t3 biases gathered tables tokens_t masks_u selected_t qkv "
                   "dense_mask k0 k1 k2 k3 v0 v1 v2 v3 attended_t "
                   "projected x1n_t hidden0 hidden1 ff",
            scalar="biases_spread qkv_scaled weights_scaled biases_sb xsT u_ready selT_ready exps "
                   "attended_sb x1n_sb hidden_sb0 hidden_sb1 tanhs0 tanhs1",
            pool="weighed_late zeroed eq_masked key_mask rstd scaled_x later_biases rstd2",
            vector="weighed_early summed_early summed_late weights spread0 spread1 spread2 spread3 eq0 eq1 eq2 eq3 ge count_ge "
                   "count_eq rank factor select_padded select tokens_ready squares square_sum mean_square "
                   "cs_prod cs_ready wsel mask_prod mask_ready qkv_ready rot_sin rot_cos roped k0_prod "
                   "k0_sum k1_prod k1_sum k2_prod k2_sum k3_prod k3_sum masked row_max shifted row_sum row_inv "
                   "v0_prod v1_prod v2_prod v3_prod v_sum "
                   "attended x1 squares2 square_sum2 mean_square2 x1n cubed0 cubed1 inner0 inner1 gated0 "
                   "gated1 slot_w x2 spread_x2_0 spread_x2_1")
        norm = {n: ctx.enter_context(nc.semaphore(f"ffn_{n}"))
                for n in ("scattered", "y", "stats", "var", "rstd", "shift", "x_new")}

        block = ctx.enter_context(nc.Block())
        banks = [ps_all[:, n, :] for n in range(8)]
        scores4, upper4 = ps_all[:, 0:4, :], ps_all[:, 4:8, :]
        P, PT = (sb[n][:].rearrange("p u h k -> p (u h k)") for n in ("P", "PT"))
        big = sb["big"][:]
        wide = sb["QW"][:].rearrange("p u h k -> p (u h k)")
        hid, gate = wide[:, 0:NT * FF], wide[:, NT * FF:2 * NT * FF]
        repeat = wide.rearrange("p (j c) -> p j c", j=TOP)
        P3, PT3 = (t.rearrange("p (b d) -> p b d", b=B) for t in (P, PT))
        wt, sel, rank = sb["wt"], sb["sel"], sb["rank"]
        sel_flat = sel[:].rearrange("p b r -> p (b r)")
        qkv = sb["qkv"]
        qk = qkv[:, :, 0:2 * D].rearrange("p t (h c) -> p t h c", c=HD)
        roped = sb["roped"][:].rearrange("p t (h c) -> p t h c", c=HD)
        rot = sb["rot"][:].rearrange("p t (h c) -> p t h c", c=HD)
        keys = big[:, 0:TOP * SLOTS].rearrange("p (j c) -> p j c", c=SLOTS)
        att = sb["att"]
        X3 = X[:]

        def padded(t, more=0):
            return big[:, SB + t * NB * 128:SB + (t + 1) * NB * 128 + more]

        PARTS = [slice(j, min(j + 4, KC)) for j in range(0, KC, 4)]
        HALVES = slice(0, NT * FF // 2), slice(NT * FF // 2, NT * FF)
        FOURS = [slice(c, c + 4) for c in range(0, B, 4)]
        EARLIER, LATER = slice(0, B // 2), slice(B // 2, B)
        BY_VECTOR = 2

        @block.tensor
        def _(pe):
            for c in range(4):
                pe.wait_ge(ev[f"spread{c}"], nth[f"spread{c}"])
                for b in range(4 * c, 4 * c + 4):
                    last = nc.tensor.transpose(banks[c][:, (b % 4) * S:(b % 4 + 1) * S],
                                               big[:, b * S:(b + 1) * S], sb["ident"][:])
                last.then_inc(ev[f"spread_t{c}"], 1)
            pe.wait_ge(late_loaded, 16 * LATE_LOADS)
            pe.wait_ge(ev["biases_spread"], nth["biases_spread"])
            for c in range(PAIRS):
                nc.tensor.matmul(banks[7][:, 0:D], sb["spread"][:, c * D:(c + 1) * D], sb["d_o"][:, c * D:(c + 1) * D],
                                 start=(c == 0), stop=(c == PAIRS - 1))
            nc.tensor.matmul(banks[7][:, D:2 * D], sb["fT"][:, 0:D], sb["e_o"][:], start=True, stop=True)\
                .then_inc(ev["biases"], 1)
            pe.wait_ge(ev["select"], nth["select"])
            pe.wait_ge(ev["select_padded"], nth["select_padded"])
            pe.wait_ge(ev["biases_sb"], nth["biases_sb"])
            for t in range(NT):
                for e in range(NB):
                    last = nc.tensor.matmul(banks[7][:, t * 128:(t + 1) * 128], padded(t)[:, e * 128:(e + 1) * 128],
                                            X3[:, NB * t + e, :], start=(e == 0), stop=(e == NB - 1))
            last.then_inc(ev["gathered"], 1)
            pe.wait_ge(late_loaded, 16 * LATE_LOADS)
            pe.wait_ge(ev["weights_scaled"], nth["weights_scaled"])
            for t in range(NT):
                last = nc.tensor.matmul(banks[5][:, t * 64:(t + 1) * 64], sel_flat[:, t * 128:(t + 1) * 128],
                                        sb["cs_table"][:].rearrange("p m c -> p (m c)"), start=True, stop=True)
            last.then_inc(ev["tables"], 1)
            pe.wait_ge(ev["tokens_ready"], nth["tokens_ready"])
            for t in range(NT):
                last = nc.tensor.transpose(banks[6][:, t * 128:(t + 1) * 128], sb["tokens"][:, t, :], sb["ident"][:])
            last.then_inc(ev["tokens_t"], 1)
            for m in range(MB):
                end = B if m == MB - 1 else m + 1
                last = nc.tensor.matmul(banks[4][:, m * TOP:end * TOP], sb["amask"][:, m, :],
                                        sel_flat[:, m * TOP:end * TOP], start=True, stop=True)
            last.then_inc(ev["masks_u"], 1)
            pe.wait_ge(ev["ge"], nth["ge"])
            for t in range(NT):
                last = nc.tensor.transpose(banks[0][:, t * 128:(t + 1) * 128], sel_flat[:, t * 128:(t + 1) * 128],
                                           sb["ident"][:])
            last.then_inc(ev["selected_t"], 1)
            pe.wait_ge(ev["xsT"], nth["xsT"])
            for t in range(NT):
                tile = sb["xsT"][:, t * 128:(t + 1) * 128]
                nc.tensor.matmul(banks[1 + t][:, 0:3 * D], tile, sb["c_qkv"][:], start=True, stop=True)
                last = nc.tensor.matmul(banks[3][:, t:t + 1], tile, sb["c_rw"][:], start=True, stop=True)
            last.then_inc(ev["qkv"], 1)
            pe.wait_ge(ev["u_ready"], nth["u_ready"])
            pe.wait_ge(ev["xsT"], nth["xsT"])
            for t in range(NT):
                last = nc.tensor.matmul(banks[6][:, t * 128:(t + 1) * 128], sb["umask"][:, t * 128:(t + 1) * 128],
                                        sel_flat[:, t * 128:(t + 1) * 128], start=True, stop=True)
            last.then_inc(ev["dense_mask"], 1)
            pe.wait_ge(ev["roped"], nth["roped"])
            pe.wait_ge(ev["selT_ready"], nth["selT_ready"])
            pe.wait_ge(ev["tokens_ready"], nth["tokens_ready"])
            pe.wait_ge(ev["mask_prod"], nth["mask_prod"])
            pe.wait_ge(ev["wsel"], nth["wsel"])
            pe.wait_ge(ev["cs_prod"], nth["cs_prod"])
            for what, source in (("k", sb["roped"][:, :, D:2 * D]), ("v", qkv[:, :, 2 * D:3 * D])):
                for part, js in enumerate(PARTS):
                    if what == "v":
                        pe.wait_ge(ev[f"k{part}_prod"], nth[f"k{part}_prod"])
                    for j in range(js.start, js.stop):
                        last = nc.tensor.matmul(banks[j // 2][:, (j % 2) * SLOTS:(j % 2 + 1) * SLOTS]
                                                .rearrange("p (t c) -> p t c", t=NT),
                                                repeat[:, j, :], source, start=True, stop=True)
                    last.then_inc(ev[f"{what}{part}"], 1)
            pe.wait_ge(ev["attended"], nth["attended"])
            for t in range(NT):
                last = nc.tensor.transpose(banks[0][:, t * 128:(t + 1) * 128], sb["attended"][:, t * D:(t + 1) * D],
                                           sb["ident"][:])
            last.then_inc(ev["attended_t"], 1)
            pe.wait_ge(ev["attended_sb"], nth["attended_sb"])
            for t in range(NT):
                last = nc.tensor.matmul(banks[1][:, t * D:(t + 1) * D], sb["fT"][:, t * 128:(t + 1) * 128],
                                        sb["c_o"][:], start=True, stop=True)
            last.then_inc(ev["projected"], 1)
            pe.wait_ge(ev["x1n"], nth["x1n"])
            for t in range(NT):
                last = nc.tensor.transpose(banks[0][:, t * 128:(t + 1) * 128], sb["attended"][:, t * D:(t + 1) * D],
                                           sb["ident"][:])
            last.then_inc(ev["x1n_t"], 1)
            pe.wait_ge(ev["x1n_sb"], nth["x1n_sb"])
            for half in range(2):
                for c in range(2 * half, 2 * half + 2):
                    last = nc.tensor.matmul(banks[2 + half][:, (c % 2) * SLOTS:(c % 2 + 1) * SLOTS],
                                            sb["c_w1"][:, c * 128:(c + 1) * 128], sb["x1nT"][:], start=True, stop=True)
                last.then_inc(ev[f"hidden{half}"], 1)
            for half in range(2):
                pe.wait_ge(ev[f"gated{half}"], nth[f"gated{half}"])
                for t in range(NT):
                    for c in range(2 * half, 2 * half + 2):
                        last = nc.tensor.matmul(banks[t][:, 0:D],
                                                gate[:, c * SLOTS + t * 128:c * SLOTS + (t + 1) * 128],
                                                sb["c_w2"][:, c * D:(c + 1) * D], start=(c == 0),
                                                stop=(c == FF // 128 - 1))
            last.then_inc(ev["ff"], 1)
            for t in range(NT):
                pe.wait_ge(ev[f"spread_x2_{t}"], nth[f"spread_x2_{t}"])
                for g in range(2):
                    nc.tensor.matmul(banks[4 + 2 * t + g], sb["selT"][:, t * 128:(t + 1) * 128],
                                     big[:, (2 * t + g) * 512:(2 * t + g + 1) * 512], start=True, stop=True)\
                        .then_inc(norm["scattered"], 1)

        @block.scalar
        def _(act):
            def out_of(event, bank, dst, ready):
                act.wait_ge(ev[event], nth[event])
                nc.scalar.activation(dst, bank, ACT.Copy).then_inc(ev[ready], 1)

            nc.scalar.activation(sb["d_qs"][:], sb["d_as"][:], ACT.Copy, scale=float(HW) ** -0.5)
            for c in range(PAIRS):
                nc.scalar.activation(sb["spread"][:, c * D:(c + 1) * D], sb["ones"][:], ACT.Identity,
                                     scale=sb["d_vb"][:, c:c + 1])
            nc.scalar.activation(sb["fT"][:, 0:D], sb["ones"][:], ACT.Identity, scale=sb["e_bv"][:])\
                .then_inc(ev["biases_spread"], 1)
            act.wait_ge(late_loaded, 16 * LATE_LOADS)
            nc.scalar.activation(sb["c_qkv"][:, 0:D], sb["c_qkv"][:, 0:D], ACT.Copy, scale=float(HD) ** -0.5)\
                .then_inc(ev["qkv_scaled"], 1)
            act.wait_ge(ev["qkv_scaled"], nth["qkv_scaled"])
            nc.scalar.activation(sb["c_qkv"][:], sb["c_qkv"][:], ACT.Identity, scale=sb["c_ln1"][:])
            nc.scalar.activation(sb["c_w1"][:], sb["c_w1"][:], ACT.Identity, scale=sb["c_ln2"][:])
            nc.scalar.activation(sb["c_w2"][:], sb["c_w2"][:], ACT.Copy, scale=0.5)
            for dst, src, scale in (("r_u", "r_u", 0.5), ("r_uo", "r_uo", 0.5), ("r_bf", "r_bf0", 0.5),
                                    ("r_bi", "r_bi0", 0.5), ("r_c0", "r_c00", 2.0)):
                last = nc.scalar.activation(sb[dst][:], sb[src][:], ACT.Copy, scale=scale)
            last.then_inc(ev["weights_scaled"], 1)
            act.wait_ge(ev["biases"], nth["biases"])
            nc.scalar.activation(sb["d_bias"][:], banks[7][:, 0:D], ACT.Copy)
            nc.scalar.activation(sb["e_bias"][:], banks[7][:, D:2 * D], ACT.Copy).then_inc(ev["biases_sb"], 1)
            out_of("tokens_t", banks[6][:, 0:SLOTS], sb["xsT"][:], "xsT")
            out_of("masks_u", banks[4][:, 0:SLOTS], sb["umask"][:], "u_ready")
            out_of("selected_t", banks[0][:, 0:SLOTS], sb["selT"][:], "selT_ready")
            act.wait_ge(ev["shifted"], nth["shifted"])
            nc.scalar.activation(att[:], att[:], ACT.Exp).then_inc(ev["exps"], 1)
            out_of("attended_t", banks[0][:, 0:SLOTS], sb["fT"][:], "attended_sb")
            out_of("x1n_t", banks[0][:, 0:SLOTS], sb["x1nT"][:], "x1n_sb")
            for half, part in enumerate(HALVES):
                act.wait_ge(ev[f"hidden{half}"], nth[f"hidden{half}"])
                nc.scalar.activation(hid[:, part], banks[2 + half], ACT.Copy).then_inc(ev[f"hidden_sb{half}"], 1)
            for half, part in enumerate(HALVES):
                act.wait_ge(ev[f"inner{half}"], nth[f"inner{half}"])
                nc.scalar.activation(gate[:, part], gate[:, part], ACT.Tanh, scale=GELU_C)\
                    .then_inc(ev[f"tanhs{half}"], 1)
            for c in range(BY_VECTOR):
                act.wait_ge(norm["shift"], c + 1)
                for b in range(4 * c, 4 * c + 4):
                    nc.scalar.activation(X3[:, b, :], PT3[:, b, :], ACT.Identity, bias=sb["nshift"][:, b:b + 1],
                                         scale=sb["ln16"][:, b:b + 1])

        @block.gpsimd
        def _(pool):
            nc.gpsimd.tensor_tensor(P3[:, LATER, :], X3[:, LATER, :], bc(sb["c_rw_row"][:], 1, B // 2), ALU.mult)\
                .then_inc(ev["weighed_late"], 1)
            nc.gpsimd.memset(big[:, SB:2 * SB], 0.0).then_inc(ev["zeroed"], 1)
            for c in range(4):
                pool.wait_ge(ev[f"eq{c}"], nth[f"eq{c}"])
                last = nc.gpsimd.tensor_tensor(PT3[:, FOURS[c], :], PT3[:, FOURS[c], :], bc(sb["upper"][:], 1, 4),
                                               ALU.mult)
            last.then_inc(ev["eq_masked"], 1)
            pool.wait_ge(late_loaded, 16 * LATE_LOADS)
            key_mask = sb["kmask"][:].rearrange("p b k -> p (b k)")
            nc.gpsimd.tensor_copy(key_mask, key_mask.bitcast(I32)).then_inc(ev["key_mask"], 1)
            pool.wait_ge(ev["mean_square"], nth["mean_square"])
            nc.gpsimd.tensor_tensor(sb["rms"][:], sb["ss"][:], sb["mhalf"][:].to_broadcast([128, NT]), ALU.pow)\
                .then_inc(ev["rstd"], 1)
            pool.wait_ge(ev["factor"], nth["factor"])
            pool.wait_ge(ev["count_ge"], nth["count_ge"])
            nc.gpsimd.tensor_tensor(P3, X3, bc(sb["factor"][:], 2, D), ALU.mult).then_inc(ev["scaled_x"], 1)
            pool.wait_ge(ev["biases_sb"], nth["biases_sb"])
            nc.gpsimd.tensor_tensor(sb["d_bias"][:], sb["d_bias"][:], sb["d_bo"][:], ALU.add)
            nc.gpsimd.tensor_tensor(sb["e_bias"][:], sb["e_bias"][:], sb["e_bp"][:], ALU.add)
            nc.gpsimd.tensor_tensor(sb["d_qbs"][:], sb["d_qb"][:], sb["d_qs"][:], ALU.mult).then_inc(ev["later_biases"], 1)
            pool.wait_ge(ev["mean_square2"], nth["mean_square2"])
            nc.gpsimd.tensor_tensor(sb["rms2"][:], sb["ss2"][:], sb["mhalf"][:].to_broadcast([128, NT]), ALU.pow)\
                .then_inc(ev["rstd2"], 1)
            for c in range(4):
                pool.wait_ge(norm["var"], c + 1)
                nc.gpsimd.tensor_tensor(sb["ln16"][:, FOURS[c]], sb["ve16"][:, FOURS[c]],
                                        sb["mhalf"][:].to_broadcast([128, 4]), ALU.pow).then_inc(norm["rstd"], 1)

        @block.vector
        def _(dve):
            def tt(out, a, b_, op, done):
                nc.vector.tensor_tensor(out, a, b_, op).then_inc(ev[done], 1)

            def total(out, in_, done, op=ALU.add):
                nc.vector.tensor_reduce(out, in_, op=op, axis=AX.X).then_inc(ev[done], 1)

            tt(P3[:, EARLIER, :], X3[:, EARLIER, :], bc(sb["c_rw_row"][:], 1, B // 2), ALU.mult, "weighed_early")
            dve.wait_ge(ev["weighed_early"], nth["weighed_early"])
            total(wt[:, EARLIER], P3[:, EARLIER, :], "summed_early")
            dve.wait_ge(ev["weighed_late"], nth["weighed_late"])
            total(wt[:, LATER], P3[:, LATER, :], "summed_late")
            dve.wait_ge(ev["summed_early"], nth["summed_early"])
            dve.wait_ge(ev["summed_late"], nth["summed_late"])
            nc.vector.tensor_scalar(wt[:], wt[:], sb["c_rb"][:], None, ALU.add).then_inc(ev["weights"], 1)
            dve.wait_ge(ev["weights"], nth["weights"])
            for c in range(4):
                nc.vector.tensor_copy(big[:, 4 * c * S:4 * (c + 1) * S].rearrange("p (b t) -> p b t", b=4),
                                      bc(wt[:, FOURS[c]], 2, S)).then_inc(ev[f"spread{c}"], 1)
            others = scores4.rearrange("p a (b j) -> p (a b) j", j=S)
            for c in range(4):
                dve.wait_ge(ev[f"spread_t{c}"], nth[f"spread_t{c}"])
                tt(PT3[:, FOURS[c], :], others[:, FOURS[c], :], bc(wt[:, FOURS[c]], 2, S), ALU.is_equal, f"eq{c}")
            tt(P3, others, bc(wt[:], 2, S), ALU.is_ge, "ge")
            dve.wait_ge(ev["ge"], nth["ge"])
            total(sb["count_ge"][:], P3, "count_ge")
            dve.wait_ge(ev["eq_masked"], nth["eq_masked"])
            total(sb["count_eq"][:], PT3, "count_eq")
            dve.wait_ge(ev["count_eq"], nth["count_eq"])
            dve.wait_ge(ev["count_ge"], nth["count_ge"])
            tt(rank[:], sb["count_ge"][:], sb["count_eq"][:], ALU.subtract, "rank")
            nc.vector.tensor_scalar(sb["factor"][:], sb["count_ge"][:], KC + 0.5, 1.0, ALU.is_gt, ALU.add)\
                .then_inc(ev["factor"], 1)
            dve.wait_ge(ev["rank"], nth["rank"])
            dve.wait_ge(ev["zeroed"], nth["zeroed"])
            for t in range(NT):
                own = slice(t * NB, (t + 1) * NB)
                last = nc.vector.tensor_tensor(padded(t, 128).rearrange("p (b w) -> p b w", w=128 + TOP)[:, :, 0:TOP],
                                               bc(rank[:, own], 2, TOP), bc(sb["iota"][:], 1, NB), ALU.is_equal)
            last.then_inc(ev["select_padded"], 1)
            tt(sel[:], bc(rank[:], 2, TOP), bc(sb["iota"][:], 1, B), ALU.is_equal, "select")
            dve.wait_ge(ev["gathered"], nth["gathered"])
            tokens = sb["tokens"]
            nc.vector.tensor_copy(tokens[:].rearrange("p t d -> p (t d)"), banks[7][:, 0:SLOTS])\
                .then_inc(ev["tokens_ready"], 1)
            dve.wait_ge(ev["tokens_ready"], nth["tokens_ready"])
            tt(sb["sq"][:], tokens[:], tokens[:], ALU.mult, "squares")
            dve.wait_ge(ev["squares"], nth["squares"])
            total(sb["ss"][:], sb["sq"][:], "square_sum")
            dve.wait_ge(ev["square_sum"], nth["square_sum"])
            nc.vector.tensor_scalar(sb["ss"][:], sb["ss"][:], 1.0 / D, RMS_EPS, ALU.mult, ALU.add)\
                .then_inc(ev["mean_square"], 1)
            dve.wait_ge(ev["tables"], nth["tables"])
            prod = sb["cs_prod"]
            for t in range(NT):
                last = nc.vector.tensor_tensor(prod[:, t, :, :],
                                               banks[5][:, t * 64:(t + 1) * 64].rearrange("p (m c) -> p m c", m=MB),
                                               bc(sb["mbatch"][:, t, :], 2, 16), ALU.mult)
            last.then_inc(ev["cs_prod"], 1)
            dve.wait_ge(ev["cs_prod"], nth["cs_prod"])
            total(sb["cs"][:], prod[:].rearrange("p t m c -> p t c m"), "cs_ready")
            dve.wait_ge(ev["qkv"], nth["qkv"])
            nc.vector.tensor_scalar(sb["wsel"][:], banks[3][:, 0:NT], sb["c_rb"][:], sb["valid"][:],
                                    ALU.add, ALU.mult).then_inc(ev["wsel"], 1)
            dve.wait_ge(ev["dense_mask"], nth["dense_mask"])
            tt(sb["mprod"][:].rearrange("p t b r -> p (t b) r"),
               banks[6][:, 0:SLOTS].rearrange("p (x r) -> p x r", r=TOP),
               bc(sb["blocks2"][:].rearrange("p t b -> p (t b)"), 2, TOP), ALU.mult, "mask_prod")
            dve.wait_ge(ev["mask_prod"], nth["mask_prod"])
            total(sb["msel"][:], sb["mprod"][:].rearrange("p t b r -> p t r b"), "mask_ready")
            dve.wait_ge(ev["rstd"], nth["rstd"])
            tt(qkv[:], ps_all[:, 1:3, 0:3 * D], bc(sb["rms"][:], 2, 3 * D), ALU.mult, "qkv_ready")
            dve.wait_ge(ev["qkv_ready"], nth["qkv_ready"])
            dve.wait_ge(ev["cs_ready"], nth["cs_ready"])
            HH = HD // 2
            for t in range(NT):
                last = nc.vector.tensor_tensor(rot[:, t, :, 0:HH], qk[:, t, :, HH:HD],
                                               bc(sb["cs"][:, t, HD:HD + HH], 1, 2 * H), ALU.mult)
                last = nc.vector.tensor_tensor(rot[:, t, :, HH:HD], qk[:, t, :, 0:HH],
                                               bc(sb["cs"][:, t, HD + HH:2 * HD], 1, 2 * H), ALU.mult)
            last.then_inc(ev["rot_sin"], 1)
            for t in range(NT):
                last = nc.vector.tensor_tensor(roped[:, t, :, :], qk[:, t, :, :],
                                               bc(sb["cs"][:, t, 0:HD], 1, 2 * H), ALU.mult)
            last.then_inc(ev["rot_cos"], 1)
            dve.wait_ge(ev["rot_sin"], nth["rot_sin"])
            dve.wait_ge(ev["rot_cos"], nth["rot_cos"])
            tt(sb["roped"][:], sb["roped"][:], sb["rot"][:], ALU.add, "roped")
            dve.wait_ge(ev["roped"], nth["roped"])
            for part, js in enumerate(PARTS):
                n, src = js.stop - js.start, ps_all[:, 2 * part:2 * part + 2, :]
                dve.wait_ge(ev[f"k{part}"], nth[f"k{part}"])
                flat = src.rearrange("p a (j t c) -> p (a j) t c", j=2, t=NT)
                for t in range(NT):
                    last = nc.vector.tensor_tensor(keys[:, js, t * D:(t + 1) * D], flat[:, 0:n, t, :],
                                                   bc(sb["roped"][:, t, 0:D], 1, n), ALU.mult)
                last.then_inc(ev[f"k{part}_prod"], 1)
                dve.wait_ge(ev[f"k{part}_prod"], nth[f"k{part}_prod"])
                total(att[:, :, js].rearrange("p x j -> p j x"),
                      keys[:, js, :].rearrange("p j (x c) -> p j x c", c=HD), f"k{part}_sum")
            for part in range(len(PARTS)):
                dve.wait_ge(ev[f"k{part}_sum"], nth[f"k{part}_sum"])
            dve.wait_ge(ev["mask_ready"], nth["mask_ready"])
            for t in range(NT):
                rows = att[:, t * H:(t + 1) * H, :]
                last = nc.vector.tensor_tensor(rows, rows, bc(sb["msel"][:, t, 0:KC], 1, H), ALU.add)
            last.then_inc(ev["masked"], 1)
            dve.wait_ge(ev["masked"], nth["masked"])
            total(sb["rmax"][:], att[:], "row_max", ALU.max)
            dve.wait_ge(ev["row_max"], nth["row_max"])
            tt(att[:], att[:], bc(sb["rmax"][:], 2, KC), ALU.subtract, "shifted")
            dve.wait_ge(ev["exps"], nth["exps"])
            total(sb["rsum32"][:], att[:], "row_sum")
            dve.wait_ge(ev["row_sum"], nth["row_sum"])
            nc.vector.reciprocal(sb["rmax"][:], sb["rsum32"][:]).then_inc(ev["row_inv"], 1)
            for part, js in enumerate(PARTS):
                n, src = js.stop - js.start, ps_all[:, 2 * part:2 * part + 2, :]
                dve.wait_ge(ev[f"v{part}"], nth[f"v{part}"])
                nc.vector.tensor_tensor(keys[:, js, :].rearrange("p j (x c) -> p j x c", c=HD),
                                        src.rearrange("p a (j x c) -> p (a j) x c", j=2, c=HD)[:, 0:n, :, :],
                                        bc(att[:, :, js].rearrange("p x j -> p j x"), 3, HD), ALU.mult)\
                    .then_inc(ev[f"v{part}_prod"], 1)
            for part in range(len(PARTS)):
                dve.wait_ge(ev[f"v{part}_prod"], nth[f"v{part}_prod"])
            total(sb["vsum"][:], keys[:, 0:KC, :].rearrange("p j c -> p c j"), "v_sum")
            dve.wait_ge(ev["v_sum"], nth["v_sum"])
            dve.wait_ge(ev["row_inv"], nth["row_inv"])
            tt(sb["attended"][:].rearrange("p (x c) -> p x c", c=HD), sb["vsum"][:].rearrange("p (x c) -> p x c", c=HD),
               bc(sb["rmax"][:], 2, HD), ALU.mult, "attended")
            dve.wait_ge(ev["projected"], nth["projected"])
            x1 = sb["x1"]
            tt(x1[:].rearrange("p t d -> p (t d)"), banks[1][:, 0:SLOTS],
               tokens[:].rearrange("p t d -> p (t d)"), ALU.add, "x1")
            dve.wait_ge(ev["x1"], nth["x1"])
            tt(sb["sq"][:], x1[:], x1[:], ALU.mult, "squares2")
            dve.wait_ge(ev["squares2"], nth["squares2"])
            total(sb["ss2"][:], sb["sq"][:], "square_sum2")
            dve.wait_ge(ev["square_sum2"], nth["square_sum2"])
            nc.vector.tensor_scalar(sb["ss2"][:], sb["ss2"][:], 1.0 / D, RMS_EPS, ALU.mult, ALU.add)\
                .then_inc(ev["mean_square2"], 1)
            dve.wait_ge(ev["rstd2"], nth["rstd2"])
            dve.wait_ge(ev["attended_t"], nth["attended_t"])
            tt(sb["attended"][:].rearrange("p (t d) -> p t d", t=NT), x1[:], bc(sb["rms2"][:], 2, D), ALU.mult, "x1n")
            for half, part in enumerate(HALVES):
                h, g = hid[:, part], gate[:, part]
                dve.wait_ge(ev[f"hidden_sb{half}"], nth[f"hidden_sb{half}"])
                nc.vector.scalar_tensor_tensor(out=g, in0=h, scalar=0.044715, in1=h,
                                               op0=ALU.mult, op1=ALU.mult).then_inc(ev[f"cubed{half}"], 1)
            for half, part in enumerate(HALVES):
                h, g = hid[:, part], gate[:, part]
                dve.wait_ge(ev[f"cubed{half}"], nth[f"cubed{half}"])
                nc.vector.scalar_tensor_tensor(out=g, in0=g, scalar=1.0, in1=h,
                                               op0=ALU.add, op1=ALU.mult).then_inc(ev[f"inner{half}"], 1)
            for half, part in enumerate(HALVES):
                h, g = hid[:, part], gate[:, part]
                dve.wait_ge(ev[f"tanhs{half}"], nth[f"tanhs{half}"])
                nc.vector.scalar_tensor_tensor(out=g, in0=g, scalar=1.0, in1=h,
                                               op0=ALU.add, op1=ALU.mult).then_inc(ev[f"gated{half}"], 1)
            for t in range(NT):
                last = nc.vector.tensor_scalar(sb["slot_w"][:, t, :], sb["blocks2"][:, t, :], sb["wsel"][:, t:t + 1],
                                               None, ALU.mult)
            last.then_inc(ev["slot_w"], 1)
            dve.wait_ge(ev["ff"], nth["ff"])
            tt(x1[:], ps_all[:, 0:NT, 0:D], x1[:], ALU.add, "x2")
            dve.wait_ge(ev["x2"], nth["x2"])
            dve.wait_ge(ev["slot_w"], nth["slot_w"])
            spread = big[:, 0:SB].rearrange("p (t b d) -> p t b d", t=NT, b=NB)
            for t in range(NT):
                tt(spread[:, t, :, :], bc(x1[:, t, :], 1, NB), bc(sb["slot_w"][:, t, :], 2, D), ALU.mult,
                   f"spread_x2_{t}")
            dve.wait_ge(ev["scaled_x"], nth["scaled_x"])
            dve.wait_ge(ev["count_eq"], nth["count_eq"])

            def shift(c):
                dve.wait_ge(norm["rstd"], c + 1)
                nc.vector.scalar_tensor_tensor(out=sb["nshift"][:, FOURS[c]], in0=sb["mv16"][:, FOURS[c], 0],
                                               scalar=-1.0, in1=sb["ln16"][:, FOURS[c]], op0=ALU.mult,
                                               op1=ALU.mult).then_inc(norm["shift"], 1)

            for c in range(4):
                dve.wait_ge(norm["scattered"], c + 1)
                nc.vector.tensor_tensor(PT3[:, FOURS[c], :], banks[4 + c].rearrange("p (b d) -> p b d", d=D),
                                        P3[:, FOURS[c], :], ALU.add).then_inc(norm["y"], 1)
                dve.wait_ge(norm["y"], c + 1)
                for b in range(4 * c, 4 * c + 4):
                    nc.vector.bn_stats(sb["bn16"][:, b, :], PT3[:, b, :])
                nc.vector.drain()
                for b in range(4 * c, 4 * c + 4):
                    last = nc.vector.bn_aggr(sb["mv16"][:, b, :], sb["bn16"][:, b, :])
                last.then_inc(norm["stats"], 1)
                dve.wait_ge(norm["stats"], c + 1)
                nc.vector.tensor_scalar(sb["ve16"][:, FOURS[c]], sb["mv16"][:, FOURS[c], 1], LN_EPS, None, ALU.add)\
                    .then_inc(norm["var"], 1)
                if 0 < c <= BY_VECTOR:
                    shift(c - 1)
            for c in range(BY_VECTOR, 4):
                dve.wait_ge(norm["rstd"], c + 1)
                for b in range(4 * c, 4 * c + 4):
                    nc.vector.tensor_scalar(X3[:, b, :], PT3[:, b, :], sb["mv16"][:, b, 0:1], sb["ln16"][:, b:b + 1],
                                            ALU.subtract, ALU.mult).then_inc(norm["x_new"], 1)
            dve.wait_ge(norm["x_new"], 4 * (4 - BY_VECTOR))


def wide_head_attention(nc, ps, sb, X, xs, late_loaded):
    S_ps, PT_ps, O_ps, M_ps = ps
    bank_a, bank_b, bank_c = S_ps[:, 2, :], S_ps[:, 3, :], M_ps
    with ExitStack() as ctx:
        def sem(what):
            return ctx.enter_context(nc.semaphore(f"wide_{what}"))

        x_loaded = [sem("x_loaded0"), sem("x_loaded1")]
        xt_done, xt_ready = sem("xt_done"), sem("xt_ready")
        q_done, q_ready, k_done, k_ready = sem("q_done"), sem("q_ready"), sem("k_done"), sem("k_ready")
        v_done, v_ready = sem("v_done"), sem("v_ready")
        s_done, max_ready, sub_ready, exp_ready = sem("s_done"), sem("max_ready"), sem("sub_ready"), sem("exp_ready")
        sum_ready, inv_ready, p_ready = sem("sum_ready"), sem("inv_ready"), sem("p_ready")
        pt_done, pt_ready, pv_done, o_ready = sem("pt_done"), sem("pt_ready"), sem("pv_done"), sem("o_ready")
        out_done, xb_ready, y_ready = sem("out_done"), sem("xb_ready"), sem("y_ready")
        var1_ready, rstd1_ready, yn_ready, y2_ready = (
            sem("var1_ready"), sem("rstd1_ready"), sem("yn_ready"), sem("y2_ready"))
        var2_ready, rstd2_ready = sem("var2_ready"), sem("rstd2_ready")
        x_new, pool_step = sem("x_new"), sem("pool_step")
        block = ctx.enter_context(nc.Block())
        HP = PAIRS // 2
        PW = 3 * HW

        @block.sync
        def _(sp):
            def slot(i, p, half, stage):
                b = i + LEAD
                if has(b):
                    after(sp, xt_done, b - 1)
                    sp.dma_start(xs[:, p, :], one(X, b)).then_inc(x_loaded[p], 16)
            slots(sp, slot)

        @block.tensor
        def _(pe):
            pe.wait_ge(late_loaded, 16 * LATE_LOADS)
            def scores(b, u, p):
                pe.wait_ge(q_ready, 2 * b + u + 1)
                pe.wait_ge(k_ready, 2 * b + u + 1)
                after(pe, sub_ready, 2 * b + u)
                for e in range(HP):
                    pair = HP * u + e
                    last = nc.tensor.matmul(S_ps[:, e // 2, (e % 2) * 2 * S:(e % 2 + 1) * 2 * S],
                                            sb["QW"][:, p, pair, :],
                                            sb["KW"][:, p, pair, :, :].rearrange("p e k -> p (e k)"),
                                            start=True, stop=True)
                last.then_inc(s_done, 1)

            def transpose_probs(b, u):
                pe.wait_ge(p_ready, 2 * b + u + 1)
                after(pe, pt_ready, 2 * b + u)
                for h in range(UH):
                    last = nc.tensor.transpose(PT_ps[:, h // 4, (h % 4) * S:(h % 4 + 1) * S],
                                               sb["P"][:, u, h, :], sb["ident"][:])
                last.then_inc(pt_done, 1)

            def values(b, u, p):
                pe.wait_ge(pt_ready, 2 * b + u + 1)
                pe.wait_ge(v_ready, 2 * b + u + 1)
                after(pe, o_ready, 2 * b + u)
                for h in range(UH):
                    at = (HP * u + h // 2) * PW + (h % 2) * HW
                    last = nc.tensor.matmul(O_ps[:, (h // 2) * S:(h // 2 + 1) * S], sb["VW"][:, p, at:at + 128],
                                            sb["PT"][:, u, h, :], start=(h % 2 == 0), stop=(h % 2 == 1))
                last.then_inc(pv_done, 1)

            def project(weight, n, q, c, bank, done):
                for e in range(HP):
                    pair = HP * c + e
                    last = nc.tensor.matmul(bank[:, e * S:(e + 1) * S], weight[:, pair * 128:(pair + 1) * 128],
                                            sb["xT"][:, q, :], start=True, stop=True)
                last.then_inc(done, 1)

            def slot(i, p, half, stage):
                q = 1 - p
                b, n, r, z = i + LEAD, i + 1, i - 1, i - LAG
                if has(i):
                    scores(i, 1, p)
                if has(n):
                    pe.wait_ge(xt_ready, n + 1)
                    project(sb["d_q"], n, q, 0, bank_a, q_done)
                if has(z):
                    if has(r):
                        pe.wait_ge(v_ready, 2 * r + 1)
                    after(pe, y_ready, z)
                    pe.wait_ge(o_ready, 2 * z + 2)
                    for c in range(PAIRS):
                        last = nc.tensor.matmul(bank_b[:, 0:D], sb["OT"][:, c // HP, (c % HP) * S:(c % HP + 1) * S],
                                                sb["d_o"][:, c * D:(c + 1) * D], start=(c == 0), stop=(c == PAIRS - 1))
                    last.then_inc(out_done, 1)
                if has(n):
                    if has(r):
                        pe.wait_ge(v_ready, 2 * r + 2)
                    project(sb["d_k"], n, q, 0, bank_c, k_done)
                if has(r):
                    transpose_probs(r, 1)
                if has(n):
                    after(pe, y_ready, i - 1)
                    project(sb["d_q"], n, q, 1, bank_b, q_done)
                    pe.wait_ge(q_ready, 2 * n + 1)
                    project(sb["d_k"], n, q, 1, bank_a, k_done)
                if has(r):
                    values(r, 0, q)
                if has(i):
                    if has(n):
                        pe.wait_ge(q_ready, 2 * n + 2)
                    else:
                        pe.wait_ge(y_ready, i - 1)
                    nc.tensor.matmul(bank_b[:], sb["xT"][:, p, :], sb["d_v"][:, 0:512], start=True, stop=True)\
                        .then_inc(v_done, 1)
                    if has(n):
                        pe.wait_ge(k_ready, 2 * n + 1)
                    else:
                        pe.wait_ge(v_ready, 2 * i)
                    nc.tensor.matmul(bank_c[:], sb["xT"][:, p, :], sb["d_v"][:, 512:1024], start=True, stop=True)\
                        .then_inc(v_done, 1)
                if has(n):
                    scores(n, 0, q)
                if has(i):
                    transpose_probs(i, 0)
                if has(b):
                    pe.wait_ge(x_loaded[p], (half + 2) * 16)
                    if has(n):
                        pe.wait_ge(k_ready, 2 * n + 2)
                    nc.tensor.transpose(bank_a[:, 0:S], xs[:, p, :], sb["ident"][:]).then_inc(xt_done, 1)
                if has(r):
                    values(r, 1, q)
            slots(pe, slot)

        @block.scalar
        def _(act):
            def exps(b, u):
                act.wait_ge(sub_ready, 2 * b + u + 1)
                nc.scalar.activation(sb["P"][:, u, :, :], sb["P"][:, u, :, :], ACT.Exp).then_inc(exp_ready, 1)

            def probs_out(b, u):
                act.wait_ge(pt_done, 2 * b + u + 1)
                after(act, pv_done, 2 * b + u - 1)
                nc.scalar.activation(sb["PT"][:, u, :, :].rearrange("p h q -> p (h q)"),
                                     PT_ps[:].rearrange("p a c -> p (a c)"), ACT.Copy).then_inc(pt_ready, 1)

            def queries_out(n, q, c):
                act.wait_ge(q_done, 2 * n + c + 1)
                after(act, s_done, 2 * (n - 2) + c + 1)
                for e in range(HP):
                    pair = HP * c + e
                    last = nc.scalar.activation(sb["QW"][:, q, pair, :], (bank_a, bank_b)[c][:, e * S:(e + 1) * S],
                                                ACT.Identity,
                                                bias=sb["d_qbs"][:, pair:pair + 1], scale=sb["d_qs"][:, pair:pair + 1])
                last.then_inc(q_ready, 1)

            def values_out(b, p, c):
                act.wait_ge(v_done, 2 * b + c + 1)
                after(act, pv_done, 2 * (b - 2) + c + 1)
                pairs = sb["VW"][:, p, c * HP * PW:(c + 1) * HP * PW].rearrange("p (a w) -> p a w", a=HP)
                for e in range(2):
                    last = nc.scalar.activation(pairs[:, :, 2 * e * HW:(2 * e + 1) * HW],
                                                (bank_b, bank_c)[c].rearrange("p (a e w) -> p a e w", a=HP, e=2)[:, :, e, :],
                                                ACT.Copy)
                last.then_inc(v_ready, 1)

            def output_out(b, u):
                act.wait_ge(pv_done, 2 * b + u + 1)
                after(act, out_done, b)
                nc.scalar.activation(sb["OT"][:, u, :], O_ps[:], ACT.Copy).then_inc(o_ready, 1)

            def slot(i, p, half, stage):
                b, n, r = i + LEAD, i + 1, i - 1
                if has(n):
                    queries_out(n, 1 - p, 0)
                if has(r):
                    probs_out(r, 1)
                if has(n):
                    queries_out(n, 1 - p, 1)
                if has(i):
                    exps(i, 1)
                if has(r):
                    output_out(r, 0)
                if has(i):
                    values_out(i, p, 0)
                    values_out(i, p, 1)
                    probs_out(i, 0)
                if has(b):
                    act.wait_ge(xt_done, b + 1)
                    after(act, v_done, 2 * i + 2)
                    nc.scalar.activation(sb["xT"][:, p, :], bank_a[:, 0:S], ACT.Copy).then_inc(xt_ready, 1)
                if has(n):
                    exps(n, 0)
                if has(r):
                    output_out(r, 1)
            slots(act, slot)

        @block.vector
        def _(dve):
            def shift(b, u):
                unit = S_ps[:, 0:2, :].rearrange("p a (h k) -> p (a h) k", k=S)
                dve.wait_ge(s_done, 2 * b + u + 1)
                after(dve, sub_ready, 2 * b + u)
                nc.vector.tensor_reduce(sb["mx"][:], unit, op=ALU.max, axis=AX.X).then_inc(max_ready, 1)
                dve.wait_ge(max_ready, 2 * b + u + 1)
                after(dve, pt_done, 2 * b + u - 1)
                nc.vector.tensor_tensor(sb["P"][:, u, :, :], unit, bc(sb["mx"][:], 2, S), ALU.subtract)\
                    .then_inc(sub_ready, 1)

            def inverse_sums(b, u):
                dve.wait_ge(exp_ready, 2 * b + u + 1)
                nc.vector.tensor_reduce(sb["rsum"][:, u, :], sb["P"][:, u, :, :], op=ALU.add, axis=AX.X)\
                    .then_inc(sum_ready, 1)
                dve.wait_ge(sum_ready, 2 * b + u + 1)
                after(dve, p_ready, 2 * b + u - 1)
                nc.vector.reciprocal(sb["rinv"][:, u, :], sb["rsum"][:, u, :]).then_inc(inv_ready, 1)

            def keys_out(n, q, c):
                dve.wait_ge(k_done, 2 * n + c + 1)
                after(dve, s_done, 2 * (n - 2) + c + 1)
                pairs = slice(c * HP, (c + 1) * HP)
                for e in range(2):
                    rows = slice(e * HW, (e + 1) * HW)
                    last = nc.vector.tensor_tensor(sb["KW"][rows, q, pairs, e, :],
                                                   (bank_c, bank_a)[c][rows, :].rearrange("p (a k) -> p a k", a=HP),
                                                   bc(sb["d_kb"][rows, pairs], 2, S), ALU.add)
                last.then_inc(k_ready, 1)

            def slot(i, p, half, stage):
                n, z = i + 1, i - LAG
                if has(i):
                    inverse_sums(i, 0)
                if has(z):
                    dve.wait_ge(out_done, z + 1)
                    dve.wait_ge(xb_ready, z + 1)
                    after(dve, yn_ready, z)
                    nc.vector.tensor_tensor(sb["Y"][:], bank_b[:, 0:D], sb["XB"][:, p, :], ALU.add).then_inc(y_ready, 1)
                    dve.wait_ge(y_ready, z + 1)
                    nc.vector.bn_stats(sb["bn"][:], sb["Y"][:])
                    nc.vector.drain()
                    nc.vector.bn_aggr(sb["mv"][:], sb["bn"][:]).then_inc(var1_ready, 1)
                if has(i):
                    shift(i, 1)
                if has(z):
                    dve.wait_ge(rstd1_ready, z + 1)
                    after(dve, y2_ready, z)
                    nc.vector.tensor_scalar(sb["YN"][:], sb["Y"][:], sb["mv"][:, 0:1], sb["rstd"][:],
                                            ALU.subtract, ALU.mult).then_inc(yn_ready, 1)
                if has(n):
                    keys_out(n, 1 - p, 0)
                    keys_out(n, 1 - p, 1)
                if has(i):
                    inverse_sums(i, 1)
                if has(z):
                    dve.wait_ge(y2_ready, z + 1)
                    nc.vector.bn_stats(sb["bn2"][:], sb["Y2"][:])
                    nc.vector.drain()
                    nc.vector.bn_aggr(sb["mv2"][:], sb["bn2"][:]).then_inc(var2_ready, 1)
                if has(n):
                    shift(n, 0)
                if has(z):
                    dve.wait_ge(rstd2_ready, z + 1)
                    nc.vector.tensor_scalar(one(X, z), sb["Y2"][:], sb["mv2"][:, 0:1], sb["rstd2"][:],
                                            ALU.subtract, ALU.mult).then_inc(x_new, 1)
            slots(dve, slot)

        @block.gpsimd
        def _(pool):
            def normalise(b, u):
                pool.wait_ge(inv_ready, 2 * b + u + 1)
                nc.gpsimd.tensor_tensor(sb["P"][:, u, :, :], sb["P"][:, u, :, :], bc(sb["rinv"][:, u, :], 2, S),
                                        ALU.mult).then_inc(p_ready, 1)

            def rstd(z, k, var, mv, out, ready):
                pool.wait_ge(var, z + 1)
                nc.gpsimd.tensor_tensor(sb["ve"][:], sb[mv][:, 1:2], sb["eps"][:], ALU.add).then_inc(pool_step, 1)
                pool.wait_ge(pool_step, 3 * z + k)
                nc.gpsimd.tensor_tensor(sb[out][:], sb["ve"][:], sb["mhalf"][:], ALU.pow).then_inc(ready, 1)

            def slot(i, p, half, stage):
                r, z = i - 1, i - LAG
                if has(i):
                    normalise(i, 0)
                if has(z):
                    rstd(z, 1, var1_ready, "mv", "rstd", rstd1_ready)
                    pool.wait_ge(yn_ready, z + 1)
                    after(pool, x_new, z)
                    nc.gpsimd.tensor_tensor(sb["Y2"][:], sb["YN"][:], sb["gamma"][:], ALU.mult).then_inc(pool_step, 1)
                    pool.wait_ge(pool_step, 3 * z + 2)
                    nc.gpsimd.tensor_tensor(sb["Y2"][:], sb["Y2"][:], sb["XG"][:, p, :], ALU.add)\
                        .then_inc(y2_ready, 1)
                if has(r):
                    after(pool, y_ready, r - 1)
                    after(pool, y2_ready, r - 1)
                    nc.gpsimd.tensor_tensor(sb["XB"][:, 1 - p, :], one(X, r), sb["d_bias"][:], ALU.add)\
                        .then_inc(xb_ready, 1)
                    nc.gpsimd.tensor_tensor(sb["XG"][:, 1 - p, :], one(X, r), sb["beta"][:], ALU.add)
                if has(i):
                    normalise(i, 1)
                if has(z):
                    rstd(z, 3, var2_ready, "mv2", "rstd2", rstd2_ready)
            slots(pool, slot)


def recurrence_output(nc, bank, sb, X, hid, out):
    with ExitStack() as ctx:
        carried, carried_sb = (ctx.enter_context(nc.semaphore(f"rec_{n}")) for n in ("carried", "carried_sb"))
        tail = {n: ctx.enter_context(nc.semaphore(f"rec_{n}"))
                for n in ("pre", "act", "residual", "stats", "var", "rstd", "shift", "normed", "stored")}
        normed_by_vector = ctx.enter_context(nc.semaphore("rec_normed_by_vector"))
        block = ctx.enter_context(nc.Block())
        CH = 4
        BY_VECTOR = 2
        chunks = [slice(c * CH, (c + 1) * CH) for c in range(B // CH)]

        @block.tensor
        def _(pe):
            nc.tensor.matmul(bank[:, 0:D], sb["c2"][:], sb["r_uo"][:], start=True, stop=True).then_inc(carried, 1)

        @block.scalar
        def _(act):
            for c, steps in enumerate(chunks):
                act.wait_ge(tail["pre"], c + 1)
                nc.scalar.activation(hid[:, steps, :], hid[:, steps, :], ACT.Tanh).then_inc(tail["act"], 1)
            for c in range(BY_VECTOR):
                act.wait_ge(tail["shift"], c + 1)
                for b in range(c * CH, (c + 1) * CH):
                    last = nc.scalar.activation(hid[:, b, :], hid[:, b, :], ACT.Identity,
                                                bias=sb["nshift"][:, b:b + 1], scale=sb["ln16"][:, b:b + 1])
                last.then_inc(tail["normed"], 1)

        @block.vector
        def _(dve):
            dve.wait_ge(carried, 1)
            nc.vector.tensor_tensor(sb["cu"][:], bank[:, 0:D], sb["r_bo"][:], ALU.add).then_inc(carried_sb, 1)
            dve.wait_ge(carried_sb, 1)
            for c, steps in enumerate(chunks):
                nc.vector.tensor_tensor(hid[:, steps, :], hid[:, steps, :], bc(sb["cu"][:], 1, CH), ALU.add)\
                    .then_inc(tail["pre"], 1)
            def shift(c):
                dve.wait_ge(tail["rstd"], c + 1)
                nc.vector.scalar_tensor_tensor(out=sb["nshift"][:, chunks[c]], in0=sb["mv16"][:, chunks[c], 0],
                                               scalar=-1.0, in1=sb["ln16"][:, chunks[c]], op0=ALU.mult,
                                               op1=ALU.mult).then_inc(tail["shift"], 1)

            for c, steps in enumerate(chunks):
                dve.wait_ge(tail["residual"], c + 1)
                for b in range(c * CH, (c + 1) * CH):
                    nc.vector.bn_stats(sb["bn16"][:, b, :], hid[:, b, :])
                nc.vector.drain()
                for b in range(c * CH, (c + 1) * CH):
                    last = nc.vector.bn_aggr(sb["mv16"][:, b, :], sb["bn16"][:, b, :])
                last.then_inc(tail["stats"], 1)
                dve.wait_ge(tail["stats"], c + 1)
                nc.vector.tensor_scalar(sb["ve16"][:, steps], sb["mv16"][:, steps, 1], LN_EPS, None, ALU.add)\
                    .then_inc(tail["var"], 1)
                if 0 < c <= BY_VECTOR:
                    shift(c - 1)
            for c in range(BY_VECTOR, B // CH):
                dve.wait_ge(tail["rstd"], c + 1)
                for b in range(c * CH, (c + 1) * CH):
                    last = nc.vector.tensor_scalar(hid[:, b, :], hid[:, b, :], sb["mv16"][:, b, 0:1],
                                                   sb["ln16"][:, b:b + 1], ALU.subtract, ALU.mult)
                last.then_inc(normed_by_vector, 1)

        @block.gpsimd
        def _(pool):
            def rstd(c):
                pool.wait_ge(tail["var"], c + 1)
                nc.gpsimd.tensor_tensor(sb["ln16"][:, chunks[c]], sb["ve16"][:, chunks[c]],
                                        sb["mhalf"][:].to_broadcast([S, CH]), ALU.pow).then_inc(tail["rstd"], 1)

            for c, steps in enumerate(chunks):
                pool.wait_ge(tail["act"], c + 1)
                nc.gpsimd.tensor_tensor(hid[:, steps, :], hid[:, steps, :], X[:, steps, :], ALU.add)\
                    .then_inc(tail["residual"], 1)
                if c >= 2:
                    rstd(c - 2)
            rstd(B // CH - 2)
            rstd(B // CH - 1)

        @block.sync
        def _(sp):
            for c, steps in enumerate(chunks):
                if c < BY_VECTOR:
                    sp.wait_ge(tail["normed"], c + 1)
                else:
                    sp.wait_ge(normed_by_vector, c - BY_VECTOR + 1)
                sp.dma_start(out[steps, :, :].rearrange("b s d -> s b d"), hid[:, steps, :]).then_inc(tail["stored"], 16)
            sp.wait_ge(tail["stored"], 16 * len(chunks))


def decoder(nc, dram, out):
    with ExitStack() as ctx:
        def buf(name, shape, dt=F32):
            return ctx.enter_context(nc.sbuf_tensor(name, shape, dt))

        banks = ctx.enter_context(nc.psum_tensor("banks", [128, 8, 512], F32))
        ps = [banks[:, 0:4, :], banks[:, 4:6, :], banks[:, 6, :], banks[:, 7, :]]
        X = buf("X", [S, B, D])
        xs = buf("xs", [S, 2, D])
        sb, packs = {}, {}
        for pack, entries in PACKS.items():
            packs[pack] = buf("loaded_" + pack, [128, width(entries)])
            at = 0
            for name, _, rows, columns in entries:
                sb[name] = packs[pack][0:rows, at:at + columns]
                at += columns
        packs["rows"], at = buf("loaded_rows", [S, width(ROWS)]), 0
        for name, _, columns in ROWS:
            sb[name] = packs["rows"][:, at:at + columns]
            at += columns
        sb["blocks2"] = sb["blocks2"].rearrange("p (t b) -> p t b", t=NT)
        sb["mbatch"] = sb["mbatch"].rearrange("p (t m) -> p t m", t=NT)
        for name, shape in dict(
                a_k=[D, D], a_v=[D, D], a_kb=[D, 1], a_vb=[D, 1], a_bias=[S, D], b_qr=[D, D], b_kr=[D, D],
                e_bias=[S, D], pos=[D, S], ones=[128, 128], spread=[D, PAIRS * D], turns=[D, S + 4 * MB],
                angle=[D, S + 4 * MB], ang=[D, 2, S + 4 * MB], trig=[D, 2, S + 4 * MB], rope=[D, 4, S],
                kmask=[D, B, S], mhalf=[S, 1], eps=[S, 1], a_qbs=[D, 1], e_qbs=[D, 1],
                xT=[D, 2, S], cT=[D, 2, S], QK=[D, 2, S], rest=[D, 2, S], RP=[D, 4 * S],
                big=[128, 2 * H * S + 128], Vx=[S, 2, H * SLOT * (UH + 1)], P=[S, 2, UH, S], PT=[S, 2, UH, S],
                mx=[S, UH], O=[128, 2 * S], rden=[S, H], ON=[S, D], ONT=[D, S],
                XB=[S, 2, D], Y=[S, D], YN=[S, D], bn=[S, 6], mv=[S, 2], ve=[S, 1], rstd=[S, 1],
                d_qs=[128, PAIRS], d_qbs=[128, PAIRS], d_bias=[S, D], QW=[128, 2, PAIRS, S],
                KW=[128, 2, PAIRS, 2, S], VW=[S, 2, PAIRS * 3 * HW], OT=[128, 2, PAIRS // 2 * S],
                rsum=[S, 2, UH], rinv=[S, 2, UH],
                pos4=[S, MB], cs_table=[S, MB, 2 * HD], amask=[S, MB, S], wt=[S, B], rank=[S, B],
                sel=[S, B, TOP], count_ge=[S, B], count_eq=[S, B], factor=[S, B], xsT=[D, NT * 128],
                umask=[S, NT * 128], selT=[128, NT * 128],
                cs_prod=[128, NT, MB, 2 * HD], cs=[128, NT, 2 * HD], tokens=[128, NT, D], sq=[128, NT, D],
                ss=[128, NT], rms=[128, NT], ss2=[128, NT], rms2=[128, NT], wsel=[128, NT],
                mprod=[128, NT, NB, TOP], msel=[128, NT, TOP], qkv=[128, NT, 3 * D], roped=[128, NT, 2 * D],
                rot=[128, NT, 2 * D], att=[128, NT * H, KC], rmax=[128, NT * H], rsum32=[128, NT * H],
                vsum=[128, NT * D], attended=[128, NT * D], fT=[D, NT * 128], x1=[128, NT, D],
                x1nT=[D, NT * 128], slot_w=[128, NT, NB], bn16=[S, B, 6], mv16=[S, B, 2], ve16=[S, B],
                r_bf=[D, 1], r_bi=[D, 1], r_c0=[D, 1], c2=[D, S], xr=[D, S], fg=[D, S], ig=[D, S], gg=[D, S],
                ca=[D, S], cb=[D, S], cu=[S, D], nshift=[S, B], ln16=[S, B], Y2=[S, D], XG=[S, 2, D],
                bn2=[S, 6], mv2=[S, 2], rstd2=[S, 1]).items():
            sb[name] = buf(name, shape)
        for name, shape, dt in (("pos_i", [D, S], I32), ("pos4_i", [S, MB], I32), ("identb", [128, 128], BF16),
                                ("causal", [S, 4, S], BF16), ("parts", [D, 2, 2 * 3, S], BF16)):
            sb[name] = buf(name, shape, dt)
        sb["stacked"] = sb["big"][:, 0:2 * H * S].bitcast(BF16).rearrange("p (e h n x) -> p e h n x", e=2, h=H, n=2)
        late_loaded = ctx.enter_context(nc.semaphore("late_loaded"))
        setup_small_heads(nc, ps, sb, packs, X, dram)
        small_heads = ps, sb, X, xs
        context = dram["ctxT"].rearrange("d (b s) -> d b s", b=B)
        self0 = dict(q=sb["a_q"], k=sb["a_k"], v=sb["a_v"], o=sb["a_o"], qb=sb["a_qbs"], kb=sb["a_kb"],
                     qs=float(HD) ** -0.5, bias=sb["a_bias"])
        cross0 = dict(q=sb["b_q"], qr=sb["b_qr"], k=sb["b_k"], kr=sb["b_kr"], v=sb["b_v"], o=sb["b_o"],
                      bias=sb["b_bias"], context=context, causal=sb["causal"],
                      rope=sb["rope"][:].rearrange("p n s -> p (n s)"))
        cross1 = dict(q=sb["e_q"], k=sb["e_k"], v=sb["e_v"], o=sb["e_o"], qb=sb["e_qbs"], kb=sb["e_kb"],
                      qs=float(HD) ** -0.5, bias=sb["e_bias"], context=context, key_mask=sb["kmask"])
        half, last = width(LATE) // 2, width(LAST) // 2
        later_loads = [
            [(packs["late"][:, 0:half], dram["late"][:, 0:half])],
            [(packs["late"][:, half:], dram["late"][:, half:])],
            [(sb["QW"][:].rearrange("p u h k -> p (u h k)"), dram["repeat"])],
            [(sb["kmask"][:].rearrange("p b k -> p (b k)").bitcast(I32),
              bc(dram["mask_BxS2_ik0"].rearrange("b k -> (b k)"), 0, D))],
            [(packs["last"][:, 0:last], dram["last"][:, 0:last])],
            [(packs["last"][:, last:], dram["last"][:, last:]),
             (sb["amask"][:], dram["L0_ffn_attention_mask"][:, 0, 0:S, 0:S].rearrange("m t k -> t m k"))]]
        small_head_attention(nc, "layer0", *small_heads, [self0, cross0], later_loads=(later_loads, late_loaded))
        routed_ffn(nc, banks, sb, X, late_loaded)
        wide_head_attention(nc, ps, sb, X, xs, late_loaded)
        own = sb["QW"][:].rearrange("p u h k -> p (u h) k")
        small_head_attention(nc, "layer1", *small_heads, [cross1], own)
        recurrence_output(nc, banks[:, 0, :], sb, X, own, out)


def constants():
    part = np.arange(128)
    ident = np.eye(128, dtype=np.float32)
    causal = np.where(part[None, :] > part[:, None], np.float32(NEG), np.float32(0))
    inv = 1.0 / np.float32(ROPE_BASE) ** (np.arange(0, HD, 2, dtype=np.float32) / np.float32(HD))
    blocks = (part[:, None] // TOP == np.arange(NB)[None]).astype(np.float32)
    mbatch = np.stack([(np.minimum(t * NB + part // TOP, MB - 1)[:, None] == np.arange(MB)[None]) for t in range(NT)], 1)
    repeat = (part[:, None, None] // TOP == part[None, None, :] // TOP) \
        & (part[:, None, None] % TOP == np.arange(TOP)[None, :, None])
    return {"upper": (part[None, :] >= part[:, None]).astype(np.float32),
            "iota": np.tile(np.arange(TOP, dtype=np.float32), (S, 1)),
            "valid": (part % TOP < KC).astype(np.float32)[:, None].copy(),
            "blocks2": np.concatenate([blocks, blocks], 1), "mbatch": mbatch.astype(np.float32).reshape(128, -1),
            "repeat": repeat.astype(np.float32).reshape(128, -1),
            "inv4": np.tile(inv.astype(np.float32), (S, 1)),
            "ident": ident, "causal": causal.astype(np.float32),
            "inv_freq": np.repeat(np.tile(inv.astype(np.float32), 2), H)[:, None].copy()}


def laid_out(inputs):
    pieces = dict(inputs, **constants())
    for name in ("L0_attn_Wl", "L0_xattn_wq", "L0_xattn_wk", "L0_xattn_wv", "L0_xattn_wo_w", "L1_xattn_Wq",
                 "L1_xattn_Wk", "L1_xattn_Wv", "L1_xattn_Wp", "L1_attn_Wq", "L1_attn_Wk", "L1_attn_Wv",
                 "L1_ffn_wo", "L1_ffn_uo"):
        pieces[name + "T"] = inputs[name].T
    for name in ("L0_attn_Wq", "L0_attn_Wk", "L0_attn_bq", "L0_attn_bk", "L0_xattn_wqT", "L0_xattn_wkT",
                 "L1_xattn_WqT", "L1_xattn_WkT", "L1_xattn_bq", "L1_xattn_bk"):
        piece = pieces[name]
        pieces[name + "_by_feature"] = piece.reshape(-1, H, HD).transpose(0, 2, 1).reshape(piece.shape)
    pieces["L0_ffn_wqkv"] = np.concatenate([inputs["L0_ffn_w" + n] for n in "qkv"], 1)
    pieces["L1_ffn_w"] = np.concatenate([inputs["L1_ffn_w" + n].T for n in "fic"], 1)
    pieces["L1_ffn_u"] = np.concatenate([inputs["L1_ffn_u" + n].T for n in "fic"], 1)
    pieces["L1_attn_Wo_pairs"] = inputs["L1_attn_Wo"].T.reshape(PAIRS, 128, D).transpose(1, 0, 2).reshape(128, -1)
    for name in ("bq", "bk", "bv"):
        pieces[f"L1_attn_{name}_pairs"] = inputs["L1_attn_" + name].reshape(PAIRS, 128).T
    pieces["L1_attn_scale_pairs"] = np.repeat(inputs["L1_attn_adaptive_scale"].reshape(PAIRS, 2).T, HW, axis=0)
    pieces["L0_ffn_w2_chunks"] = inputs["L0_ffn_w2"].reshape(FF // 128, 128, D).transpose(1, 0, 2).reshape(128, -1)
    pieces["L0_ffn_router_w_row"] = inputs["L0_ffn_router_w"].reshape(D)

    arrays = {name: pieces[name] for name in ("x", "pos_S2", "mask_BxS2_ik0", "L0_ffn_attention_mask", "repeat")}
    for pack, entries in PACKS.items():
        packed, at = np.zeros((128, width(entries)), np.float32), 0
        for _, name, rows, columns in entries:
            packed[0:rows, at:at + columns] = pieces[name].reshape(rows, columns)
            at += columns
        arrays[pack] = packed
    arrays["rows"] = np.concatenate([pieces[name].reshape(-1) for _, name, _ in ROWS])
    arrays["ctxT"] = inputs["ctx_1024"].transpose(2, 0, 1).reshape(D, B * S)
    arrays["L0_ffn_position_ids_t"] = inputs["L0_ffn_position_ids"].T
    return {name: np.ascontiguousarray(a) for name, a in arrays.items()}


def kernel(**inputs):
    import numpy as _np
    import concourse.bacc as _bacc
    from concourse import mybir as _mybir
    from concourse.bass_utils import run_bass_kernel_spmd as _run

    nc = _bacc.Bacc("TRN2", target_bir_lowering=False, num_devices=1)
    arrays = laid_out({name: _np.asarray(a) for name, a in inputs.items()})
    dram = {name: nc.dram_tensor(f"in_{name}_dram", a.shape, _mybir.dt.from_np(a.dtype), kind="ExternalInput").ap()
            for name, a in arrays.items()}
    out = nc.dram_tensor("out_0_dram", (B, S, D), F32, kind="ExternalOutput").ap()
    decoder(nc, dram, out)
    r = _run(nc, [{f"in_{name}_dram": a for name, a in arrays.items()}], core_ids=[0])
    return r.results[0]["out_0_dram"]
```
